# Optimizing a Trainium2 kernel written in Bass

```python
import numpy as np
import jax
import jax.numpy as jnp

def _softmax(x, axis=-1):
    return jax.nn.softmax(x, axis=axis)

def _gelu(x):
    return jax.nn.gelu(x, approximate=True)

def _silu(x):
    return jax.nn.silu(x)

def _sigmoid(x):
    return jax.nn.sigmoid(x)

def _layernorm(x, axis=-1, eps=1e-05):
    m = jnp.mean(x, axis=axis, keepdims=True)
    v = jnp.var(x, axis=axis, keepdims=True)
    return (x - m) / jnp.sqrt(v + eps)

def _scatter_add(tgt, idx, src, axis=0):
    return tgt.at[idx].add(src)

def _segment_sum(src, seg, n):
    return jax.ops.segment_sum(src, seg, n)
kernel_name = 'mk_decoder_postln_d2_seqx_r8_20b8dc'

def setup_inputs(seed: int=0):
    np.random.seed(seed)
    _w = jnp.asarray

    def _rec_inputs():
        import jax
        import jax.numpy as jnp
        _rk = jax.random.key(seed)
        x = 0.002226 + 0.9996 * jax.random.normal(jax.random.fold_in(_rk, 1), (4, 512, 128), jnp.float32)
        _lenS = 512 - jax.random.randint(jax.random.fold_in(_rk, 7), (4,), 0, max(1, 512 // 4) + 1, jnp.int32)
        _lenS2 = 154 - jax.random.randint(jax.random.fold_in(_rk, 8), (4,), 0, max(1, 154 // 4) + 1, jnp.int32)
        _ctx_1024P = jax.random.normal(jax.random.fold_in(_rk, 11), (4, 16, 128), jnp.float32)
        _ctx_1024c = jax.random.dirichlet(jax.random.fold_in(_rk, 511), 0.3 * jnp.ones((16,), jnp.float32), (4, 154))
        _ctx_1024t = jnp.einsum('bsk,bkd->bsd', _ctx_1024c, _ctx_1024P)
        _ctx_1024t = _ctx_1024t * jax.lax.rsqrt(jnp.mean(jnp.square(_ctx_1024t)) + 1e-12) * 0.953939
        ctx_1024 = -7.10856e-05 + 0.999911 * (_ctx_1024t + 0.3 * jax.random.normal(jax.random.fold_in(_rk, 611), (4, 154, 128), jnp.float32))
        return (x, ctx_1024)
    x, ctx_1024 = _rec_inputs()

    def _L0_attn_setup():
        import jax, jax.numpy as jnp
        import numpy as np
        D_MODEL = 128
        N_HEADS = 16
        LATENT_HEADS = 8
        LATENT_DIM = 64
        N_LATENTS = 64
        WINDOW = 32
        HEAD_DIM = D_MODEL // N_HEADS
        LAT_HD = LATENT_DIM // LATENT_HEADS
        B, S = (2, 512)

        def _pool_to_latents(x):
            Bx, Sx, C = x.shape
            chunk = max(1, Sx // N_LATENTS)
            return x.reshape(Bx, N_LATENTS, chunk, C).mean(axis=2)

        def _local_window_attn(Q, K, V):
            Bx, H, Sx, D = Q.shape
            W = WINDOW
            nb = Sx // W
            Qb = Q.reshape(Bx, H, nb, W, D)
            Kp = jnp.pad(K, ((0, 0), (0, 0), (W, 0), (0, 0))).reshape(Bx, H, nb + 1, W, D)
            Vp = jnp.pad(V, ((0, 0), (0, 0), (W, 0), (0, 0))).reshape(Bx, H, nb + 1, W, D)
            Kw = jnp.concatenate([Kp[:, :, :-1], Kp[:, :, 1:]], axis=3)
            Vw = jnp.concatenate([Vp[:, :, :-1], Vp[:, :, 1:]], axis=3)
            i = jnp.arange(W)[:, None]
            j = jnp.arange(2 * W)[None, :]
            base = (j > i) & (j <= i + W)
            blk0 = (jnp.arange(nb) > 0)[:, None, None] | (j >= W)[None, :, :]
            mask = base[None, :, :] & blk0
            sc = jnp.einsum('bhnid,bhnjd->bhnij', Qb, Kw) / np.sqrt(D).astype(np.float32)
            sc = jnp.where(mask[None, None], sc, -jnp.inf)
            p = jax.nn.softmax(sc, axis=-1)
            out = jnp.einsum('bhnij,bhnjd->bhnid', p, Vw)
            return out.reshape(Bx, H, Sx, D)
        key = jax.random.key(seed)
        ks = jax.random.split(key, 11)
        std = 0.02
        w = lambda k, shp: jax.random.normal(k, shp, jnp.float32) * std
        return {'x': jax.random.normal(ks[0], (B, S, D_MODEL), jnp.float32), 'wq': w(ks[1], (D_MODEL, D_MODEL)), 'wk': w(ks[2], (D_MODEL, D_MODEL)), 'wv': w(ks[3], (D_MODEL, D_MODEL)), 'wgq': w(ks[4], (D_MODEL, LATENT_DIM)), 'wgk': w(ks[5], (D_MODEL, LATENT_DIM)), 'wgv': w(ks[6], (D_MODEL, LATENT_DIM)), 'r_out_w': w(ks[7], (LATENT_DIM, D_MODEL)), 'gate_local_w': w(ks[8], (N_HEADS, HEAD_DIM)), 'gate_remote_w': w(ks[9], (N_HEADS, HEAD_DIM)), 'w_out': w(ks[10], (D_MODEL, D_MODEL))}
    _L0_attn_all = _L0_attn_setup()
    _L0_attn_in = {k: v for k, v in _L0_attn_all.items() if k in ('wq', 'wk', 'wv', 'wgq', 'wgk', 'wgv', 'r_out_w', 'gate_local_w', 'gate_remote_w', 'w_out')}
    del _L0_attn_all

    def _L0_xattn_setup():
        import jax, jax.numpy as jnp
        import numpy as np
        DIM = 128
        HEAD_DIM = 64
        NUM_HEADS = 8
        INNER = HEAD_DIM * NUM_HEADS
        ROT_DIM = HEAD_DIM
        ROPE_BASE = 10000.0
        EPS = 1e-05

        def layer_norm(x, g, b):
            mu = jnp.mean(x, axis=-1, keepdims=True)
            var = jnp.var(x, axis=-1, keepdims=True)
            return (x - mu) * jax.lax.rsqrt(var + EPS) * g + b

        def rope_rotate_k(k):
            n = k.shape[1]
            half = ROT_DIM // 2
            inv_freq = 1.0 / ROPE_BASE ** (jnp.arange(0, ROT_DIM, 2, dtype=jnp.float32) / ROT_DIM)
            theta = jnp.arange(n, dtype=jnp.float32)[:, None] * inv_freq[None, :]
            angles = jnp.concatenate([theta, theta], axis=-1)
            cos = jnp.cos(angles)[None, :, None, :].astype(k.dtype)
            sin = jnp.sin(angles)[None, :, None, :].astype(k.dtype)
            k_rope, k_pass = (k[..., :ROT_DIM], k[..., ROT_DIM:])
            neg_half = jnp.concatenate([-k_rope[..., half:], k_rope[..., :half]], axis=-1)
            k_rope = k_rope * cos + neg_half * sin
            return jnp.concatenate([k_rope, k_pass], axis=-1)
        key = jax.random.key(seed)
        ks = jax.random.split(key, 5)
        b, n, m = (8, 1024, 64)
        s = 1.0 / np.sqrt(DIM)
        return {'x': jax.random.normal(ks[0], (b, n, DIM), jnp.float32), 'latents': jax.random.normal(ks[1], (b, m, DIM), jnp.float32), 'gamma_x': jnp.ones((DIM,), jnp.float32), 'beta_x': jnp.zeros((DIM,), jnp.float32), 'gamma_l': jnp.ones((DIM,), jnp.float32), 'beta_l': jnp.zeros((DIM,), jnp.float32), 'Wq': jax.random.normal(ks[2], (DIM, INNER), jnp.float32) * s, 'Wkv': jax.random.normal(ks[3], (DIM, 2 * INNER), jnp.float32) * s, 'Wo': jax.random.normal(ks[4], (INNER, DIM), jnp.float32) * (1.0 / np.sqrt(INNER))}
    _L0_xattn_all = _L0_xattn_setup()
    _L0_xattn_in = {k: v for k, v in _L0_xattn_all.items() if k in ('gamma_x', 'beta_x', 'gamma_l', 'beta_l', 'Wq', 'Wkv', 'Wo')}
    del _L0_xattn_all

    def _L0_ffn_setup():
        import jax, jax.numpy as jnp
        import numpy as np
        B, K, D = (128, 32, 128)
        E = 32
        H = int(D * 0.25)

        def _rsqrt_uniform(key, shape, d):
            bound = d ** (-0.5)
            return jax.random.uniform(key, shape, jnp.float32, -bound, bound)
        key = jax.random.key(seed)
        ks = jax.random.split(key, 7)
        return {'x': jax.random.normal(ks[0], (B, K, D), jnp.float32), 'router_w': _rsqrt_uniform(ks[1], (E, D), D), 'router_b': _rsqrt_uniform(ks[2], (E,), D), 'weights1': _rsqrt_uniform(ks[3], (E, D, H), H), 'bias1': _rsqrt_uniform(ks[4], (E, H), H), 'weights2': _rsqrt_uniform(ks[5], (E, H, D), D), 'bias2': _rsqrt_uniform(ks[6], (E, D), D)}
    _L0_ffn_all = _L0_ffn_setup()
    _L0_ffn_in = {k: v for k, v in _L0_ffn_all.items() if k in ('router_w', 'router_b', 'weights1', 'bias1', 'weights2', 'bias2')}
    del _L0_ffn_all

    def _L1_attn_setup():
        import jax, jax.numpy as jnp
        import numpy as np
        NEG_FILL = jnp.finfo(jnp.float32).min
        key = jax.random.key(seed)
        k0, k1, k2, k3, k4 = jax.random.split(key, 5)
        B, N, E, D = (4, 512, 128, 32)
        STD = 0.05
        inputs = jax.random.normal(k0, (B, N, E), dtype=jnp.float32)
        Wq = STD * jax.random.normal(k1, (E, D), dtype=jnp.float32)
        Wk = STD * jax.random.normal(k2, (E, D), dtype=jnp.float32)
        Wvdown = STD * jax.random.normal(k3, (E, D), dtype=jnp.float32)
        Wvup = STD * jax.random.normal(k4, (D, E), dtype=jnp.float32)
        return {'inputs': inputs, 'Wq': Wq, 'Wk': Wk, 'Wvdown': Wvdown, 'Wvup': Wvup}
    _L1_attn_all = _L1_attn_setup()
    _L1_attn_in = {k: v for k, v in _L1_attn_all.items() if k in ('Wq', 'Wk', 'Wvdown', 'Wvup')}
    del _L1_attn_all

    def _L1_xattn_setup():
        import jax, jax.numpy as jnp
        import numpy as np
        EMBED_DIM = 128
        N_HEADS = 16
        HEAD_DIM = EMBED_DIM // N_HEADS
        key = jax.random.key(seed)
        ks = jax.random.split(key, 8)
        B, Tq, Tk, C = (2, 256, 256, EMBED_DIM)
        s = 1.0 / np.sqrt(C)
        return {'query': jax.random.normal(ks[0], (B, Tq, C), jnp.float32), 'context': jax.random.normal(ks[1], (B, Tk, C), jnp.float32), 'Wq': jax.random.normal(ks[2], (C, C), jnp.float32) * s, 'bq': jnp.zeros((C,), jnp.float32), 'Wkv': jax.random.normal(ks[3], (C, 2 * C), jnp.float32) * s, 'bkv': jnp.zeros((2 * C,), jnp.float32), 'Wo': jax.random.normal(ks[4], (C, C), jnp.float32) * s, 'bo': jnp.zeros((C,), jnp.float32)}
    _L1_xattn_all = _L1_xattn_setup()
    _L1_xattn_in = {k: v for k, v in _L1_xattn_all.items() if k in ('Wq', 'bq', 'Wkv', 'bkv', 'Wo', 'bo')}
    del _L1_xattn_all

    def _L1_ffn_setup():
        import jax, jax.numpy as jnp
        import numpy as np
        EPS = 1e-06
        LN_EPS = 1e-05

        def _absmean_core(W):
            gamma = jnp.mean(jnp.abs(W)) + EPS
            Ws = W / gamma
            Wq = jnp.sign(Ws) * jnp.minimum(jnp.round(jnp.abs(Ws)), 1.0)
            return (Wq, gamma)

        @jax.custom_vjp
        def absmean(W):
            return _absmean_core(W)[0]

        def _absmean_fwd(W):
            Wq, gamma = _absmean_core(W)
            return (Wq, gamma)

        def _absmean_bwd(gamma, g):
            return (g / gamma,)
        absmean.defvjp(_absmean_fwd, _absmean_bwd)

        def layernorm(x, w, b, eps=LN_EPS):
            mu = jnp.mean(x, axis=-1, keepdims=True)
            var = jnp.mean((x - mu) ** 2, axis=-1, keepdims=True)
            return (x - mu) * jax.lax.rsqrt(var + eps) * w + b
        key = jax.random.key(seed)
        k1, k2, k3 = jax.random.split(key, 3)
        d, h = (128, 512)
        B, T = (8, 256)
        return {'x': jax.random.normal(k1, (B, T, d), jnp.float32), 'W_fc': jax.random.normal(k2, (h, d), jnp.float32), 'ln_w': jnp.ones((h,), jnp.float32), 'ln_b': jnp.zeros((h,), jnp.float32), 'W_proj': jax.random.normal(k3, (d, h), jnp.float32)}
    _L1_ffn_all = _L1_ffn_setup()
    _L1_ffn_in = {k: v for k, v in _L1_ffn_all.items() if k in ('W_fc', 'ln_w', 'ln_b', 'W_proj')}
    del _L1_ffn_all
    return {'x': x, 'ctx_1024': ctx_1024, 'L0_attn_wq': _L0_attn_in['wq'], 'L0_attn_wk': _L0_attn_in['wk'], 'L0_attn_wv': _L0_attn_in['wv'], 'L0_attn_wgq': _L0_attn_in['wgq'], 'L0_attn_wgk': _L0_attn_in['wgk'], 'L0_attn_wgv': _L0_attn_in['wgv'], 'L0_attn_r_out_w': _L0_attn_in['r_out_w'], 'L0_attn_gate_local_w': _L0_attn_in['gate_local_w'], 'L0_attn_gate_remote_w': _L0_attn_in['gate_remote_w'], 'L0_attn_w_out': _L0_attn_in['w_out'], 'L0_xattn_gamma_x': _L0_xattn_in['gamma_x'], 'L0_xattn_beta_x': _L0_xattn_in['beta_x'], 'L0_xattn_gamma_l': _L0_xattn_in['gamma_l'], 'L0_xattn_beta_l': _L0_xattn_in['beta_l'], 'L0_xattn_Wq': _L0_xattn_in['Wq'], 'L0_xattn_Wkv': _L0_xattn_in['Wkv'], 'L0_xattn_Wo': _L0_xattn_in['Wo'], 'L0_ffn_router_w': _L0_ffn_in['router_w'], 'L0_ffn_router_b': _L0_ffn_in['router_b'], 'L0_ffn_weights1': _L0_ffn_in['weights1'], 'L0_ffn_bias1': _L0_ffn_in['bias1'], 'L0_ffn_weights2': _L0_ffn_in['weights2'], 'L0_ffn_bias2': _L0_ffn_in['bias2'], 'L1_attn_Wq': _L1_attn_in['Wq'], 'L1_attn_Wk': _L1_attn_in['Wk'], 'L1_attn_Wvdown': _L1_attn_in['Wvdown'], 'L1_attn_Wvup': _L1_attn_in['Wvup'], 'L1_xattn_Wq': _L1_xattn_in['Wq'], 'L1_xattn_bq': _L1_xattn_in['bq'], 'L1_xattn_Wkv': _L1_xattn_in['Wkv'], 'L1_xattn_bkv': _L1_xattn_in['bkv'], 'L1_xattn_Wo': _L1_xattn_in['Wo'], 'L1_xattn_bo': _L1_xattn_in['bo'], 'L1_ffn_W_fc': _L1_ffn_in['W_fc'], 'L1_ffn_ln_w': _L1_ffn_in['ln_w'], 'L1_ffn_ln_b': _L1_ffn_in['ln_b'], 'L1_ffn_W_proj': _L1_ffn_in['W_proj']}

def reference(x, ctx_1024, L0_attn_wq, L0_attn_wk, L0_attn_wv, L0_attn_wgq, L0_attn_wgk, L0_attn_wgv, L0_attn_r_out_w, L0_attn_gate_local_w, L0_attn_gate_remote_w, L0_attn_w_out, L0_xattn_gamma_x, L0_xattn_beta_x, L0_xattn_gamma_l, L0_xattn_beta_l, L0_xattn_Wq, L0_xattn_Wkv, L0_xattn_Wo, L0_ffn_router_w, L0_ffn_router_b, L0_ffn_weights1, L0_ffn_bias1, L0_ffn_weights2, L0_ffn_bias2, L1_attn_Wq, L1_attn_Wk, L1_attn_Wvdown, L1_attn_Wvup, L1_xattn_Wq, L1_xattn_bq, L1_xattn_Wkv, L1_xattn_bkv, L1_xattn_Wo, L1_xattn_bo, L1_ffn_W_fc, L1_ffn_ln_w, L1_ffn_ln_b, L1_ffn_W_proj):
    import jax
    import jax.numpy as jnp

    def _L0_attn_ref(x, wq, wk, wv, wgq, wgk, wgv, r_out_w, gate_local_w, gate_remote_w, w_out):
        import jax, jax.numpy as jnp
        import numpy as np
        D_MODEL = 128
        N_HEADS = 16
        LATENT_HEADS = 8
        LATENT_DIM = 64
        N_LATENTS = 64
        WINDOW = 32
        HEAD_DIM = D_MODEL // N_HEADS
        LAT_HD = LATENT_DIM // LATENT_HEADS
        B, S = (2, 512)

        def _pool_to_latents(x):
            Bx, Sx, C = x.shape
            chunk = max(1, Sx // N_LATENTS)
            return x.reshape(Bx, N_LATENTS, chunk, C).mean(axis=2)

        def _local_window_attn(Q, K, V):
            Bx, H, Sx, D = Q.shape
            W = WINDOW
            nb = Sx // W
            Qb = Q.reshape(Bx, H, nb, W, D)
            Kp = jnp.pad(K, ((0, 0), (0, 0), (W, 0), (0, 0))).reshape(Bx, H, nb + 1, W, D)
            Vp = jnp.pad(V, ((0, 0), (0, 0), (W, 0), (0, 0))).reshape(Bx, H, nb + 1, W, D)
            Kw = jnp.concatenate([Kp[:, :, :-1], Kp[:, :, 1:]], axis=3)
            Vw = jnp.concatenate([Vp[:, :, :-1], Vp[:, :, 1:]], axis=3)
            i = jnp.arange(W)[:, None]
            j = jnp.arange(2 * W)[None, :]
            base = (j > i) & (j <= i + W)
            blk0 = (jnp.arange(nb) > 0)[:, None, None] | (j >= W)[None, :, :]
            mask = base[None, :, :] & blk0
            sc = jnp.einsum('bhnid,bhnjd->bhnij', Qb, Kw) / np.sqrt(D).astype(np.float32)
            sc = jnp.where(mask[None, None], sc, -jnp.inf)
            p = jax.nn.softmax(sc, axis=-1)
            out = jnp.einsum('bhnij,bhnjd->bhnid', p, Vw)
            return out.reshape(Bx, H, Sx, D)
        Bx, Sx, _ = x.shape
        chunk = max(1, Sx // N_LATENTS)
        Q = (x @ wq).reshape(Bx, Sx, N_HEADS, HEAD_DIM).transpose(0, 2, 1, 3)
        K = (x @ wk).reshape(Bx, Sx, N_HEADS, HEAD_DIM).transpose(0, 2, 1, 3)
        V = (x @ wv).reshape(Bx, Sx, N_HEADS, HEAD_DIM).transpose(0, 2, 1, 3)
        local = _local_window_attn(Q, K, V)
        GQ = (x @ wgq).reshape(Bx, Sx, LATENT_HEADS, LAT_HD).transpose(0, 2, 1, 3)
        GK = _pool_to_latents(x @ wgk).reshape(Bx, N_LATENTS, LATENT_HEADS, LAT_HD).transpose(0, 2, 1, 3)
        GV = _pool_to_latents(x @ wgv).reshape(Bx, N_LATENTS, LATENT_HEADS, LAT_HD).transpose(0, 2, 1, 3)
        lsc = jnp.einsum('bhsd,bhnd->bhsn', GQ, GK) / np.sqrt(LAT_HD).astype(np.float32)
        lmask = jnp.arange(N_LATENTS)[None, :] <= (jnp.arange(Sx) // chunk)[:, None]
        lsc = jnp.where(lmask[None, None], lsc, -jnp.inf)
        lp = jax.nn.softmax(lsc, axis=-1)
        rem = jnp.einsum('bhsn,bhnd->bhsd', lp, GV)
        rem = rem.transpose(0, 2, 1, 3).reshape(Bx, Sx, LATENT_DIM) @ r_out_w
        rem = rem.reshape(Bx, Sx, N_HEADS, HEAD_DIM).transpose(0, 2, 1, 3)
        gl = jax.nn.sigmoid(jnp.einsum('bhsd,hd->bhs', Q, gate_local_w))[..., None]
        gr = jax.nn.sigmoid(jnp.einsum('bhsd,hd->bhs', Q, gate_remote_w))[..., None]
        out = gl * local + gr * rem
        out = out.transpose(0, 2, 1, 3).reshape(Bx, Sx, D_MODEL)
        return out @ w_out

    def _L0_xattn_ref(x, latents, gamma_x, beta_x, gamma_l, beta_l, Wq, Wkv, Wo):
        import jax, jax.numpy as jnp
        import numpy as np
        DIM = 128
        HEAD_DIM = 64
        NUM_HEADS = 8
        INNER = HEAD_DIM * NUM_HEADS
        ROT_DIM = HEAD_DIM
        ROPE_BASE = 10000.0
        EPS = 1e-05

        def layer_norm(x, g, b):
            mu = jnp.mean(x, axis=-1, keepdims=True)
            var = jnp.var(x, axis=-1, keepdims=True)
            return (x - mu) * jax.lax.rsqrt(var + EPS) * g + b

        def rope_rotate_k(k):
            n = k.shape[1]
            half = ROT_DIM // 2
            inv_freq = 1.0 / ROPE_BASE ** (jnp.arange(0, ROT_DIM, 2, dtype=jnp.float32) / ROT_DIM)
            theta = jnp.arange(n, dtype=jnp.float32)[:, None] * inv_freq[None, :]
            angles = jnp.concatenate([theta, theta], axis=-1)
            cos = jnp.cos(angles)[None, :, None, :].astype(k.dtype)
            sin = jnp.sin(angles)[None, :, None, :].astype(k.dtype)
            k_rope, k_pass = (k[..., :ROT_DIM], k[..., ROT_DIM:])
            neg_half = jnp.concatenate([-k_rope[..., half:], k_rope[..., :half]], axis=-1)
            k_rope = k_rope * cos + neg_half * sin
            return jnp.concatenate([k_rope, k_pass], axis=-1)
        b, n, _ = x.shape
        m = latents.shape[1]
        h, d = (NUM_HEADS, HEAD_DIM)
        scale = d ** (-0.5)
        xn = layer_norm(x, gamma_x, beta_x)
        ln = layer_norm(latents, gamma_l, beta_l)
        q = (ln @ Wq).reshape(b, m, h, d)
        kv_x = xn @ Wkv
        k_x, v_x = (kv_x[..., :INNER], kv_x[..., INNER:])
        kv_l = ln @ Wkv
        k_l, v_l = (kv_l[..., :INNER], kv_l[..., INNER:])
        k_x = k_x.reshape(b, n, h, d)
        v_x = v_x.reshape(b, n, h, d)
        k_x = rope_rotate_k(k_x)
        q = jnp.transpose(q, (0, 2, 1, 3)) * scale
        k_x = jnp.transpose(k_x, (0, 2, 1, 3))
        v_x = jnp.transpose(v_x, (0, 2, 1, 3))
        k_l = jnp.transpose(k_l.reshape(b, m, h, d), (0, 2, 1, 3))
        v_l = jnp.transpose(v_l.reshape(b, m, h, d), (0, 2, 1, 3))
        k = jnp.concatenate([k_x, k_l], axis=2)
        v = jnp.concatenate([v_x, v_l], axis=2)
        sim = jnp.einsum('bhid,bhjd->bhij', q, k)
        attn = jax.nn.softmax(sim, axis=-1)
        out = jnp.einsum('bhij,bhjd->bhid', attn, v)
        out = jnp.transpose(out, (0, 2, 1, 3)).reshape(b, m, INNER)
        return out @ Wo

    def _L0_ffn_ref(x, router_w, router_b, weights1, bias1, weights2, bias2):
        import jax, jax.numpy as jnp
        import numpy as np
        B, K, D = (128, 32, 128)
        E = 32
        H = int(D * 0.25)

        def _rsqrt_uniform(key, shape, d):
            bound = d ** (-0.5)
            return jax.random.uniform(key, shape, jnp.float32, -bound, bound)
        b, k, d = x.shape
        x_flat = x.reshape(-1, d)
        n = x_flat.shape[0]
        logits = x_flat @ router_w.T + router_b
        routed_idx = jnp.argmax(logits, axis=-1)

        def expert_mlp(w1, b1, w2, b2):
            h = jax.nn.relu(x_flat @ w1 + b1)
            return jax.nn.relu(h @ w2 + b2)
        y_all = jax.vmap(expert_mlp)(weights1, bias1, weights2, bias2)
        out_flat = y_all[routed_idx, jnp.arange(n)]
        return out_flat.reshape(b, k, d)

    def _L1_attn_ref(inputs, Wq, Wk, Wvdown, Wvup):
        import jax, jax.numpy as jnp
        import numpy as np
        NEG_FILL = jnp.finfo(jnp.float32).min
        B, N, E = inputs.shape
        D = Wq.shape[1]
        Q = inputs @ Wq
        K = inputs @ Wk
        score = jnp.einsum('bqd,bkd->bqk', Q, K)
        score = score / jnp.sqrt(jnp.float32(D))
        causal = jnp.tril(jnp.ones((N, N), dtype=bool))
        score = jnp.where(causal, score, 0.0)
        score = jnp.where(score != 0, score, NEG_FILL)
        attn = jax.nn.softmax(score, axis=-1)
        V = inputs @ (Wvdown @ Wvup)
        return attn @ V

    def _L1_xattn_ref(query, context, Wq, bq, Wkv, bkv, Wo, bo):
        import jax, jax.numpy as jnp
        import numpy as np
        EMBED_DIM = 128
        N_HEADS = 16
        HEAD_DIM = EMBED_DIM // N_HEADS
        B, Tq, C = query.shape
        Tk = context.shape[1]
        H, D = (N_HEADS, HEAD_DIM)
        q = (query @ Wq + bq).reshape(B, Tq, H, D)
        kv = (context @ Wkv + bkv).reshape(B, Tk, 2, H, D)
        k = kv[:, :, 0]
        v = kv[:, :, 1]
        scale = D ** (-0.5)
        attn = jnp.einsum('bqhd,bkhd->bhqk', q, k) * scale
        attn = jax.nn.softmax(attn, axis=-1)
        out = jnp.einsum('bhqk,bkhd->bqhd', attn, v).reshape(B, Tq, C)
        return out @ Wo + bo

    def _L1_ffn_ref(x, W_fc, ln_w, ln_b, W_proj):
        import jax, jax.numpy as jnp
        import numpy as np
        EPS = 1e-06
        LN_EPS = 1e-05

        def _absmean_core(W):
            gamma = jnp.mean(jnp.abs(W)) + EPS
            Ws = W / gamma
            Wq = jnp.sign(Ws) * jnp.minimum(jnp.round(jnp.abs(Ws)), 1.0)
            return (Wq, gamma)

        @jax.custom_vjp
        def absmean(W):
            return _absmean_core(W)[0]

        def _absmean_fwd(W):
            Wq, gamma = _absmean_core(W)
            return (Wq, gamma)

        def _absmean_bwd(gamma, g):
            return (g / gamma,)
        absmean.defvjp(_absmean_fwd, _absmean_bwd)

        def layernorm(x, w, b, eps=LN_EPS):
            mu = jnp.mean(x, axis=-1, keepdims=True)
            var = jnp.mean((x - mu) ** 2, axis=-1, keepdims=True)
            return (x - mu) * jax.lax.rsqrt(var + eps) * w + b
        h = jnp.einsum('btd,hd->bth', x, absmean(W_fc))
        h = jax.nn.gelu(h, approximate=False)
        h = layernorm(h, ln_w, ln_b)
        return jnp.einsum('bth,dh->btd', h, absmean(W_proj))
    x = _layernorm(x + _L0_attn_ref(x, L0_attn_wq, L0_attn_wk, L0_attn_wv, L0_attn_wgq, L0_attn_wgk, L0_attn_wgv, L0_attn_r_out_w, L0_attn_gate_local_w, L0_attn_gate_remote_w, L0_attn_w_out), axis=-1)
    x = _layernorm(x + _L0_xattn_ref(ctx_1024, x, L0_xattn_gamma_x, L0_xattn_beta_x, L0_xattn_gamma_l, L0_xattn_beta_l, L0_xattn_Wq, L0_xattn_Wkv, L0_xattn_Wo), axis=-1)
    x = _layernorm(x + _L0_ffn_ref(x, L0_ffn_router_w, L0_ffn_router_b, L0_ffn_weights1, L0_ffn_bias1, L0_ffn_weights2, L0_ffn_bias2), axis=-1)
    x = _layernorm(x + _L1_attn_ref(x, L1_attn_Wq, L1_attn_Wk, L1_attn_Wvdown, L1_attn_Wvup), axis=-1)
    x = _layernorm(x + _L1_xattn_ref(x, ctx_1024, L1_xattn_Wq, L1_xattn_bq, L1_xattn_Wkv, L1_xattn_bkv, L1_xattn_Wo, L1_xattn_bo), axis=-1)
    x = _layernorm(x + _L1_ffn_ref(x, L1_ffn_W_fc, L1_ffn_ln_w, L1_ffn_ln_b, L1_ffn_W_proj), axis=-1)
    return x

_drawn_inputs = setup_inputs


def setup_inputs(seed=0):
    import zlib

    import numpy as np

    out = dict(_drawn_inputs(seed))
    spreads = {'L0_xattn_gamma_x': (1.0, 0.2),
     'L0_xattn_beta_x': (0.0, 0.1),
     'L0_xattn_gamma_l': (1.0, 0.2),
     'L0_xattn_beta_l': (0.0, 0.1),
     'L1_xattn_bq': (0.0, 0.343),
     'L1_xattn_bkv': (0.0, 0.1),
     'L1_xattn_bo': (0.0, 0.1),
     'L1_ffn_ln_w': (1.0, 0.2),
     'L1_ffn_ln_b': (0.0, 0.1)}
    factors = {'L0_attn_wq': 8.0,
     'L0_attn_wk': 8.0,
     'L0_attn_wv': 5.073,
     'L0_attn_wgq': 8.0,
     'L0_attn_wgk': 8.0,
     'L0_attn_wgv': 8.0,
     'L0_attn_r_out_w': 8.0,
     'L0_attn_gate_local_w': 8.0,
     'L0_attn_gate_remote_w': 8.0,
     'L0_attn_w_out': 4.87,
     'L0_ffn_bias1': 3.909,
     'L1_attn_Wq': 7.756,
     'L1_attn_Wk': 7.629}
    for name, (base, spread) in spreads.items():
        noise = np.random.default_rng([zlib.crc32(name.encode()), seed]).standard_normal(out[name].shape)
        drawn = base * np.exp(spread * noise) if base else spread * noise
        out[name] = jnp.asarray(drawn.astype(out[name].dtype))
    for name, factor in factors.items():
        out[name] = (out[name] * factor).astype(out[name].dtype)
    return out
```

```python
from contextlib import ExitStack

import numpy as np

import concourse.bass as bass
from concourse import mybir
from concourse.alu_op_type import AluOpType as ALU

F32 = mybir.dt.float32
BF16 = mybir.dt.bfloat16
ACT = mybir.ActivationFunctionType
AX = mybir.AxisListType.X

B, S, D, SC = 4, 512, 128, 154
P = 128
NT = S // P
STREAMS = 2
TURNS = B // STREAMS
CH = SC // 2
BANK = 512
EPS = 1e-5
INNER = 4
MASKED = -1e30
FMIN = float(np.finfo(np.float32).min)
W, HD, NL = 32, 8, 64
XH, XD = 8, 64
NK = S + SC
E, EH = 32, 32
EC = E * EH // P
FH = 512
FC = FH // P

CONST = dict(ident=P, mask4=4, mask8=8, headblk=P, gvmask=4 * 64, iota=E, cos=SC, sin=SC, tri=2 * S - P,
             hmaskf=4 * P)
CONST16 = dict(winq=P, winmask=5 * P, latmask=NT * NL, sel=EC * P)


def constants():
    p = np.arange(P)[:, None]
    f = np.arange(P)[None, :]
    c = {}
    c["ident"] = p == f
    c["mask4"] = (p % 32) // HD == np.arange(4)[None, :]
    c["mask8"] = p // HD == np.arange(8)[None, :]
    c["headblk"] = p // HD == f // HD
    c["winq"] = p % W == f % W
    i, j = p % W, np.arange(2 * W)[None, :]
    band = (j > i) & (j <= i + W)
    usual = np.where(np.tile(band, (1, 2)), 0.0, MASKED)
    first = np.where(np.concatenate([band & (j >= W), band], 1), 0.0, MASKED)
    c["winmask"] = np.concatenate([first] + [usual] * 4, 1)
    t, n = np.arange(NT)[None, :, None], np.arange(NL)[None, None, :]
    c["latmask"] = np.where(n <= (t * P + p[:, :, None]) // (S // NL), 0.0, MASKED)
    k, g = np.arange(4)[None, :, None], np.arange(64)[None, None, :]
    c["gvmask"] = g // HD == 2 * k + p[:, :, None] // NL
    c["iota"] = np.broadcast_to(np.arange(E)[None, :] - 2.0 * E, (P, E))
    inv = (1.0 / np.float32(10000.0) ** (np.arange(0, XD, 2, dtype=np.float32) / np.float32(XD))).astype(np.float32)
    theta = (np.arange(SC, dtype=np.float32)[:, None] * inv[None, :]).astype(np.float32)
    angle = np.concatenate([theta, theta] * 2, 1).T
    c["cos"], c["sin"] = np.cos(angle), np.sin(angle)
    j = np.arange(2 * S - P)[None, :]
    c["tri"] = j - (S - P) <= p
    h4 = np.arange(4)[None, :, None]
    c["hmaskf"] = np.broadcast_to((f[:, None, :] // HD) % 4 == h4, (P, 4, P))
    k = np.arange(EC)[None, :, None]
    c["sel"] = np.where(p[:, :, None] == 4 * k + f[:, None, :] // EH, -MASKED, 0.0)
    return [np.concatenate([np.asarray(c[n], np.float32).reshape(P, w) for n, w in names.items()], 1)
            for names in (CONST, CONST16)]


class Signal:

    def __init__(self, sem, per, step=1, before=0):
        self.sem, self.per, self.step, self.before = sem, per, step, before

    def at(self, turn, k):
        return turn * (self.per * self.step) + (self.before + k) * self.step


def build(nc, io, out):
    with ExitStack() as ctx:
        def sb(name, shape, dt=F32):
            return ctx.enter_context(nc.sbuf_tensor(name, shape, dt))

        def sem(name):
            return ctx.enter_context(nc.semaphore(name))

        def signal(name, per, step=1):
            return [Signal(sem(f"{name}{s}"), per, step) for s in range(STREAMS)]

        def signals(name, *pers):
            sems = [sem(f"{name}{s}") for s in range(STREAMS)]
            return [[Signal(q, sum(pers), 1, sum(pers[:k])) for q in sems] for k in range(len(pers))]

        ncon = sum(CONST.values())
        table = sb("table", [P, ncon])
        con, at = {}, 0
        for name, w in CONST.items():
            con[name] = table[:, at:at + w]
            at += w
        ident = con["ident"]
        mask4 = con["mask4"]
        latmask = sb("latmask_b", [P, NT, NL], BF16)
        winmask = sb("winmask_b", [P, 5 * P], BF16)
        winq = sb("winq_b", [P, P], BF16)
        identb = sb("ident_b", [P, P], BF16)
        selb = sb("sel_b", [E, EC, P], BF16)
        ones = sb("ones", [P, P])
        halves, epsilon = sb("halves", [P, NT]), sb("epsilon", [P, NT])
        w_q, w_k, w_v, w_o = (sb(f"a_{n}", [P, P]) for n in ("wq", "wk", "wv", "wo"))
        w_gq, w_gk, w_gv = (sb(f"a_{n}", [P, 64]) for n in ("wgq", "wgk", "wgv"))
        w_rout = sb("a_rout", [64, P])
        vec_rows, vec = sb("vec_rows", [24, P]), sb("vec", [P, 24])
        gatew, lnp, e_bq, e_bk = vec[:, 0:2], vec[:, 2:6], vec[:, 6:7], vec[:, 7:8]
        b1, f_w, f_b = vec[:, 8:16], vec[:, 16:20], vec[:, 20:24]
        gate_l, gate_r = sb("a_gl", [P, P]), sb("a_gr", [P, P])
        xw_q, xw_kv = sb("b_wq", [P, 512]), sb("b_wkv", [P, 1024])
        xw_kr = sb("b_wkr", [P, 512])
        xw_o = sb("b_wo", [P, 4, P])
        rw = sb("c_rw", [P, E])
        rb = sb("c_rb", [P, E])
        w1 = sb("c_w1", [P, E, EH])
        w2 = sb("c_w2", [P, EC, P])
        b2 = sb("c_b2", [E, P])
        dw_q, dw_k = (sb(f"d_{n}", [P, 32]) for n in ("wq", "wk"))
        dw_vdT, dw_vu, dw_v = sb("d_wvdT", [32, P]), sb("d_wvu", [32, P]), sb("d_wv", [P, P])
        ew_q, ew_kv, ew_o = sb("e_wq", [P, P]), sb("e_wkv", [P, 2 * P]), sb("e_wo", [P, P])
        e_bv, e_bo = sb("e_bv", [P, P]), sb("e_bo", [1, P])
        wfcT, wpT = sb("f_wfcT", [P, FH]), sb("f_wpT", [P, FC, P])
        gam = sb("f_gam", [P, 8])

        x_tm = [sb(f"x_tm{s}", [P, NT, D]) for s in range(STREAMS)]
        xT = [sb(f"xT{s}", [P, W + S]) for s in range(STREAMS)]
        y = [sb(f"y{s}", [P, NT, D]) for s in range(STREAMS)]
        c_tm = [sb(f"c_tm{s}", [CH, 2, D]) for s in range(STREAMS)]
        cn = [sb(f"cn{s}", [CH, 2, D]) for s in range(STREAMS)]
        cT = [sb(f"cT{s}", [P, SC]) for s in range(STREAMS)]
        cnT = [sb(f"cnT{s}", [P, SC]) for s in range(STREAMS)]
        bn = [sb(f"bn{s}", [P, NT, 6]) for s in range(STREAMS)]
        mv = [sb(f"mv{s}", [P, NT, 2]) for s in range(STREAMS)]
        veps = [sb(f"veps{s}", [P, NT]) for s in range(STREAMS)]
        rstd = [sb(f"rstd{s}", [P, NT]) for s in range(STREAMS)]
        mx, nb, sums, rsum = ([sb(f"{n}{s}", [P, 64]) for s in range(STREAMS)] for n in ("mx", "nb", "sums", "rsum"))
        spacer = sb("spacer", [P, 1])
        spread = [sb(f"spread{s}", [P, S]) for s in range(STREAMS)]
        arena_w = [sb(f"arena_w{s}", [P, 6144]) for s in range(STREAMS)]
        arena_q = [sb(f"arena_q{s}", [P, 11164]) for s in range(STREAMS)]

        def view(arena, at, *shape):
            n = int(np.prod(shape))
            v = arena[:, at:at + n]
            if len(shape) == 2:
                v = v.rearrange("p (a b) -> p a b", b=shape[1])
            if len(shape) == 3:
                v = v.rearrange("p (a b c) -> p a b c", b=shape[1], c=shape[2])
            return v

        Qm = [view(a, 0, S // W, 4, W) for a in arena_q]
        QT = [view(a, 2048, S) for a in arena_q]
        GQ = [view(a, 2560, S) for a in arena_q]
        GKm = [view(a, 3072, 8, NL) for a in arena_q]
        GVm = [view(a, 3584, 4, 64) for a in arena_q]
        Vw = [view(a, 3840, 8, P) for a in arena_q]
        tl = [view(a, 4864, S) for a in arena_q]
        tr = [view(a, 5376, S) for a in arena_q]
        loc = [view(a, 5888, S) for a in arena_q]
        pooled = [view(a, 6400, 2, NL) for a in arena_q]
        remT = [view(a, 6528, S) for a in arena_q]
        mixT = [view(a, 7040, S) for a in arena_q]
        picked = [view(a, 7552, 8, 4, W) for a in arena_q]
        KP = [view(a, 8576, W + S) for a in arena_q]
        sc = [view(a, 0, 32, 64) for a in arena_w]
        PT = [view(a, 2048, 4, S) for a in arena_w]
        xq = [view(a, 0, 4, S) for a in arena_q]
        xk = [view(a, 2048, 4, NK) for a in arena_q]
        xv = [view(a, 4712, 6, 512) for a in arena_q]
        xp = [view(a, 7784, 2, NK) for a in arena_q]
        xo = [view(a, 9116, 4, S) for a in arena_q]
        xPT = [view(a, 0, 2, 6, S) for a in arena_w]
        rot = [view(a, 0, 4, SC) for a in arena_w]
        xr = [v[:].rearrange("p a b -> p (a b)") for v in y]
        lg = [view(a, 0, NT, E) for a in arena_q]
        eq = [view(a, 128, NT, E) for a in arena_q]
        pick = [view(a, 256, NT, E) for a in arena_q]
        oh = [view(a, 384, NT, E) for a in arena_q]
        ohT = [view(a, 512, S) for a in arena_q]
        ohm = [a[:, 1024:1024 + S // 2].bitcast(BF16) for a in arena_q]
        hid = [view(a, 1280, EC, S) for a in arena_q]
        dq = [view(a, 0, S) for a in arena_q]
        dk = [view(a, 512, S) for a in arena_q]
        dv = [view(a, 1024, NT, P) for a in arena_q]
        dz = [view(a, 1536, NT, S) for a in arena_q]
        de = [view(a, 3584, NT, S) for a in arena_q]
        eqT = [view(a, 5632, S) for a in arena_q]
        ekb = [view(a, 6144, SC) for a in arena_q]
        ekm = [view(a, 6298, 4, SC) for a in arena_q]
        evb = [view(a, 6914, 2, P) for a in arena_q]
        evm = [view(a, 7170, 2, 4, P) for a in arena_q]
        esc = [view(a, 8194, 2, 4 * SC) for a in arena_q]
        eo = [view(a, 9426, S) for a in arena_q]
        er = [view(a, 9938, P) for a in arena_q]
        ePT = [view(a, 0, 4, 8, P) for a in arena_w]
        fg = [view(a, 0, NT, FH) for a in arena_q]
        fhT = [view(a, 2048, FC, S) for a in arena_q]

        table16 = arena_w[0][:, 0:sum(CONST16.values())]
        con16, at = {}, 0
        for name, w in CONST16.items():
            con16[name] = table16[:, at:at + w]
            at += w
        wf_raw, wp_raw, wf_t, wp_t = (view(arena_w[1], 512 * k, FC, P) for k in range(4))
        below = view(arena_w[1], 2048, 2, FC, P)
        absd = view(arena_w[1], 3072, 2, FC, P)
        rw_rows = arena_w[1][0:E, 4096:4096 + P]
        dw_vd = arena_w[1][:, 4224:4256]

        PS = [ctx.enter_context(nc.psum_tensor(f"PS{s}", [P, 4 * BANK], F32)) for s in range(STREAMS)]

        def bank(s, i, n=1):
            return PS[s][:, i * BANK:(i + n) * BANK]

        s_table = sem("tables_loaded")
        s_vec = sem("vectors_loaded")
        s_wA, s_wB, s_wC, s_wD, s_wE, s_wF = (sem(f"weights_{n}") for n in "ABCDEF")
        s_pool0 = sem("constants_set")
        s_casts = sem("constants_cast")
        s_absum = sem("abs_summed")
        s_setup_pe = sem("setup_products")
        s_setup_act = sem("setup_copies")
        s_setup_vec = sem("setup_vector")

        gate = signal("turn_open", 1)
        x_in = signal("x_in", 1, 16)
        c_in = signal("c_in", 1, 16)
        stored = signal("stored", 1, 16)
        vown = signal("vector_own", 100)
        var_ready = signal("var_ready", 9)
        rstd_ready = signal("rstd_ready", 9)
        normed = signal("normed", 9)
        turned = signal("turned", 8)
        xT_ready = signal("xT_ready", 8)
        branch = signal("branch_done", 6)
        a_qk, a_lat, a_vw, a_z, a_ro = signals("a_products", 2, 2, 1, 1, 1)
        a_sp, a_vwc, a_tanh, a_rem = signals("a_copied", 3, 1, 1, 1)
        a_pool, a_qm, a_gkv, a_loc, a_mix = signals("a_vector", 1, 1, 2, 2, 1)
        r_sc, r_turn, r_pv = (signal(f"round_{n}", 3) for n in ("scores", "turned", "values"))
        r_exp, r_ea = (signal(f"round_{n}", 3) for n in ("exp", "copied_s"))
        r_sub, r_rs, r_ev = (signal(f"round_{n}", 3) for n in ("subtracted", "rsum", "copied_v"))
        r_p = signal("round_probs", 3)
        x_ck, x_pr = signals("x_products", 3, 3)
        x_ckv, x_cv = signals("x_copied_v", 2, 3)
        x_cva, x_ca = signals("x_copied_s", 1, 3)
        x_sc, x_turn = signal("x_scores", 32), signal("x_turned", 32)
        x_nb, x_e0 = signal("x_bias", 32), signal("x_evac_v", 32)
        x_exp, x_e1 = signal("x_exp", 32), signal("x_evac_s", 32)
        x_pv, x_rr = signal("x_values", 4), signal("x_rsum_spread", 4)
        x_rs, x_no = signal("x_rsum", 4), signal("x_normalised", 4)
        x_rc = signal("x_rsum_copied", 4)
        c_lg, c_ot, c_h = signals("c_products", 1, 1, EC)
        c_oa, c_ha = signals("c_scalar", 1, EC // 2)
        c_oh, c_ov, c_hv = signals("c_vector", 1, 1, EC // 2)
        d_qkv, d_sc, d_tu = signals("d_products", 1, 1, 1)
        d_ca, d_exp, d_ea = signals("d_scalar", 1, 1, 1)
        d_cv, d_nb, d_ev = signals("d_vector", 1, 1, 1)
        e_qkv, e_sc = signals("e_scores", 1, 16)
        e_ca, e_exp = signals("e_exp", 1, 16)
        e_cv, e_sub = signals("e_subtracted", 1, 16)
        e_tu, e_c = signal("e_turned", 16), signal("e_evac", 16)
        e_rs, e_no = signal("e_rsum", NT), signal("e_normalised", NT)
        e_pv, e_rc = signal("e_values", NT), signal("e_rsum_copied", NT)
        f_h, f_tu = signals("f_products", 1, 1)
        f_g, f_ea = signals("f_scalar", 1, 1)
        f_ev = signal("f_evac_v", 1)
        eps_done = signal("eps_added", 9)
        kp_zero = signal("window_zeroed", 1)

        block = ctx.enter_context(nc.Block())

        @block.sync
        def _(sp):
            def load(dst, name, s, ap=None):
                sp.dma_start(dst, io[name] if ap is None else ap).then_inc(s, 16)

            load(table[:], "table", s_table)
            load(table16, "table16", s_table)

            def stream_in(turn, s):
                sp.wait_ge(gate[s].sem, turn + 1)
                b = bass.ds(STREAMS * turn + s, 1)
                sp.dma_start(x_tm[s][:], io["x"][b].rearrange("o (t p) d -> (o p) t d", p=P)).then_inc(x_in[s].sem, 16)
                sp.dma_start(c_tm[s][:], io["ctx_1024"][b].rearrange("o (t p) d -> (o p) t d", p=CH)).then_inc(c_in[s].sem, 16)

            for n, dst in (("wq", w_q), ("wk", w_k), ("wv", w_v), ("wgq", w_gq), ("wgk", w_gk), ("wgv", w_gv),
                           ("r_out_w", w_rout), ("w_out", w_o)):
                load(dst[:], "L0_attn_" + n, s_wA)
            row = 0
            for n in ("L0_attn_gate_local_w", "L0_attn_gate_remote_w"):
                load(vec_rows[row:row + 1, :], None, s_vec, io[n].rearrange("(o h) d -> o (h d)", o=1))
                row += 1
            for n in ("L0_xattn_gamma_x", "L0_xattn_beta_x", "L0_xattn_gamma_l", "L0_xattn_beta_l", "L1_xattn_bq",
                      "L1_xattn_bkv", "L0_ffn_bias1", "L1_ffn_ln_w", "L1_ffn_ln_b"):
                v = io[n][0:P] if n == "L1_xattn_bkv" else io[n]
                v = v.rearrange("(c e) h -> c (e h)", c=EC) if n == "L0_ffn_bias1" else v.rearrange("(c p) -> c p", p=P)
                load(vec_rows[row:row + v.shape[0], :], None, s_vec, v)
                row += v.shape[0]
            assert row == 24
            load(xw_q[:], "L0_xattn_Wq", s_wB)
            load(xw_kv[:], "L0_xattn_Wkv", s_wB)
            load(xw_o[:], None, s_wB, io["L0_xattn_Wo"].rearrange("(c p) n -> p c n", p=P))
            load(rw_rows, "L0_ffn_router_w", s_wC)
            load(rb[:], None, s_wC, io["L0_ffn_router_b"].rearrange("(o e) -> o e", o=1).to_broadcast([P, E]))
            load(w1[:], None, s_wC, io["L0_ffn_weights1"].rearrange("e d h -> d e h"))
            load(w2[:], None, s_wC, io["L0_ffn_weights2"].rearrange("(c e) h d -> (e h) c d", c=EC))
            load(b2[:], "L0_ffn_bias2", s_wC)
            load(dw_q[:], "L1_attn_Wq", s_wD)
            load(dw_k[:], "L1_attn_Wk", s_wD)
            load(dw_vd, "L1_attn_Wvdown", s_wD)
            load(dw_vu[:], "L1_attn_Wvup", s_wD)
            load(ew_q[:], "L1_xattn_Wq", s_wE)
            load(ew_kv[:], "L1_xattn_Wkv", s_wE)
            load(ew_o[:], "L1_xattn_Wo", s_wE)
            load(e_bv[:], None, s_wE, io["L1_xattn_bkv"][P:2 * P].rearrange("(o d) -> o d", o=1).to_broadcast([P, P]))
            load(e_bo[:], None, s_wE, io["L1_xattn_bo"].rearrange("(o d) -> o d", o=1))
            load(wf_raw, None, s_wF, io["L1_ffn_W_fc"].rearrange("(c p) d -> p c d", p=P))
            load(wp_raw, None, s_wF, io["L1_ffn_W_proj"].rearrange("d (c h) -> d c h", h=P))
            with sp.Fori(0, TURNS) as turn:
                for s in range(STREAMS):
                    stream_in(turn, s)
                for s in range(STREAMS):
                    sp.wait_ge(normed[s].sem, normed[s].at(turn, 9))
                    b = bass.ds(STREAMS * turn + s, 1)
                    sp.dma_start(out[b].rearrange("o (t p) d -> (o p) t d", p=P), x_tm[s][:]).then_inc(stored[s].sem, 16)
            for s in range(STREAMS):
                sp.wait_ge(stored[s].sem, 16 * TURNS)

        @block.gpsimd
        def _(pool):
            pool.memset(ones[:], 1.0).then_inc(s_pool0, 1)
            pool.memset(halves[:], -0.5).then_inc(s_pool0, 1)
            pool.memset(epsilon[:], EPS).then_inc(s_pool0, 1)
            for s in range(STREAMS):
                pool.memset(xT[s][:, 0:W], 0.0).then_inc(s_pool0, 1)
            pool.wait_ge(s_pool0, 3 + STREAMS)
            with pool.Fori(0, TURNS) as turn:
                def wait(sig, k):
                    pool.wait_ge(sig.sem, sig.at(turn, k))

                def inv_std(k, s):
                    wait(var_ready[s], k)
                    pool.tensor_tensor(veps[s][:], mv[s][:, :, 1], epsilon[:], ALU.add).then_inc(eps_done[s].sem, 1)
                    wait(eps_done[s], k)
                    pool.tensor_tensor(rstd[s][:], veps[s][:], halves[:], ALU.pow).then_inc(rstd_ready[s].sem, 1)

                def probs(r, s):
                    wait(r_rs[s], r)
                    pool.tensor_tensor(sc[s], sc[s], rsum[s][:, 0:32].unsqueeze(2).to_broadcast([P, 32, 64]),
                                       ALU.mult).then_inc(r_p[s].sem, 1)

                for s in range(STREAMS):
                    inv_std(1, s)
                    pool.memset(KP[s][:, 0:W], 0.0).then_inc(kp_zero[s].sem, 1)
                for r in (1, 2, 3):
                    for s in range(STREAMS):
                        probs(r, s)
                for k in range(2, 10):
                    for s in range(STREAMS):
                        inv_std(k, s)

        @block.tensor
        def _(pe):
            pe.wait_ge(s_pool0, 3 + STREAMS)
            pe.wait_ge(s_absum, 2)
            pe.matmul(bank(0, 0)[:, 0:2], ones[:], gam[:, 0:2], start=True, stop=True).then_inc(s_setup_pe, 1)
            pe.wait_ge(s_table, 32)
            pe.wait_ge(s_vec, 16 * 11)
            pe.transpose(bank(1, 0)[:, 0:24], vec_rows[:], ident[0:24, 0:24]).then_inc(s_setup_pe, 1)
            pe.wait_ge(s_wC, 16 * 5)
            pe.wait_ge(s_wD, 16 * 4)
            pe.transpose(bank(0, 3)[:, 0:E], rw_rows, ident[0:E, 0:E])
            pe.transpose(bank(0, 3)[0:32, E:E + P], dw_vd, ident).then_inc(s_setup_pe, 1)
            pe.wait_ge(s_setup_vec, 12)
            for c in range(FC):
                pe.transpose(bank(0, 1)[:, c * P:(c + 1) * P], wf_t[:, c, :], ident)
            for c in range(FC):
                mm = pe.transpose(bank(0, 2)[:, c * P:(c + 1) * P], wp_t[:, c, :], ident)
            mm.then_inc(s_setup_pe, 1)
            pe.wait_ge(s_setup_act, 2)
            pe.matmul(bank(0, 0)[:, P:2 * P], dw_vdT[:], dw_vu[:], start=True, stop=True).then_inc(s_setup_pe, 1)
            pe.wait_ge(s_setup_act, 5)
            pe.wait_ge(s_casts, 5)
            for q, n in ((s_wA, 8), (s_wB, 3), (s_wE, 5)):
                pe.wait_ge(q, 16 * n)

            with pe.Fori(0, TURNS) as turn:
                def wait(sig, k):
                    pe.wait_ge(sig.sem, sig.at(turn, k))

                def mm(out_, lhsT, rhs, start=True, stop=True):
                    return pe.matmul(out_, lhsT, rhs, start=start, stop=stop, skip_group_check=True)

                def turn_in(s):
                    wait(x_in[s], 1)
                    for t in range(NT):
                        m = pe.transpose(bank(s, 2)[:, t * P:(t + 1) * P], x_tm[s][:, t, :], ident)
                    m.then_inc(turned[s].sem, 1)
                    wait(c_in[s], 1)
                    for t in range(2):
                        m = pe.transpose(bank(s, 3)[:, t * CH:(t + 1) * CH], c_tm[s][:, t, :], ident[0:CH, 0:CH])
                    m.then_inc(turned[s].sem, 1)

                def tokens(s, t):
                    return xT[s][:, W + t * P:W + (t + 1) * P]

                def turn_rows(k, ln, s):
                    wait(normed[s], ln)
                    wait(xT_ready[s], k - 1)
                    for t in range(NT):
                        src = y[s] if k == INNER else x_tm[s]
                        m = pe.transpose(bank(s, 2)[:, t * P:(t + 1) * P], src[:, t, :], ident)
                    m.then_inc(turned[s].sem, 1)

                def qk(s):
                    wait(xT_ready[s], 1)
                    for i, w in enumerate((w_q, w_k)):
                        mm(bank(s, i), w[:], xT[s][:, W:]).then_inc(a_qk[s].sem, 1)

                def latent_qkv(s):
                    wait(xT_ready[s], 2)
                    mm(bank(s, 3)[0:64, :], w_gq[:], xT[s][:, W:]).then_inc(a_lat[s].sem, 1)
                    wait(a_pool[s], 1)
                    mm(bank(s, 2)[0:64, 0:NL], w_gk[:], pooled[s][:, 0, :])
                    mm(bank(s, 2)[:, NL:NL + 64], pooled[s].rearrange("p a n -> p (a n)"),
                       w_gv[:]).then_inc(a_lat[s].sem, 1)

                def window_v(s):
                    wait(a_qm[s], 1)
                    wait(a_sp[s], 2)
                    for m in range(8):
                        for b in range(2):
                            a = 64 * m + W * b
                            v = mm(PS[s][64 * b:64 * b + 64, m * P:(m + 1) * P], xT[s][:, a:a + 64], w_v[:])
                    v.then_inc(a_vw[s].sem, 1)

                def gates(s):
                    wait(a_gkv[s], 2)
                    wait(a_sp[s], 3)
                    mm(bank(s, 2), gate_l[:], QT[s])
                    mm(bank(s, 3), gate_r[:], QT[s]).then_inc(a_z[s].sem, 1)

                def window_scores(r, s):
                    if r == 1:
                        wait(kp_zero[s], 1)
                        wait(a_tanh[s], 1)
                    else:
                        wait(a_loc[s], r - 1)
                    for g in range(4):
                        q = slice(32 * g, 32 * g + 32)
                        mm(bank(s, g), winq[q, :], winmask[q, (r - 1) * P:(r + 3) * P], stop=False)
                    for u in range(8):
                        n = 8 * (r - 1) + u
                        for g in range(4):
                            q = slice(32 * g, 32 * g + 32)
                            m = mm(bank(s, g)[:, u * 64:(u + 1) * 64], Qm[s][q, n].rearrange("p h q -> p (h q)"),
                                   KP[s][q, n * W:(n + 2) * W], start=False)
                    m.then_inc(r_sc[s].sem, 1)

                def latent_scores(s):
                    wait(a_loc[s], 2)
                    for t in range(NT):
                        mm(bank(s, t), identb[:], latmask[:, t, :].unsqueeze(1).to_broadcast([P, 8, NL]), stop=False)
                        m = mm(bank(s, t), GQ[s][0:64, t * P:(t + 1) * P],
                               GKm[s][0:64].rearrange("p h n -> p (h n)"), start=False)
                    m.then_inc(r_sc[s].sem, 1)

                def turn_probs(r, s):
                    wait(r_p[s], r)
                    flat = sc[s].rearrange("p a b -> p (a b)")
                    for i in range(4):
                        for j in range(4):
                            a = (i * 4 + j) * P if r < 3 else (j * 4 + i) * P
                            m = pe.transpose(bank(s, i)[:, j * P:(j + 1) * P], flat[:, a:a + P], ident)
                    m.then_inc(r_turn[s].sem, 1)

                def window_values(r, s):
                    wait(r_ev[s], r)
                    wait(r_ea[s], r)
                    mm(bank(s, 0)[0:32, 0:1], ident[:, 0:32], ident[:, 0:1])
                    for j in range(4):
                        for b in range(2):
                            k = slice(64 * b, 64 * b + 64)
                            for g in range(4):
                                m = mm(bank(s, b)[32 * g:32 * g + 32, j * P:(j + 1) * P],
                                       Vw[s][k, 4 * (r - 1) + j, 32 * g:32 * g + 32], PT[s][k, g, j * P:(j + 1) * P])
                    m.then_inc(r_pv[s].sem, 1)

                def latent_values(s):
                    wait(r_ev[s], 3)
                    wait(r_ea[s], 3)
                    for c in range(4):
                        m = mm(bank(s, 0)[0:64, :], GVm[s][:, c, :], PT[s][:, c, :], start=c == 0, stop=c == 3)
                    m.then_inc(r_pv[s].sem, 1)
                    wait(a_rem[s], 1)
                    mm(bank(s, 1), w_rout[:], remT[s][0:64, :]).then_inc(a_ro[s].sem, 1)

                def out_a(s):
                    wait(a_mix[s], 1)
                    for t in range(NT):
                        m = mm(bank(s, 3)[:, t * P:(t + 1) * P], mixT[s][:, t * P:(t + 1) * P], w_o[:])
                    m.then_inc(branch[s].sem, 1)

                def turn_ctx(s):
                    wait(normed[s], 1)
                    for t in range(2):
                        m = pe.transpose(bank(s, 0)[:, t * CH:(t + 1) * CH], cn[s][:, t, :], ident[0:CH, 0:CH])
                    m.then_inc(turned[s].sem, 1)

                def ctx_keys(s, rotated):
                    if rotated:
                        wait(x_ckv[s], 1)
                    else:
                        wait(xT_ready[s], 3)
                    w = xw_kr if rotated else xw_kv
                    for c in range(4):
                        m = mm(bank(s, c // 2)[:, (c % 2) * SC:(c % 2 + 1) * SC], w[:, c * P:(c + 1) * P], cnT[s][:])
                    m.then_inc(x_ck[s].sem, 1)

                def ctx_values(s):
                    wait(x_ckv[s], 2)
                    for t in range(2):
                        m = mm(bank(s, t)[0:CH, :], cnT[s][:, t * CH:(t + 1) * CH], xw_kv[:, 512:1024])
                    m.then_inc(x_ck[s].sem, 1)

                def x_products(k, s):
                    if k == 1:
                        wait(xT_ready[s], 4)
                        wait(x_cva[s], 1)
                    else:
                        wait(x_cv[s], k - 1)
                        wait(x_ca[s], k - 1)
                    for c in range(4):
                        if k == 1:
                            m = mm(bank(s, c), xw_q[:, c * P:(c + 1) * P], xT[s][:, W:])
                        elif k == 2:
                            m = mm(bank(s, c), xw_kv[:, c * P:(c + 1) * P], xT[s][:, W:])
                        else:
                            m = mm(bank(s, c), tokens(s, c), xw_kv[:, 512:1024])
                    m.then_inc(x_pr[s].sem, 1)

                def x_scores(u, s):
                    h, t = u // 4, u % 4
                    if u == 0:
                        wait(x_cv[s], 3)
                        wait(x_ca[s], 3)
                    else:
                        wait(x_exp[s], u)
                        wait(x_e1[s], u)
                    r = slice(64 * (h % 2), 64 * (h % 2) + 64)
                    q = xq[s][r, h // 2, t * P:(t + 1) * P]
                    mm(bank(s, 0), q, xk[s][r, h // 2, 0:S])
                    mm(bank(s, 1)[:, 0:SC], q, xk[s][r, h // 2, S:NK]).then_inc(x_sc[s].sem, 1)

                def x_turn_probs(u, s):
                    wait(x_exp[s], u + 1)
                    if u:
                        wait(x_e0[s], u)
                    if u % 8 == 0 and u:
                        wait(x_rc[s], u // 8)
                    p = xp[s][:, u % 2, :]
                    for c in range(4):
                        pe.transpose(bank(s, 2)[:, c * P:(c + 1) * P], p[:, c * P:(c + 1) * P], ident)
                    for c in range(2):
                        m = pe.transpose(bank(s, 1)[0:CH, 256 + c * P:256 + (c + 1) * P],
                                         p[:, S + c * CH:S + (c + 1) * CH], ident)
                    m.then_inc(x_turn[s].sem, 1)

                def x_values(hp, s):
                    wait(x_e0[s], 8 * hp + 8)
                    wait(x_e1[s], 8 * hp + 8)
                    if hp:
                        wait(x_no[s], hp)
                    for c in range(6):
                        k = P if c < 4 else CH
                        for h in range(2):
                            col = (2 * hp + h) * 64
                            m = mm(bank(s, 3)[64 * h:64 * h + 64, :], xv[s][0:k, c, col:col + 64],
                                   xPT[s][0:k, h, c, :], start=c == 0, stop=c == 5)
                    m.then_inc(x_pv[s].sem, 1)
                    wait(x_rs[s], hp + 1)
                    for t in range(NT):
                        m = mm(bank(s, 2)[:, t * P:(t + 1) * P], spread[s][:, t * P:(t + 1) * P], ident)
                    m.then_inc(x_rr[s].sem, 1)

                def out_b(s):
                    wait(x_no[s], 4)
                    for t in range(NT):
                        for c in range(4):
                            m = mm(bank(s, 3)[:, t * P:(t + 1) * P], xo[s][:, c, t * P:(t + 1) * P], xw_o[:, c, :],
                                   start=c == 0, stop=c == 3)
                    m.then_inc(branch[s].sem, 1)

                def logits(s):
                    wait(xT_ready[s], 5)
                    for t in range(NT):
                        m = mm(bank(s, 2)[:, t * E:(t + 1) * E], tokens(s, t), rw[:])
                    m.then_inc(c_lg[s].sem, 1)

                def turn_onehot(s):
                    wait(c_oh[s], 1)
                    for t in range(NT):
                        m = pe.transpose(bank(s, 2)[0:E, t * P:(t + 1) * P], oh[s][:, t, :], ident)
                    m.then_inc(c_ot[s].sem, 1)

                def hidden(c, s):
                    if c == 0:
                        wait(c_ov[s], 1)
                        wait(c_oa[s], 1)
                    if c >= 3:
                        wait((c_ha, c_hv)[(c - 3) % 2][s], (c - 3) // 2 + 1)
                    mm(bank(s, c % 3), selb[:, c, :], ohm[s][0:E, :], stop=False)
                    mm(bank(s, c % 3), w1[:, 4 * c:4 * c + 4, :].rearrange("p e h -> p (e h)"), xT[s][:, W:],
                       start=False).then_inc(c_h[s].sem, 1)

                def out_c(s):
                    wait(c_ha[s], 4)
                    wait(c_hv[s], 4)
                    for t in range(NT):
                        cols = slice(t * P, (t + 1) * P)
                        for c in range(EC):
                            mm(bank(s, 3)[:, cols], hid[s][:, c, cols], w2[:, c, :], start=c == 0, stop=False)
                        m = mm(bank(s, 3)[:, cols], ohT[s][0:E, cols], b2[:], start=False)
                    m.then_inc(branch[s].sem, 1)

                def d_products(s):
                    wait(xT_ready[s], 6)
                    mm(bank(s, 0)[0:32, :], dw_q[:], xT[s][:, W:])
                    mm(bank(s, 1)[0:32, :], dw_k[:], xT[s][:, W:])
                    for t in range(NT):
                        m = mm(bank(s, 3)[:, t * P:(t + 1) * P], tokens(s, t), dw_v[:])
                    m.then_inc(d_qkv[s].sem, 1)

                def d_scores(s):
                    wait(d_ca[s], 1)
                    wait(d_cv[s], 1)
                    for t in range(NT):
                        m = mm(bank(s, t), dq[s][0:32, t * P:(t + 1) * P], dk[s][0:32, :])
                    m.then_inc(d_sc[s].sem, 1)

                def d_turn(s):
                    wait(d_exp[s], 1)
                    for c in range(4):
                        for t in range(NT):
                            m = pe.transpose(bank(s, c)[:, t * P:(t + 1) * P], dz[s][:, t, c * P:(c + 1) * P], ident)
                    m.then_inc(d_tu[s].sem, 1)

                def out_d(s):
                    wait(d_ea[s], 1)
                    wait(d_ev[s], 1)
                    for t in range(NT):
                        for c in range(4):
                            m = mm(bank(s, 3)[:, t * P:(t + 1) * P], PT[s][:, c, t * P:(t + 1) * P], dv[s][:, c, :],
                                   start=c == 0, stop=c == 3)
                    m.then_inc(branch[s].sem, 1)

                def e_products(s):
                    wait(xT_ready[s], 7)
                    mm(bank(s, 0), ew_q[:], xT[s][:, W:])
                    mm(bank(s, 1)[:, 0:SC], ew_kv[:, 0:P], cT[s][:])
                    for t in range(2):
                        m = mm(bank(s, 2)[0:CH, t * P:(t + 1) * P], cT[s][:, t * CH:(t + 1) * CH], ew_kv[:, P:2 * P])
                    m.then_inc(e_qkv[s].sem, 1)

                def e_scores(u, s):
                    t, g = u // 4, u % 4
                    if u == 0:
                        wait(e_ca[s], 1)
                        wait(e_cv[s], 1)
                    else:
                        wait(e_sub[s], u)
                        if u % 4 == 1 and u > 4:
                            wait(e_rc[s], u // 4)
                            wait(e_no[s], u // 4)
                    r = slice(32 * g, 32 * g + 32)
                    for k in range(2):
                        m = mm(bank(s, k)[:, 0:2 * SC], eqT[s][r, t * P:(t + 1) * P],
                               ekm[s][r, 2 * k:2 * k + 2, :].rearrange("p h n -> p (h n)"))
                    m.then_inc(e_sc[s].sem, 1)

                def e_turn(u, s):
                    wait(e_exp[s], u + 1)
                    if u:
                        wait(e_c[s], u)
                    for j in range(8):
                        m = pe.transpose(bank(s, 2 + j // 4)[0:CH, (j % 4) * P:(j % 4 + 1) * P],
                                         esc[s][:, u % 2, j * CH:(j + 1) * CH], ident)
                    m.then_inc(e_tu[s].sem, 1)

                def e_values(t, s):
                    wait(e_c[s], 4 * t + 4)
                    if t:
                        wait(e_no[s], t)
                    if t < NT - 1:
                        wait(e_sub[s], 4 * t + 5)
                    for j in range(8):
                        for g in range(4):
                            r = slice(32 * g, 32 * g + 32)
                            mm(bank(s, 1)[r, 384:512], evm[s][0:CH, j % 2, j // 2, r], ePT[s][0:CH, g, j, :],
                               start=j == 0, stop=j == 7)
                    wait(e_rs[s], t + 1)
                    mm(bank(s, 0)[:, 384:512], spread[s][:, t * P:(t + 1) * P], ident).then_inc(e_pv[s].sem, 1)

                def out_e(s):
                    wait(e_no[s], 4)
                    for t in range(NT):
                        cols = slice(t * P, (t + 1) * P)
                        mm(bank(s, 3)[:, cols], eo[s][:, cols], ew_o[:], stop=False)
                        m = mm(bank(s, 3)[:, cols], ones[0:1, :], e_bo[:], start=False)
                    m.then_inc(branch[s].sem, 1)

                def f_hidden(s):
                    wait(xT_ready[s], 8)
                    for t in range(NT):
                        m = mm(bank(s, t), tokens(s, t), wfcT[:])
                    m.then_inc(f_h[s].sem, 1)

                def f_turn(s):
                    wait(normed[s], 8)
                    for c in range(FC):
                        for t in range(NT):
                            m = pe.transpose(bank(s, c)[:, t * P:(t + 1) * P], fg[s][:, t, c * P:(c + 1) * P], ident)
                    m.then_inc(f_tu[s].sem, 1)

                def out_f(s):
                    wait(f_ea[s], 1)
                    wait(f_ev[s], 1)
                    for t in range(NT):
                        for c in range(FC):
                            m = mm(bank(s, 3)[:, t * P:(t + 1) * P], fhT[s][:, c, t * P:(t + 1) * P], wpT[:, c, :],
                                   start=c == 0, stop=c == 3)
                    m.then_inc(branch[s].sem, 1)

                both = range(STREAMS)
                for step in (turn_in, qk, latent_qkv, window_v, gates):
                    for s in both:
                        step(s)
                for r in (1, 2, 3):
                    for s in both:
                        window_scores(r, s) if r < 3 else latent_scores(s)
                    for s in both:
                        turn_probs(r, s)
                    for s in both:
                        window_values(r, s) if r < 3 else latent_values(s)
                for s in both:
                    out_a(s)
                for s in both:
                    turn_ctx(s)
                for s in both:
                    ctx_keys(s, False)
                for s in both:
                    ctx_keys(s, True)
                for s in both:
                    turn_rows(INNER, 3, s)
                for s in both:
                    ctx_values(s)
                for k in (1, 2, 3):
                    for s in both:
                        x_products(k, s)
                steps = [(u, s) for u in range(32) for s in both]
                for n in range(len(steps) + 3):
                    if n < len(steps):
                        x_scores(*steps[n])
                    if n >= 3 and steps[n - 3][0] % 8 == 7:
                        x_values(steps[n - 3][0] // 8, steps[n - 3][1])
                    if 1 <= n <= len(steps):
                        x_turn_probs(*steps[n - 1])
                for s in both:
                    out_b(s)
                for s in both:
                    turn_rows(5, 4, s)
                for s in both:
                    logits(s)
                for s in both:
                    turn_onehot(s)
                for c in range(EC):
                    for s in both:
                        hidden(c, s)
                for s in both:
                    out_c(s)
                for s in both:
                    turn_rows(6, 5, s)
                for step in (d_products, d_scores, d_turn, out_d):
                    for s in both:
                        step(s)
                for s in both:
                    turn_rows(7, 6, s)
                for s in both:
                    e_products(s)
                steps = [(u, s) for u in range(16) for s in both]
                for n in range(len(steps) + 3):
                    if n < len(steps):
                        e_scores(*steps[n])
                    if 1 <= n <= len(steps):
                        e_turn(*steps[n - 1])
                    if n >= 3 and steps[n - 3][0] % 4 == 3:
                        e_values(steps[n - 3][0] // 4, steps[n - 3][1])
                for s in both:
                    out_e(s)
                for s in both:
                    turn_rows(8, 7, s)
                for step in (f_hidden, f_turn, out_f):
                    for s in both:
                        step(s)

        @block.scalar
        def _(act):
            def copy(dst, src):
                return act.activation(dst, src, ACT.Copy)

            act.wait_ge(s_wF, 16 * 2)
            for k, w in enumerate((wf_raw, wp_raw)):
                act.activation(absd[:, k], w, ACT.Abs, accum_out=gam[:, k:k + 1]).then_inc(s_absum, 1)
            act.wait_ge(s_setup_pe, 3)
            copy(rw[:], bank(0, 3)[:, 0:E]).then_inc(s_setup_act, 1)
            copy(dw_vdT[:], bank(0, 3)[0:32, E:E + P]).then_inc(s_setup_act, 1)
            act.wait_ge(s_setup_pe, 4)
            copy(wfcT[:], bank(0, 1)).then_inc(s_setup_act, 1)
            copy(wpT[:].rearrange("p c d -> p (c d)"), bank(0, 2)).then_inc(s_setup_act, 1)
            act.wait_ge(s_setup_pe, 5)
            copy(dw_v[:], bank(0, 0)[:, P:2 * P]).then_inc(s_setup_act, 1)
            act.wait_ge(s_setup_vec, 1)

            with act.Fori(0, TURNS) as turn:
                def wait(sig, k):
                    act.wait_ge(sig.sem, sig.at(turn, k))

                def affine(dst, src, scale, bias):
                    return act.activation(dst, src, ACT.Identity, scale=scale, bias=bias)

                def rows_to_T(k, s):
                    wait(turned[s], k)
                    if k == 2:
                        m = copy(cT[s][:], bank(s, 3)[:, 0:SC])
                    elif k == 3:
                        m = affine(cnT[s][:], bank(s, 0)[:, 0:SC], lnp[:, 0:1], lnp[:, 1:2])
                    elif k == INNER:
                        m = affine(xT[s][:, W:], bank(s, 2), lnp[:, 2:3], lnp[:, 3:4])
                    else:
                        m = copy(xT[s][:, W:], bank(s, 2))
                    m.then_inc(xT_ready[s].sem, 1)

                def copy_qk(s):
                    wait(a_qk[s], 2)
                    copy(KP[s][:, W:], bank(s, 1)).then_inc(a_sp[s].sem, 1)
                    wait(a_qm[s], 1)
                    copy(QT[s], bank(s, 0)).then_inc(a_sp[s].sem, 1)

                def copy_gq(s):
                    wait(a_lat[s], 1)
                    copy(GQ[s][0:64, :], bank(s, 3)[0:64, :]).then_inc(a_sp[s].sem, 1)

                def copy_window_v(s):
                    wait(a_vw[s], 1)
                    copy(Vw[s].rearrange("p a b -> p (a b)"), bank(s, 0, 2)).then_inc(a_vwc[s].sem, 1)

                def tanh_gates(s):
                    wait(a_z[s], 1)
                    act.activation(tl[s], bank(s, 2), ACT.Tanh, scale=0.5)
                    act.activation(tr[s], bank(s, 3), ACT.Tanh, scale=0.5).then_inc(a_tanh[s].sem, 1)

                def exp_round(r, s):
                    wait(r_sub[s], r)
                    act.activation(sc[s], sc[s], ACT.Exp, scale=HD ** -0.5).then_inc(r_exp[s].sem, 1)

                def copy_round(r, s):
                    wait(r_turn[s], r)
                    copy(PT[s][:, 2:4, :].rearrange("p a b -> p (a b)"), bank(s, 2, 2)).then_inc(r_ea[s].sem, 1)

                def copy_remote(s):
                    wait(r_pv[s], 3)
                    copy(remT[s][0:64, :], bank(s, 0)[0:64, :]).then_inc(a_rem[s].sem, 1)

                def copy_ctx_values(s):
                    wait(x_ck[s], 3)
                    copy(xv[s][0:CH, 4:6, :].rearrange("p a b -> p (a b)"),
                         bank(s, 0, 2)[0:CH, :]).then_inc(x_cva[s].sem, 1)

                def copy_x(k, s):
                    wait(x_pr[s], k)
                    dst = (xq[s][:, 2:4, :], xk[s][:, 2:4, 0:S], xv[s][:, 2:4, :])[k - 1]
                    copy(dst, bank(s, 2, 2).rearrange("p (a b) -> p a b", a=2)).then_inc(x_ca[s].sem, 1)

                def x_exp_unit(u, s):
                    wait(x_nb[s], u + 1)
                    if u >= 2:
                        wait(x_turn[s], u - 1)
                    act.activation(xp[s][:, u % 2, :], PS[s][:, 0:NK], ACT.Exp, scale=XD ** -0.5, bias=nb[s][:, u:u + 1],
                                   accum_out=sums[s][:, u:u + 1]).then_inc(x_exp[s].sem, 1)

                def x_copy_ctx_part(u, s):
                    wait(x_turn[s], u + 1)
                    if u % 8 == 0 and u:
                        wait(x_pv[s], u // 8)
                    t = u % 4
                    copy(xPT[s][0:CH, (u // 4) % 2, 4:6, t * P:(t + 1) * P],
                         bank(s, 1)[0:CH, 256:512].rearrange("p (a b) -> p a b", a=2)).then_inc(x_e1[s].sem, 1)

                def x_copy_rsum(hp, s):
                    wait(x_rr[s], hp + 1)
                    if hp:
                        wait(x_no[s], hp)
                    copy(xr[s], bank(s, 2)).then_inc(x_rc[s].sem, 1)

                def copy_onehot(s):
                    wait(c_ot[s], 1)
                    copy(ohT[s][0:E, :], bank(s, 2)[0:E, :]).then_inc(c_oa[s].sem, 1)

                def relu(c, s):
                    wait(c_h[s], c + 1)
                    act.activation(hid[s][:, c, :], bank(s, c % 3), ACT.Relu, bias=b1[:, c:c + 1]).then_inc(c_ha[s].sem, 1)

                def copy_dqk(s):
                    wait(d_qkv[s], 1)
                    copy(dq[s][0:32, :], bank(s, 0)[0:32, :])
                    copy(dk[s][0:32, :], bank(s, 1)[0:32, :]).then_inc(d_ca[s].sem, 1)

                def d_exp_rows(s):
                    wait(d_nb[s], 1)
                    for t in range(NT):
                        m = act.activation(dz[s][:, t, :], dz[s][:, t, :], ACT.Exp, bias=nb[s][:, t:t + 1],
                                           accum_out=sums[s][:, t:t + 1])
                    m.then_inc(d_exp[s].sem, 1)

                def copy_d(s):
                    wait(d_tu[s], 1)
                    copy(PT[s][:, 2:4, :].rearrange("p a b -> p (a b)"), bank(s, 2, 2)).then_inc(d_ea[s].sem, 1)

                def copy_eq(s):
                    wait(e_qkv[s], 1)
                    act.activation(eqT[s], bank(s, 0), ACT.Identity, bias=e_bq).then_inc(e_ca[s].sem, 1)

                def e_exp_unit(u, s):
                    wait(e_sub[s], u + 1)
                    act.activation(esc[s][:, u % 2, :], esc[s][:, u % 2, :], ACT.Exp,
                                   scale=HD ** -0.5).then_inc(e_exp[s].sem, 1)

                def e_copy_probs(u, s):
                    wait(e_tu[s], u + 1)
                    if u % 4 == 0 and u:
                        wait(e_pv[s], u // 4)
                    copy(ePT[s][0:CH, u % 4].rearrange("p a b -> p (a b)"), bank(s, 2, 2)[0:CH, :]).then_inc(e_c[s].sem, 1)

                def e_copy_rsum(t, s):
                    wait(e_pv[s], t + 1)
                    if t:
                        wait(e_no[s], t)
                    copy(er[s], bank(s, 0)[:, 384:512]).then_inc(e_rc[s].sem, 1)

                def gelu(s):
                    wait(f_h[s], 1)
                    act.activation(fg[s].rearrange("p a b -> p (a b)"), PS[s][:], ACT.Gelu).then_inc(f_g[s].sem, 1)

                def copy_f(s):
                    wait(f_tu[s], 1)
                    for c in (2, 3):
                        m = affine(fhT[s][:, c, :], bank(s, c), f_w[:, c:c + 1], f_b[:, c:c + 1])
                    m.then_inc(f_ea[s].sem, 1)

                both = range(STREAMS)
                for s in both:
                    rows_to_T(1, s)
                    rows_to_T(2, s)
                for step in (copy_qk, copy_gq, copy_window_v, tanh_gates):
                    for s in both:
                        step(s)
                for r in (1, 2, 3):
                    for s in both:
                        exp_round(r, s)
                    for s in both:
                        copy_round(r, s)
                for s in both:
                    copy_remote(s)
                for s in both:
                    rows_to_T(3, s)
                for s in both:
                    rows_to_T(INNER, s)
                for s in both:
                    copy_ctx_values(s)
                for k in (1, 2, 3):
                    for s in both:
                        copy_x(k, s)
                steps = [(u, s) for u in range(32) for s in both]
                for n in range(len(steps) + 3):
                    if n < len(steps):
                        x_exp_unit(*steps[n])
                    if n >= 3 and steps[n - 3][0] % 8 == 7:
                        x_copy_rsum(steps[n - 3][0] // 8, steps[n - 3][1])
                    if 1 <= n <= len(steps):
                        x_copy_ctx_part(*steps[n - 1])
                for s in both:
                    rows_to_T(5, s)
                for s in both:
                    copy_onehot(s)
                for c in range(0, EC, 2):
                    for s in both:
                        relu(c, s)
                for s in both:
                    rows_to_T(6, s)
                for step in (copy_dqk, d_exp_rows, copy_d):
                    for s in both:
                        step(s)
                for s in both:
                    rows_to_T(7, s)
                for s in both:
                    copy_eq(s)
                steps = [(u, s) for u in range(16) for s in both]
                for n in range(len(steps) + 3):
                    if n < len(steps):
                        e_exp_unit(*steps[n])
                    if 1 <= n <= len(steps):
                        e_copy_probs(*steps[n - 1])
                    if n >= 3 and steps[n - 3][0] % 4 == 3:
                        e_copy_rsum(steps[n - 3][0] // 4, steps[n - 3][1])
                for s in both:
                    rows_to_T(8, s)
                for step in (gelu, copy_f):
                    for s in both:
                        step(s)

        @block.vector
        def _(dve):
            dve.wait_ge(s_table, 32)
            for dst, src in ((latmask[:].rearrange("p a b -> p (a b)"), con16["latmask"]), (winmask[:], con16["winmask"]),
                             (winq[:], con16["winq"]), (identb[:], ident),
                             (selb[:].rearrange("p a b -> p (a b)"), con16["sel"][0:E])):
                dve.tensor_copy(dst, src).then_inc(s_casts, 1)
            dve.wait_ge(s_setup_pe, 2)
            dve.tensor_copy(vec[:], bank(1, 0)[:, 0:24]).then_inc(s_setup_vec, 1)
            dve.wait_ge(s_setup_vec, 1)
            dve.tensor_scalar(gate_l[:], con["headblk"], gatew[:, 0:1], None, ALU.mult).then_inc(s_setup_vec, 1)
            dve.tensor_scalar(gate_r[:], con["headblk"], gatew[:, 1:2], None, ALU.mult).then_inc(s_setup_vec, 1)
            dve.wait_ge(s_wB, 16 * 3)
            wk, wr = (w.rearrange("p (h d) -> p h d", d=XD) for w in (xw_kv[:, 0:512], xw_kr[:]))
            dve.tensor_scalar(wr[:, :, 0:32], wk[:, :, 32:64], -1.0, None, ALU.mult).then_inc(s_setup_vec, 1)
            dve.tensor_copy(wr[:, :, 32:64], wk[:, :, 0:32]).then_inc(s_setup_vec, 1)
            dve.wait_ge(s_setup_pe, 1)
            dve.tensor_scalar(gam[:, 2:4], bank(0, 0)[:, 0:2], 1.0 / (FH * D), 1e-6, ALU.mult, ALU.add).then_inc(s_setup_vec, 1)
            dve.wait_ge(s_setup_vec, 6)
            dve.tensor_scalar(gam[:, 4:6], gam[:, 2:4], 0.5, None, ALU.mult).then_inc(s_setup_vec, 1)
            dve.tensor_scalar(gam[:, 6:8], gam[:, 2:4], -0.5, None, ALU.mult).then_inc(s_setup_vec, 1)
            dve.wait_ge(s_setup_vec, 8)
            dve.wait_ge(s_wF, 16 * 2)
            for k, w in enumerate((wf_raw, wp_raw)):
                dve.tensor_scalar(below[:, k], w, gam[:, 6 + k:7 + k], None, ALU.is_lt).then_inc(s_setup_vec, 1)
            dve.wait_ge(s_setup_vec, 10)
            for k, (w, t) in enumerate(((wf_raw, wf_t), (wp_raw, wp_t))):
                dve.scalar_tensor_tensor(out=t, in0=w, scalar=gam[:, 4 + k:5 + k], in1=below[:, k], op0=ALU.is_gt,
                                         op1=ALU.subtract).then_inc(s_setup_vec, 1)
            for s in range(STREAMS):
                dve.memset(mv[s][:], 1.0).then_inc(gate[s].sem, 1)
            for q, n in ((s_wC, 5), (s_wE, 5)):
                dve.wait_ge(q, 16 * n)

            with dve.Fori(0, TURNS) as turn:
                steps_own = [0] * STREAMS

                def wait(sig, k):
                    dve.wait_ge(sig.sem, sig.at(turn, k))

                def own(s, ins):
                    steps_own[s] += 1
                    ins.then_inc(vown[s].sem, 1)
                    wait(vown[s], steps_own[s])

                def stats(k, s, src, n, rows=P):
                    for t in range(n):
                        m = dve.bn_stats(bn[s][0:rows, t, :], src[:, t, :])
                    own(s, m)
                    dve.memset(spacer[:], 0.0)
                    for t in range(n):
                        m = dve.bn_aggr(mv[s][0:rows, t, :], bn[s][0:rows, t, :])
                    m.then_inc(var_ready[s].sem, 1)

                def normalise(k, s, dst, src, n, rows=P):
                    wait(rstd_ready[s], k)
                    for t in range(n):
                        m = dve.tensor_scalar(dst[:, t, :], src[:, t, :], mv[s][0:rows, t, 0:1], rstd[s][0:rows, t:t + 1],
                                              ALU.subtract, ALU.mult)
                    m.then_inc(normed[s].sem, 1)

                def residual(b, k, s, scalar, op):
                    wait(branch[s], b)
                    own(s, dve.scalar_tensor_tensor(out=y[s][:].rearrange("p a b -> p (a b)"), in0=bank(s, 3),
                                                    scalar=scalar, in1=x_tm[s][:].rearrange("p a b -> p (a b)"),
                                                    op0=op, op1=ALU.add))
                    stats(k, s, y[s], NT)

                def ctx_stats(s):
                    wait(c_in[s], 1)
                    stats(1, s, c_tm[s], 2, CH)

                def pool_latents(s):
                    wait(xT_ready[s], 1)
                    own(s, dve.tensor_reduce(pooled[s][:, 0, :], xT[s][:, W:].rearrange("p (n k) -> p n k", k=S // NL), AX, ALU.add))
                    own(s, dve.tensor_scalar(pooled[s][:, 1, :], pooled[s][:, 0, :], NL / S, None, ALU.mult))
                    dve.tensor_copy(pooled[s][:, 0, :], pooled[s][:, 1, :]).then_inc(a_pool[s].sem, 1)

                def mask_q(s):
                    wait(a_qk[s], 1)
                    shape = [P, S // W, 4, W]
                    dve.tensor_tensor(Qm[s], bank(s, 0).rearrange("p (n q) -> p n q", q=W).unsqueeze(2).to_broadcast(shape),
                                      mask4.unsqueeze(1).unsqueeze(3).to_broadcast(shape), ALU.mult).then_inc(a_qm[s].sem, 1)

                def mask_latents(s):
                    wait(a_lat[s], 2)
                    dve.tensor_tensor(GKm[s][0:64], bank(s, 2)[0:64, 0:NL].unsqueeze(1).to_broadcast([64, 8, NL]),
                                      con["mask8"][0:64].unsqueeze(2).to_broadcast([64, 8, NL]),
                                      ALU.mult).then_inc(a_gkv[s].sem, 1)
                    dve.tensor_tensor(GVm[s], bank(s, 2)[:, NL:NL + 64].unsqueeze(1).to_broadcast([P, 4, 64]),
                                      con["gvmask"].rearrange("p (c f) -> p c f", c=4), ALU.mult).then_inc(a_gkv[s].sem, 1)

                def subtract_max(r, s):
                    wait(r_sc[s], r)
                    scores = PS[s][:].rearrange("p (u n) -> p u n", n=64)
                    own(s, dve.tensor_reduce(mx[s][:, 0:32], scores, AX, ALU.max))
                    dve.tensor_tensor(sc[s], scores, mx[s][:, 0:32].unsqueeze(2).to_broadcast([P, 32, 64]),
                                      ALU.subtract).then_inc(r_sub[s].sem, 1)

                def row_sums(r, s):
                    wait(r_exp[s], r)
                    own(s, dve.tensor_reduce(sums[s][:, 0:32], sc[s], AX, ALU.add))
                    dve.reciprocal(rsum[s][:, 0:32], sums[s][:, 0:32]).then_inc(r_rs[s].sem, 1)

                def copy_round(r, s):
                    wait(r_turn[s], r)
                    dve.tensor_copy(PT[s][:, 0:2, :].rearrange("p a b -> p (a b)"), bank(s, 0, 2)).then_inc(r_ev[s].sem, 1)

                def pick_heads(r, s):
                    wait(r_pv[s], r)
                    own(s, dve.tensor_tensor(picked[s].rearrange("p u h q -> p u h q"),
                                             bank(s, 0, 2).rearrange("p (u h q) -> p u h q", h=4, q=W),
                                             mask4.unsqueeze(1).unsqueeze(3).to_broadcast([P, 8, 4, W]), ALU.mult))
                    half = loc[s][:, (r - 1) * 256:r * 256].rearrange("p (m b q) -> p m b q", m=4, b=2)
                    for b in range(2):
                        m = dve.tensor_reduce(half[:, :, b, :],
                                              picked[s][:, 4 * b:4 * b + 4].rearrange("p u h q -> p u q h"), AX, ALU.add)
                    m.then_inc(a_loc[s].sem, 1)

                def mix(s):
                    wait(a_tanh[s], 1)
                    wait(a_loc[s], 2)
                    own(s, dve.scalar_tensor_tensor(out=loc[s], in0=tl[s], scalar=1.0, in1=loc[s], op0=ALU.add, op1=ALU.mult))
                    wait(a_ro[s], 1)
                    own(s, dve.scalar_tensor_tensor(out=tr[s], in0=tr[s], scalar=1.0, in1=bank(s, 1), op0=ALU.add,
                                                    op1=ALU.mult))
                    dve.tensor_tensor(mixT[s], loc[s], tr[s], ALU.add).then_inc(a_mix[s].sem, 1)

                def ctx_keys(s):
                    pairs = PS[s][:, 0:2 * BANK].rearrange("p (b c) -> p b c", b=2)[:, :, 0:2 * SC]
                    pairs = pairs.rearrange("p b (k j) -> p b k j", k=2)
                    spread = [con[n].unsqueeze(1).unsqueeze(1).to_broadcast([P, 2, 2, SC]) for n in ("cos", "sin")]
                    keys = xk[s][:, :, S:NK]
                    wait(x_ck[s], 1)
                    dve.tensor_tensor(keys.rearrange("p (b k) j -> p b k j", b=2), pairs, spread[0],
                                      ALU.mult).then_inc(x_ckv[s].sem, 1)
                    wait(x_ck[s], 2)
                    own(s, dve.tensor_tensor(rot[s].rearrange("p (b k) j -> p b k j", b=2), pairs, spread[1], ALU.mult))
                    wait(x_ckv[s], 1)
                    dve.tensor_tensor(keys, keys, rot[s], ALU.add).then_inc(x_ckv[s].sem, 1)

                def copy_x(k, s):
                    wait(x_pr[s], k)
                    dst = (xq[s][:, 0:2, :], xk[s][:, 0:2, 0:S], xv[s][:, 0:2, :])[k - 1]
                    dve.tensor_copy(dst, bank(s, 0, 2).rearrange("p (a b) -> p a b", a=2)).then_inc(x_cv[s].sem, 1)

                def x_max(u, s):
                    wait(x_sc[s], u + 1)
                    own(s, dve.tensor_reduce(mx[s][:, u:u + 1], PS[s][:, 0:NK], AX, ALU.max))
                    dve.tensor_scalar(nb[s][:, u:u + 1], mx[s][:, u:u + 1], -(XD ** -0.5), None,
                                      ALU.mult).then_inc(x_nb[s].sem, 1)

                def x_copy_probs(u, s):
                    wait(x_turn[s], u + 1)
                    if u % 8 == 0 and u:
                        wait(x_pv[s], u // 8)
                    t = u % 4
                    dve.tensor_copy(xPT[s][:, (u // 4) % 2, 0:4, t * P:(t + 1) * P],
                                    bank(s, 2).rearrange("p (a b) -> p a b", a=4)).then_inc(x_e0[s].sem, 1)

                def x_rsum(hp, s):
                    wait(x_exp[s], 8 * hp + 8)
                    if hp:
                        wait(x_rr[s], hp)
                    total = sums[s][:, 8 * hp:8 * hp + 8].rearrange("p (h t) -> p t h", h=2)
                    inv = rsum[s][:, 8 * hp:8 * hp + 8].rearrange("p (t h) -> p t h", h=2)
                    own(s, dve.reciprocal(inv, total))
                    dve.tensor_copy(spread[s][:].rearrange("p (t h d) -> p t h d", t=NT, h=2),
                                    inv.unsqueeze(3).to_broadcast([P, NT, 2, 64])).then_inc(x_rs[s].sem, 1)

                def x_normalise(hp, s):
                    wait(x_pv[s], hp + 1)
                    wait(x_rc[s], hp + 1)
                    dve.tensor_tensor(xo[s][:, hp, :], bank(s, 3), xr[s], ALU.mult).then_inc(x_no[s].sem, 1)

                def choose(s):
                    wait(c_lg[s], 1)
                    iota = con["iota"].unsqueeze(1).to_broadcast([P, NT, E])
                    own(s, dve.tensor_tensor(lg[s], bank(s, 2)[:, 0:NT * E].rearrange("p (t e) -> p t e", t=NT),
                                             rb[:].unsqueeze(1).to_broadcast([P, NT, E]), ALU.add))
                    own(s, dve.tensor_reduce(mx[s][:, 0:NT], lg[s], AX, ALU.max))
                    own(s, dve.tensor_tensor(eq[s], lg[s], mx[s][:, 0:NT].unsqueeze(2).to_broadcast([P, NT, E]),
                                             ALU.is_equal))
                    own(s, dve.tensor_tensor(pick[s], eq[s], iota, ALU.mult))
                    own(s, dve.tensor_reduce(mx[s][:, NT:2 * NT], pick[s], AX, ALU.min))
                    dve.tensor_tensor(oh[s], iota, mx[s][:, NT:2 * NT].unsqueeze(2).to_broadcast([P, NT, E]),
                                      ALU.is_equal).then_inc(c_oh[s].sem, 1)

                def onehot_less_one(s):
                    wait(c_oa[s], 1)
                    dve.tensor_scalar(ohm[s][0:E, :], ohT[s][0:E, :], -1.0, None, ALU.add).then_inc(c_ov[s].sem, 1)

                def relu(c, s):
                    wait(c_h[s], c + 1)
                    dve.tensor_scalar(hid[s][:, c, :], bank(s, c % 3), b1[:, c:c + 1], 0.0, ALU.add,
                                      ALU.max).then_inc(c_hv[s].sem, 1)

                def copy_dv(s):
                    wait(d_qkv[s], 1)
                    dve.tensor_copy(dv[s].rearrange("p a b -> p (a b)"), bank(s, 3)).then_inc(d_cv[s].sem, 1)

                def d_mask(s):
                    wait(d_sc[s], 1)
                    for t in range(NT):
                        a = S - P - t * P
                        m = dve.scalar_tensor_tensor(out=dz[s][:, t, :], in0=bank(s, t), scalar=32 ** -0.5,
                                                     in1=con["tri"][:, a:a + S], op0=ALU.mult, op1=ALU.mult)
                    own(s, m)
                    own(s, dve.tensor_scalar(de[s], dz[s], 0.0, FMIN, ALU.is_equal, ALU.mult))
                    own(s, dve.tensor_tensor(dz[s], dz[s], de[s], ALU.add))
                    own(s, dve.tensor_reduce(mx[s][:, 0:NT], dz[s], AX, ALU.max))
                    dve.tensor_scalar(nb[s][:, 0:NT], mx[s][:, 0:NT], -1.0, None, ALU.mult).then_inc(d_nb[s].sem, 1)

                def copy_d(s):
                    wait(d_exp[s], 1)
                    own(s, dve.reciprocal(rsum[s][:, 0:NT], sums[s][:, 0:NT]))
                    wait(d_tu[s], 1)
                    dve.tensor_copy(PT[s][:, 0:2, :].rearrange("p a b -> p (a b)"), bank(s, 0, 2)).then_inc(d_ev[s].sem, 1)

                def residual_d(s):
                    wait(branch[s], 4)
                    for t in range(NT):
                        m = dve.scalar_tensor_tensor(out=y[s][:, t, :], in0=bank(s, 3)[:, t * P:(t + 1) * P],
                                                     scalar=rsum[s][:, t:t + 1], in1=x_tm[s][:, t, :], op0=ALU.mult,
                                                     op1=ALU.add)
                    own(s, m)
                    stats(6, s, y[s], NT)

                def mask_ctx(s):
                    wait(e_qkv[s], 1)
                    own(s, dve.tensor_scalar(ekb[s], bank(s, 1)[:, 0:SC], e_bk, None, ALU.add))
                    dve.tensor_tensor(ekm[s], ekb[s].unsqueeze(1).to_broadcast([P, 4, SC]),
                                      mask4.unsqueeze(2).to_broadcast([P, 4, SC]), ALU.mult)
                    own(s, dve.tensor_tensor(evb[s][0:CH], bank(s, 2)[0:CH, 0:2 * P].rearrange("p (c f) -> p c f", c=2),
                                             e_bv[0:CH].unsqueeze(1).to_broadcast([CH, 2, P]), ALU.add))
                    heads = con["hmaskf"][0:CH].rearrange("p (h f) -> p h f", h=4)
                    dve.tensor_tensor(evm[s][0:CH], evb[s][0:CH].unsqueeze(2).to_broadcast([CH, 2, 4, P]),
                                      heads.unsqueeze(1).to_broadcast([CH, 2, 4, P]), ALU.mult).then_inc(e_cv[s].sem, 1)

                def e_subtract_max(u, s):
                    wait(e_sc[s], u + 1)
                    if u >= 2:
                        wait(e_tu[s], u - 1)
                    scores = PS[s][:, 0:2 * BANK].rearrange("p (b c) -> p b c", b=2)[:, :, 0:2 * SC]
                    scores = scores.rearrange("p b (k j) -> p b k j", k=2)
                    top = mx[s][:, 4 * u:4 * u + 4].rearrange("p (b k) -> p b k", b=2)
                    own(s, dve.tensor_reduce(top, scores, AX, ALU.max))
                    dve.tensor_tensor(esc[s][:, u % 2, :].rearrange("p (b k j) -> p b k j", b=2, k=2), scores,
                                      top.unsqueeze(3).to_broadcast([P, 2, 2, SC]), ALU.subtract).then_inc(e_sub[s].sem, 1)

                def e_sums(u, s):
                    wait(e_exp[s], u + 1)
                    m = dve.tensor_reduce(sums[s][:, 4 * u:4 * u + 4],
                                          esc[s][:, u % 2, :].rearrange("p (h j) -> p h j", h=4), AX, ALU.add)
                    if u % 4 == 3:
                        own(s, m)
                        t = u // 4
                        heads = slice(16 * t, 16 * t + 16)
                        own(s, dve.reciprocal(rsum[s][:, heads], sums[s][:, heads]))
                        dve.tensor_copy(spread[s][:, t * P:(t + 1) * P].rearrange("p (h d) -> p h d", h=16),
                                        rsum[s][:, heads].unsqueeze(2).to_broadcast([P, 16, HD])
                                        ).then_inc(e_rs[s].sem, 1)

                def e_normalise(t, s):
                    wait(e_pv[s], t + 1)
                    wait(e_rc[s], t + 1)
                    dve.tensor_tensor(eo[s][:, t * P:(t + 1) * P], bank(s, 1)[:, 384:512], er[s],
                                      ALU.mult).then_inc(e_no[s].sem, 1)

                def copy_f(s):
                    wait(f_tu[s], 1)
                    for c in (0, 1):
                        m = dve.tensor_scalar(fhT[s][:, c, :], bank(s, c), f_w[:, c:c + 1], f_b[:, c:c + 1],
                                              ALU.mult, ALU.add)
                    m.then_inc(f_ev[s].sem, 1)

                both = range(STREAMS)
                for s in both:
                    ctx_stats(s)
                for s in both:
                    pool_latents(s)
                for s in both:
                    mask_q(s)
                for s in both:
                    normalise(1, s, cn[s], c_tm[s], 2, CH)
                    mask_latents(s)
                for r in (1, 2, 3):
                    for s in both:
                        subtract_max(r, s)
                    for s in both:
                        row_sums(r, s)
                    for s in both:
                        copy_round(r, s)
                    if r < 3:
                        for s in both:
                            pick_heads(r, s)
                for s in both:
                    mix(s)
                for s in both:
                    residual(1, 2, s, 0.5, ALU.mult)
                for s in both:
                    normalise(2, s, x_tm[s], y[s], NT)
                for s in both:
                    wait(normed[s], 2)
                    stats(3, s, x_tm[s], NT)
                for s in both:
                    normalise(3, s, y[s], x_tm[s], NT)
                for s in both:
                    ctx_keys(s)
                for k in (1, 2, 3):
                    for s in both:
                        copy_x(k, s)
                steps = [(u, s) for u in range(32) for s in both]
                for n in range(len(steps) + 3):
                    if n < len(steps):
                        x_max(*steps[n])
                    if n >= 3 and steps[n - 3][0] % 8 == 7:
                        x_rsum(steps[n - 3][0] // 8, steps[n - 3][1])
                        x_normalise(steps[n - 3][0] // 8, steps[n - 3][1])
                    if 1 <= n <= len(steps):
                        x_copy_probs(*steps[n - 1])
                for s in both:
                    residual(2, 4, s, 1.0, ALU.mult)
                for s in both:
                    normalise(4, s, x_tm[s], y[s], NT)
                for s in both:
                    choose(s)
                for s in both:
                    onehot_less_one(s)
                for c in range(1, EC, 2):
                    for s in both:
                        relu(c, s)
                for s in both:
                    residual(3, 5, s, 0.0, ALU.max)
                for s in both:
                    normalise(5, s, x_tm[s], y[s], NT)
                for step in (copy_dv, d_mask, copy_d, residual_d):
                    for s in both:
                        step(s)
                for s in both:
                    normalise(6, s, x_tm[s], y[s], NT)
                for s in both:
                    mask_ctx(s)
                steps = [(u, s) for u in range(16) for s in both]
                for n in range(len(steps) + 3):
                    if n < len(steps):
                        e_subtract_max(*steps[n])
                    if 1 <= n <= len(steps):
                        e_sums(*steps[n - 1])
                    if n >= 3 and steps[n - 3][0] % 4 == 3:
                        e_normalise(steps[n - 3][0] // 4, steps[n - 3][1])
                for s in both:
                    residual(5, 7, s, 1.0, ALU.mult)
                for s in both:
                    normalise(7, s, x_tm[s], y[s], NT)
                for s in both:
                    wait(f_g[s], 1)
                    stats(8, s, fg[s], NT)
                for s in both:
                    normalise(8, s, fg[s], fg[s], NT)
                for s in both:
                    copy_f(s)
                for s in both:
                    residual(6, 9, s, 1.0, ALU.mult)
                for s in both:
                    normalise(9, s, x_tm[s], y[s], NT)
                for s in both:
                    wait(stored[s], 1)
                    dve.memset(mv[s][:], 1.0).then_inc(gate[s].sem, 1)
                assert steps_own == [vown[0].per] * STREAMS, steps_own


_INS = ["L0_attn_wq", "L0_attn_wk", "L0_attn_wv", "L0_attn_wgq", "L0_attn_wgk", "L0_attn_wgv", "L0_attn_r_out_w",
        "L0_attn_gate_local_w", "L0_attn_gate_remote_w", "L0_attn_w_out", "L0_xattn_gamma_x", "L0_xattn_beta_x",
        "L0_xattn_gamma_l", "L0_xattn_beta_l", "L0_xattn_Wq", "L0_xattn_Wkv", "L0_xattn_Wo", "L0_ffn_router_w",
        "L0_ffn_router_b", "L0_ffn_weights1", "L0_ffn_bias1", "L0_ffn_weights2", "L0_ffn_bias2", "L1_attn_Wq",
        "L1_attn_Wk", "L1_attn_Wvdown", "L1_attn_Wvup", "L1_xattn_Wq", "L1_xattn_bq", "L1_xattn_Wkv", "L1_xattn_bkv",
        "L1_xattn_Wo", "L1_xattn_bo", "L1_ffn_W_fc", "L1_ffn_ln_w", "L1_ffn_ln_b", "L1_ffn_W_proj"]


def kernel(**inputs):
    import concourse.bacc as bacc
    from concourse.bass_utils import run_bass_kernel_spmd

    nc = bacc.Bacc("TRN2", target_bir_lowering=False, num_devices=1)
    arrays = {n: np.ascontiguousarray(inputs[n]) for n in ["x", "ctx_1024"] + _INS}
    arrays["table"], arrays["table16"] = constants()
    io = {n: nc.dram_tensor(f"in_{n}", a.shape, mybir.dt.from_np(a.dtype), kind="ExternalInput").ap()
          for n, a in arrays.items()}
    out = nc.dram_tensor("out_x", (B, S, D), F32, kind="ExternalOutput").ap()
    build(nc, io, out)
    r = run_bass_kernel_spmd(nc, [{f"in_{n}": a for n, a in arrays.items()}], core_ids=[0])
    return r.results[0]["out_x"]
```

```python
from contextlib import ExitStack

import numpy as np

import concourse.bass as bass
from concourse import mybir
from concourse.alu_op_type import AluOpType as ALU

F32 = mybir.dt.float32
BF16 = mybir.dt.bfloat16
ACT = mybir.ActivationFunctionType
AX = mybir.AxisListType.X

B, S, D, SC = 4, 512, 128, 154
P = 128
NT = S // P
STREAMS = 2
TURNS = B // STREAMS
CH = SC // 2
BANK = 512
EPS = 1e-5
INNER = 4
MASKED = -1e30
FMIN = float(np.finfo(np.float32).min)
W, HD, NL = 32, 8, 64
XH, XD = 8, 64
XU = XH * NT
NK = S + SC
E, EH = 32, 32
EC = E * EH // P
FH = 512
FC = FH // P

CONST = dict(ident=P, mask4=4, mask8=8, headblk=P, gvmask=4 * 64, iota=E, cos=SC, sin=SC, tri=2 * S - P,
             hmaskf=4 * P)
CONST16 = dict(winq=P, winmask=5 * P, latmask=NT * NL, sel=EC * P)


def constants():
    p = np.arange(P)[:, None]
    f = np.arange(P)[None, :]
    c = {}
    c["ident"] = p == f
    c["mask4"] = (p % 32) // HD == np.arange(4)[None, :]
    c["mask8"] = p // HD == np.arange(8)[None, :]
    c["headblk"] = p // HD == f // HD
    c["winq"] = p % W == f % W
    i, j = p % W, np.arange(2 * W)[None, :]
    band = (j > i) & (j <= i + W)
    usual = np.where(np.tile(band, (1, 2)), 0.0, MASKED)
    first = np.where(np.concatenate([band & (j >= W), band], 1), 0.0, MASKED)
    c["winmask"] = np.concatenate([first] + [usual] * 4, 1)
    t, n = np.arange(NT)[None, :, None], np.arange(NL)[None, None, :]
    c["latmask"] = np.where(n <= (t * P + p[:, :, None]) // (S // NL), 0.0, MASKED)
    k, g = np.arange(4)[None, :, None], np.arange(64)[None, None, :]
    c["gvmask"] = g // HD == 2 * k + p[:, :, None] // NL
    c["iota"] = np.broadcast_to(np.arange(E)[None, :] - 2.0 * E, (P, E))
    inv = (1.0 / np.float32(10000.0) ** (np.arange(0, XD, 2, dtype=np.float32) / np.float32(XD))).astype(np.float32)
    theta = (np.arange(SC, dtype=np.float32)[:, None] * inv[None, :]).astype(np.float32)
    angle = np.concatenate([theta, theta] * 2, 1).T
    c["cos"], c["sin"] = np.cos(angle), np.sin(angle)
    j = np.arange(2 * S - P)[None, :]
    c["tri"] = j - (S - P) <= p
    h4 = np.arange(4)[None, :, None]
    c["hmaskf"] = np.broadcast_to((f[:, None, :] // HD) % 4 == h4, (P, 4, P))
    k = np.arange(EC)[None, :, None]
    c["sel"] = np.where(p[:, :, None] == 4 * k + f[:, None, :] // EH, -MASKED, 0.0)
    return [np.concatenate([np.asarray(c[n], np.float32).reshape(P, w) for n, w in names.items()], 1)
            for names in (CONST, CONST16)]


class Signal:

    def __init__(self, sem, per, step=1, before=0):
        self.sem, self.per, self.step, self.before = sem, per, step, before

    def at(self, turn, k):
        return turn * (self.per * self.step) + (self.before + k) * self.step


def build(nc, io, out):
    with ExitStack() as ctx:
        def sb(name, shape, dt=F32):
            return ctx.enter_context(nc.sbuf_tensor(name, shape, dt))

        def sem(name):
            return ctx.enter_context(nc.semaphore(name))

        def signal(name, per, step=1):
            return [Signal(sem(f"{name}{s}"), per, step) for s in range(STREAMS)]

        def signals(name, *pers):
            sems = [sem(f"{name}{s}") for s in range(STREAMS)]
            return [[Signal(q, sum(pers), 1, sum(pers[:k])) for q in sems] for k in range(len(pers))]

        ncon = sum(CONST.values())
        table = sb("table", [P, ncon])
        con, at = {}, 0
        for name, w in CONST.items():
            con[name] = table[:, at:at + w]
            at += w
        ident = con["ident"]
        mask4 = con["mask4"]
        latmask = sb("latmask_b", [P, NT, NL], BF16)
        winmask = sb("winmask_b", [P, 5 * P], BF16)
        winq = sb("winq_b", [P, P], BF16)
        identb = sb("ident_b", [P, P], BF16)
        selb = sb("sel_b", [E, EC, P], BF16)
        ones = sb("ones", [P, P])
        halves, epsilon = sb("halves", [P, NT]), sb("epsilon", [P, NT])
        w_q, w_k, w_v, w_o = (sb(f"a_{n}", [P, P]) for n in ("wq", "wk", "wv", "wo"))
        w_gq, w_gk, w_gv = (sb(f"a_{n}", [P, 64]) for n in ("wgq", "wgk", "wgv"))
        w_rout = sb("a_rout", [64, P])
        vec_rows, vec = sb("vec_rows", [24, P]), sb("vec", [P, 24])
        gatew, lnp, e_bq, e_bk = vec[:, 0:2], vec[:, 2:6], vec[:, 6:7], vec[:, 7:8]
        b1, f_w, f_b = vec[:, 8:16], vec[:, 16:20], vec[:, 20:24]
        gate_l, gate_r = sb("a_gl", [P, P]), sb("a_gr", [P, P])
        xw_q, xw_kv = sb("b_wq", [P, 512]), sb("b_wkv", [P, 1024])
        xw_kr = sb("b_wkr", [P, 512])
        xw_o = sb("b_wo", [P, 4, P])
        rw = sb("c_rw", [P, E])
        rb = sb("c_rb", [P, E])
        w1 = sb("c_w1", [P, E, EH])
        w2 = sb("c_w2", [P, EC, P])
        b2 = sb("c_b2", [E, P])
        dw_q, dw_k = (sb(f"d_{n}", [P, 32]) for n in ("wq", "wk"))
        dw_vdT, dw_vu, dw_v = sb("d_wvdT", [32, P]), sb("d_wvu", [32, P]), sb("d_wv", [P, P])
        ew_q, ew_kv, ew_o = sb("e_wq", [P, P]), sb("e_wkv", [P, 2 * P]), sb("e_wo", [P, P])
        e_bv, e_bo = sb("e_bv", [P, P]), sb("e_bo", [1, P])
        wfcT, wpT = sb("f_wfcT", [P, FH]), sb("f_wpT", [P, FC, P])
        gam = sb("f_gam", [P, 8])

        x_tm = [sb(f"x_tm{s}", [P, NT, D]) for s in range(STREAMS)]
        xT = [sb(f"xT{s}", [P, W + S]) for s in range(STREAMS)]
        y = [sb(f"y{s}", [P, NT, D]) for s in range(STREAMS)]
        c_tm = [sb(f"c_tm{s}", [CH, 2, D]) for s in range(STREAMS)]
        cn = [sb(f"cn{s}", [CH, 2, D]) for s in range(STREAMS)]
        cT = [sb(f"cT{s}", [P, SC]) for s in range(STREAMS)]
        cnT = [sb(f"cnT{s}", [P, SC]) for s in range(STREAMS)]
        bn = [sb(f"bn{s}", [P, NT, 6]) for s in range(STREAMS)]
        mv = [sb(f"mv{s}", [P, NT, 2]) for s in range(STREAMS)]
        veps = [sb(f"veps{s}", [P, NT]) for s in range(STREAMS)]
        rstd = [sb(f"rstd{s}", [P, NT]) for s in range(STREAMS)]
        mx, nb, sums, rsum = ([sb(f"{n}{s}", [P, 64]) for s in range(STREAMS)] for n in ("mx", "nb", "sums", "rsum"))
        spacer = sb("spacer", [P, 1])
        spread = [sb(f"spread{s}", [P, P]) for s in range(STREAMS)]
        arena_w = [sb(f"arena_w{s}", [P, 6144]) for s in range(STREAMS)]
        arena_q = [sb(f"arena_q{s}", [P, 11164]) for s in range(STREAMS)]

        def view(arena, at, *shape):
            n = int(np.prod(shape))
            v = arena[:, at:at + n]
            if len(shape) == 2:
                v = v.rearrange("p (a b) -> p a b", b=shape[1])
            if len(shape) == 3:
                v = v.rearrange("p (a b c) -> p a b c", b=shape[1], c=shape[2])
            return v

        Qm = [view(a, 0, S // W, 4, W) for a in arena_q]
        QT = [view(a, 2048, S) for a in arena_q]
        GQ = [view(a, 2560, S) for a in arena_q]
        GKm = [view(a, 3072, 8, NL) for a in arena_q]
        GVm = [view(a, 3584, 4, 64) for a in arena_q]
        Vw = [view(a, 3840, 8, P) for a in arena_q]
        tl = [view(a, 4864, S) for a in arena_q]
        tr = [view(a, 5376, S) for a in arena_q]
        loc = [view(a, 5888, S) for a in arena_q]
        pooled = [view(a, 6400, 2, NL) for a in arena_q]
        remT = [view(a, 6528, S) for a in arena_q]
        mixT = [view(a, 7040, S) for a in arena_q]
        picked = [view(a, 7552, 8, 4, W) for a in arena_q]
        KP = [view(a, 8576, W + S) for a in arena_q]
        sc = [view(a, 0, 32, 64) for a in arena_w]
        PT = [view(a, 2048, 4, S) for a in arena_w]
        xq = [view(a, 0, 4, S) for a in arena_q]
        xk = [view(a, 2048, 4, NK) for a in arena_q]
        xv = [view(a, 4712, 6, 512) for a in arena_q]
        xp = [view(a, 7784, 2, NK) for a in arena_q]
        xo = [view(a, 9116, 4, S) for a in arena_q]
        xPT = [view(a, 0, 4, 6, P) for a in arena_w]
        rot = [view(a, 0, 4, SC) for a in arena_w]
        xr = [v[:].rearrange("p a b -> p (a b)")[:, 0:P] for v in y]
        lg = [view(a, 0, NT, E) for a in arena_q]
        eq = [view(a, 128, NT, E) for a in arena_q]
        pick = [view(a, 256, NT, E) for a in arena_q]
        oh = [view(a, 384, NT, E) for a in arena_q]
        ohT = [view(a, 512, S) for a in arena_q]
        ohm = [a[:, 1024:1024 + S // 2].bitcast(BF16) for a in arena_q]
        hid = [view(a, 1280, EC, S) for a in arena_q]
        dq = [view(a, 0, S) for a in arena_q]
        dk = [view(a, 512, S) for a in arena_q]
        dv = [view(a, 1024, NT, P) for a in arena_q]
        dz = [view(a, 1536, NT, S) for a in arena_q]
        de = [view(a, 3584, NT, S) for a in arena_q]
        eqT = [view(a, 5632, S) for a in arena_q]
        ekb = [view(a, 6144, SC) for a in arena_q]
        ekm = [view(a, 6298, 4, SC) for a in arena_q]
        evb = [view(a, 6914, 2, P) for a in arena_q]
        evm = [view(a, 7170, 2, 4, P) for a in arena_q]
        esc = [view(a, 8194, 2, 4 * SC) for a in arena_q]
        eo = [view(a, 9426, S) for a in arena_q]
        er = [view(a, 9938, P) for a in arena_q]
        ePT = [view(a, 0, 4, 8, P) for a in arena_w]
        fg = [view(a, 0, NT, FH) for a in arena_q]
        fhT = [view(a, 2048, FC, S) for a in arena_q]

        table16 = arena_w[0][:, 0:sum(CONST16.values())]
        con16, at = {}, 0
        for name, w in CONST16.items():
            con16[name] = table16[:, at:at + w]
            at += w
        wf_raw, wp_raw, wf_t, wp_t = (view(arena_w[1], 512 * k, FC, P) for k in range(4))
        below = view(arena_w[1], 2048, 2, FC, P)
        absd = view(arena_w[1], 3072, 2, FC, P)
        rw_rows = arena_w[1][0:E, 4096:4096 + P]
        dw_vd = arena_w[1][:, 4224:4256]

        PS = [ctx.enter_context(nc.psum_tensor(f"PS{s}", [P, 4 * BANK], F32)) for s in range(STREAMS)]

        def bank(s, i, n=1):
            return PS[s][:, i * BANK:(i + n) * BANK]

        s_table = sem("tables_loaded")
        s_vec = sem("vectors_loaded")
        s_wA, s_wB, s_wC, s_wD, s_wE, s_wF = (sem(f"weights_{n}") for n in "ABCDEF")
        s_pool0 = sem("constants_set")
        s_casts = sem("constants_cast")
        s_absum = sem("abs_summed")
        s_setup_pe = sem("setup_products")
        s_setup_act = sem("setup_copies")
        s_setup_vec = sem("setup_vector")

        gate = signal("turn_open", 1)
        x_in = signal("x_in", 1, 16)
        c_in = signal("c_in", 1, 16)
        stored = signal("stored", 1, 16)
        vown = signal("vector_own", 112)
        var_ready = signal("var_ready", 9)
        rstd_ready = signal("rstd_ready", 9)
        normed = signal("normed", 9)
        turned = signal("turned", 8)
        xT_ready = signal("xT_ready", 8)
        branch = signal("branch_done", 6)
        a_qk, a_lat, a_vw, a_z, a_ro = signals("a_products", 2, 2, 1, 1, 1)
        a_sp, a_vwc, a_tanh, a_rem = signals("a_copied", 3, 1, 1, 1)
        a_pool, a_qm, a_gkv, a_loc, a_mix = signals("a_vector", 1, 1, 2, 2, 1)
        r_sc, r_turn, r_pv = (signal(f"round_{n}", 3) for n in ("scores", "turned", "values"))
        r_exp, r_ea = (signal(f"round_{n}", 3) for n in ("exp", "copied_s"))
        r_sub, r_rs, r_ev = (signal(f"round_{n}", 3) for n in ("subtracted", "rsum", "copied_v"))
        r_p = signal("round_probs", 3)
        x_ck, x_pr = signals("x_products", 3, 3)
        x_ckv, x_cv = signals("x_copied_v", 2, 3)
        x_cva, x_ca = signals("x_copied_s", 1, 3)
        x_sc = signal("x_scores", XU + 1)
        x_nb, x_exp = signal("x_bias", XU), signal("x_exp", XU)
        x_ta, x_tb = signal("x_turned_a", XU), signal("x_turned_b", XU)
        x_ea, x_eb = signal("x_evac_a", XU), signal("x_evac_b", XU)
        x_pv, x_rs = signal("x_values", XU // 2), signal("x_spread", XU // 2)
        x_rc, x_no = signal("x_rsum_copied", XU // 2), signal("x_normalised", XU // 2)
        c_lg, c_ot, c_h = signals("c_products", 1, 1, EC)
        c_oa, c_ha = signals("c_scalar", 1, EC // 2)
        c_oh, c_ov, c_hv = signals("c_vector", 1, 1, EC // 2)
        d_qkv, d_sc, d_tu = signals("d_products", 1, 1, 1)
        d_ca, d_exp, d_ea = signals("d_scalar", 1, 1, 1)
        d_cv, d_nb, d_ev = signals("d_vector", 1, 1, 1)
        e_qkv, e_sc = signals("e_scores", 1, 17)
        e_ca, e_exp = signals("e_exp", 1, 16)
        e_cv, e_sub = signals("e_subtracted", 1, 16)
        e_tu, e_c = signal("e_turned", 16), signal("e_evac", 16)
        e_rs, e_no = signal("e_rsum", NT), signal("e_normalised", NT)
        e_rc = signal("e_rsum_copied", NT)
        f_h, f_tu = signals("f_products", 1, 1)
        f_g, f_ea = signals("f_scalar", 1, 1)
        f_ev = signal("f_evac_v", 1)
        eps_done = signal("eps_added", 9)
        kp_zero = signal("window_zeroed", 1)

        block = ctx.enter_context(nc.Block())

        @block.sync
        def _(sp):
            def load(dst, name, s, ap=None):
                sp.dma_start(dst, io[name] if ap is None else ap).then_inc(s, 16)

            load(table[:], "table", s_table)
            load(table16, "table16", s_table)

            def stream_in(turn, s):
                sp.wait_ge(gate[s].sem, turn + 1)
                b = bass.ds(STREAMS * turn + s, 1)
                sp.dma_start(x_tm[s][:], io["x"][b].rearrange("o (t p) d -> (o p) t d", p=P)).then_inc(x_in[s].sem, 16)
                sp.dma_start(c_tm[s][:], io["ctx_1024"][b].rearrange("o (t p) d -> (o p) t d", p=CH)).then_inc(c_in[s].sem, 16)

            for n, dst in (("wq", w_q), ("wk", w_k), ("wv", w_v), ("wgq", w_gq), ("wgk", w_gk), ("wgv", w_gv),
                           ("r_out_w", w_rout), ("w_out", w_o)):
                load(dst[:], "L0_attn_" + n, s_wA)
            row = 0
            for n in ("L0_attn_gate_local_w", "L0_attn_gate_remote_w"):
                load(vec_rows[row:row + 1, :], None, s_vec, io[n].rearrange("(o h) d -> o (h d)", o=1))
                row += 1
            for n in ("L0_xattn_gamma_x", "L0_xattn_beta_x", "L0_xattn_gamma_l", "L0_xattn_beta_l", "L1_xattn_bq",
                      "L1_xattn_bkv", "L0_ffn_bias1", "L1_ffn_ln_w", "L1_ffn_ln_b"):
                v = io[n][0:P] if n == "L1_xattn_bkv" else io[n]
                v = v.rearrange("(c e) h -> c (e h)", c=EC) if n == "L0_ffn_bias1" else v.rearrange("(c p) -> c p", p=P)
                load(vec_rows[row:row + v.shape[0], :], None, s_vec, v)
                row += v.shape[0]
            assert row == 24
            load(xw_q[:], "L0_xattn_Wq", s_wB)
            load(xw_kv[:], "L0_xattn_Wkv", s_wB)
            load(xw_o[:], None, s_wB, io["L0_xattn_Wo"].rearrange("(c p) n -> p c n", p=P))
            load(rw_rows, "L0_ffn_router_w", s_wC)
            load(rb[:], None, s_wC, io["L0_ffn_router_b"].rearrange("(o e) -> o e", o=1).to_broadcast([P, E]))
            load(w1[:], None, s_wC, io["L0_ffn_weights1"].rearrange("e d h -> d e h"))
            load(w2[:], None, s_wC, io["L0_ffn_weights2"].rearrange("(c e) h d -> (e h) c d", c=EC))
            load(b2[:], "L0_ffn_bias2", s_wC)
            load(dw_q[:], "L1_attn_Wq", s_wD)
            load(dw_k[:], "L1_attn_Wk", s_wD)
            load(dw_vd, "L1_attn_Wvdown", s_wD)
            load(dw_vu[:], "L1_attn_Wvup", s_wD)
            load(ew_q[:], "L1_xattn_Wq", s_wE)
            load(ew_kv[:], "L1_xattn_Wkv", s_wE)
            load(ew_o[:], "L1_xattn_Wo", s_wE)
            load(e_bv[:], None, s_wE, io["L1_xattn_bkv"][P:2 * P].rearrange("(o d) -> o d", o=1).to_broadcast([P, P]))
            load(e_bo[:], None, s_wE, io["L1_xattn_bo"].rearrange("(o d) -> o d", o=1))
            load(wf_raw, None, s_wF, io["L1_ffn_W_fc"].rearrange("(c p) d -> p c d", p=P))
            load(wp_raw, None, s_wF, io["L1_ffn_W_proj"].rearrange("d (c h) -> d c h", h=P))
            with sp.Fori(0, TURNS) as turn:
                for s in range(STREAMS):
                    stream_in(turn, s)
                for s in range(STREAMS):
                    sp.wait_ge(normed[s].sem, normed[s].at(turn, 9))
                    b = bass.ds(STREAMS * turn + s, 1)
                    sp.dma_start(out[b].rearrange("o (t p) d -> (o p) t d", p=P), x_tm[s][:]).then_inc(stored[s].sem, 16)
            for s in range(STREAMS):
                sp.wait_ge(stored[s].sem, 16 * TURNS)

        @block.gpsimd
        def _(pool):
            pool.memset(ones[:], 1.0).then_inc(s_pool0, 1)
            pool.memset(halves[:], -0.5).then_inc(s_pool0, 1)
            pool.memset(epsilon[:], EPS).then_inc(s_pool0, 1)
            for s in range(STREAMS):
                pool.memset(xT[s][:, 0:W], 0.0).then_inc(s_pool0, 1)
            pool.wait_ge(s_pool0, 3 + STREAMS)
            with pool.Fori(0, TURNS) as turn:
                def wait(sig, k):
                    pool.wait_ge(sig.sem, sig.at(turn, k))

                def inv_std(k, s):
                    wait(var_ready[s], k)
                    pool.tensor_tensor(veps[s][:], mv[s][:, :, 1], epsilon[:], ALU.add).then_inc(eps_done[s].sem, 1)
                    wait(eps_done[s], k)
                    pool.tensor_tensor(rstd[s][:], veps[s][:], halves[:], ALU.pow).then_inc(rstd_ready[s].sem, 1)

                def probs(r, s):
                    wait(r_rs[s], r)
                    pool.tensor_tensor(sc[s], sc[s], rsum[s][:, 0:32].unsqueeze(2).to_broadcast([P, 32, 64]),
                                       ALU.mult).then_inc(r_p[s].sem, 1)

                for s in range(STREAMS):
                    inv_std(1, s)
                    pool.memset(KP[s][:, 0:W], 0.0).then_inc(kp_zero[s].sem, 1)
                for r in (1, 2, 3):
                    for s in range(STREAMS):
                        probs(r, s)
                for k in range(2, 10):
                    for s in range(STREAMS):
                        inv_std(k, s)

        @block.tensor
        def _(pe):
            pe.wait_ge(s_pool0, 3 + STREAMS)
            pe.wait_ge(s_absum, 2)
            pe.matmul(bank(0, 0)[:, 0:2], ones[:], gam[:, 0:2], start=True, stop=True).then_inc(s_setup_pe, 1)
            pe.wait_ge(s_table, 32)
            pe.wait_ge(s_vec, 16 * 11)
            pe.transpose(bank(1, 0)[:, 0:24], vec_rows[:], ident[0:24, 0:24]).then_inc(s_setup_pe, 1)
            pe.wait_ge(s_wC, 16 * 5)
            pe.wait_ge(s_wD, 16 * 4)
            pe.transpose(bank(0, 3)[:, 0:E], rw_rows, ident[0:E, 0:E])
            pe.transpose(bank(0, 3)[0:32, E:E + P], dw_vd, ident).then_inc(s_setup_pe, 1)
            pe.wait_ge(s_setup_vec, 12)
            for c in range(FC):
                pe.transpose(bank(0, 1)[:, c * P:(c + 1) * P], wf_t[:, c, :], ident)
            for c in range(FC):
                mm = pe.transpose(bank(0, 2)[:, c * P:(c + 1) * P], wp_t[:, c, :], ident)
            mm.then_inc(s_setup_pe, 1)
            pe.wait_ge(s_setup_act, 2)
            pe.matmul(bank(0, 0)[:, P:2 * P], dw_vdT[:], dw_vu[:], start=True, stop=True).then_inc(s_setup_pe, 1)
            pe.wait_ge(s_setup_act, 5)
            pe.wait_ge(s_casts, 5)
            for q, n in ((s_wA, 8), (s_wB, 3), (s_wE, 5)):
                pe.wait_ge(q, 16 * n)

            with pe.Fori(0, TURNS) as turn:
                def wait(sig, k):
                    pe.wait_ge(sig.sem, sig.at(turn, k))

                def mm(out_, lhsT, rhs, start=True, stop=True):
                    return pe.matmul(out_, lhsT, rhs, start=start, stop=stop, skip_group_check=True)

                def turn_in(s):
                    wait(x_in[s], 1)
                    for t in range(NT):
                        m = pe.transpose(bank(s, 2)[:, t * P:(t + 1) * P], x_tm[s][:, t, :], ident)
                    m.then_inc(turned[s].sem, 1)
                    wait(c_in[s], 1)
                    for t in range(2):
                        m = pe.transpose(bank(s, 3)[:, t * CH:(t + 1) * CH], c_tm[s][:, t, :], ident[0:CH, 0:CH])
                    m.then_inc(turned[s].sem, 1)

                def tokens(s, t):
                    return xT[s][:, W + t * P:W + (t + 1) * P]

                def turn_rows(k, ln, s):
                    wait(normed[s], ln)
                    wait(xT_ready[s], k - 1)
                    for t in range(NT):
                        src = y[s] if k == INNER else x_tm[s]
                        m = pe.transpose(bank(s, 2)[:, t * P:(t + 1) * P], src[:, t, :], ident)
                    m.then_inc(turned[s].sem, 1)

                def qk(s):
                    wait(xT_ready[s], 1)
                    for i, w in enumerate((w_q, w_k)):
                        mm(bank(s, i), w[:], xT[s][:, W:]).then_inc(a_qk[s].sem, 1)

                def latent_qkv(s):
                    wait(xT_ready[s], 2)
                    mm(bank(s, 3)[0:64, :], w_gq[:], xT[s][:, W:]).then_inc(a_lat[s].sem, 1)
                    wait(a_pool[s], 1)
                    mm(bank(s, 2)[0:64, 0:NL], w_gk[:], pooled[s][:, 0, :])
                    mm(bank(s, 2)[:, NL:NL + 64], pooled[s].rearrange("p a n -> p (a n)"),
                       w_gv[:]).then_inc(a_lat[s].sem, 1)

                def window_v(s):
                    wait(a_qm[s], 1)
                    wait(a_sp[s], 2)
                    for m in range(8):
                        for b in range(2):
                            a = 64 * m + W * b
                            v = mm(PS[s][64 * b:64 * b + 64, m * P:(m + 1) * P], xT[s][:, a:a + 64], w_v[:])
                    v.then_inc(a_vw[s].sem, 1)

                def gates(s):
                    wait(a_gkv[s], 2)
                    wait(a_sp[s], 3)
                    mm(bank(s, 2), gate_l[:], QT[s])
                    mm(bank(s, 3), gate_r[:], QT[s]).then_inc(a_z[s].sem, 1)

                def window_scores(r, s):
                    if r == 1:
                        wait(kp_zero[s], 1)
                        wait(a_tanh[s], 1)
                    else:
                        wait(a_loc[s], r - 1)
                    for g in range(4):
                        q = slice(32 * g, 32 * g + 32)
                        mm(bank(s, g), winq[q, :], winmask[q, (r - 1) * P:(r + 3) * P], stop=False)
                    for u in range(8):
                        n = 8 * (r - 1) + u
                        for g in range(4):
                            q = slice(32 * g, 32 * g + 32)
                            m = mm(bank(s, g)[:, u * 64:(u + 1) * 64], Qm[s][q, n].rearrange("p h q -> p (h q)"),
                                   KP[s][q, n * W:(n + 2) * W], start=False)
                    m.then_inc(r_sc[s].sem, 1)

                def latent_scores(s):
                    wait(a_loc[s], 2)
                    for t in range(NT):
                        mm(bank(s, t), identb[:], latmask[:, t, :].unsqueeze(1).to_broadcast([P, 8, NL]), stop=False)
                        m = mm(bank(s, t), GQ[s][0:64, t * P:(t + 1) * P],
                               GKm[s][0:64].rearrange("p h n -> p (h n)"), start=False)
                    m.then_inc(r_sc[s].sem, 1)

                def turn_probs(r, s):
                    wait(r_p[s], r)
                    flat = sc[s].rearrange("p a b -> p (a b)")
                    for i in range(4):
                        for j in range(4):
                            a = (i * 4 + j) * P if r < 3 else (j * 4 + i) * P
                            m = pe.transpose(bank(s, i)[:, j * P:(j + 1) * P], flat[:, a:a + P], ident)
                    m.then_inc(r_turn[s].sem, 1)

                def window_values(r, s):
                    wait(r_ev[s], r)
                    wait(r_ea[s], r)
                    mm(bank(s, 0)[0:32, 0:1], ident[:, 0:32], ident[:, 0:1])
                    for j in range(4):
                        for b in range(2):
                            k = slice(64 * b, 64 * b + 64)
                            for g in range(4):
                                m = mm(bank(s, b)[32 * g:32 * g + 32, j * P:(j + 1) * P],
                                       Vw[s][k, 4 * (r - 1) + j, 32 * g:32 * g + 32], PT[s][k, g, j * P:(j + 1) * P])
                    m.then_inc(r_pv[s].sem, 1)

                def latent_values(s):
                    wait(r_ev[s], 3)
                    wait(r_ea[s], 3)
                    for c in range(4):
                        m = mm(bank(s, 0)[0:64, :], GVm[s][:, c, :], PT[s][:, c, :], start=c == 0, stop=c == 3)
                    m.then_inc(r_pv[s].sem, 1)
                    wait(a_rem[s], 1)
                    mm(bank(s, 1), w_rout[:], remT[s][0:64, :]).then_inc(a_ro[s].sem, 1)

                def out_a(s):
                    wait(a_mix[s], 1)
                    for t in range(NT):
                        m = mm(bank(s, 3)[:, t * P:(t + 1) * P], mixT[s][:, t * P:(t + 1) * P], w_o[:])
                    m.then_inc(branch[s].sem, 1)

                def turn_ctx(s):
                    wait(normed[s], 1)
                    for t in range(2):
                        m = pe.transpose(bank(s, 0)[:, t * CH:(t + 1) * CH], cn[s][:, t, :], ident[0:CH, 0:CH])
                    m.then_inc(turned[s].sem, 1)

                def ctx_keys(s, rotated):
                    if rotated:
                        wait(x_ckv[s], 1)
                    else:
                        wait(xT_ready[s], 3)
                    w = xw_kr if rotated else xw_kv
                    for c in range(4):
                        m = mm(bank(s, c // 2)[:, (c % 2) * SC:(c % 2 + 1) * SC], w[:, c * P:(c + 1) * P], cnT[s][:])
                    m.then_inc(x_ck[s].sem, 1)

                def ctx_values(s):
                    wait(x_ckv[s], 2)
                    for t in range(2):
                        m = mm(bank(s, t)[0:CH, :], cnT[s][:, t * CH:(t + 1) * CH], xw_kv[:, 512:1024])
                    m.then_inc(x_ck[s].sem, 1)

                def x_products(k, s):
                    if k == 1:
                        wait(xT_ready[s], 4)
                        wait(x_cva[s], 1)
                    else:
                        wait(x_cv[s], k - 1)
                        wait(x_ca[s], k - 1)
                    for c in range(4):
                        if k == 1:
                            m = mm(bank(s, c), xw_q[:, c * P:(c + 1) * P], xT[s][:, W:])
                        elif k == 2:
                            m = mm(bank(s, c), xw_kv[:, c * P:(c + 1) * P], xT[s][:, W:])
                        else:
                            m = mm(bank(s, c), tokens(s, c), xw_kv[:, 512:1024])
                    m.then_inc(x_pr[s].sem, 1)

                def x_turn_a(u, s):
                    wait(x_exp[s], u + 1)
                    if u:
                        wait(x_eb[s], u)
                    for c in range(3):
                        m = pe.transpose(bank(s, 2)[:, c * P:(c + 1) * P], xp[s][:, u % 2, c * P:(c + 1) * P], ident)
                    m.then_inc(x_ta[s].sem, 1)

                def x_scores(u, s):
                    hp, t, h = u // 8, u // 2 % 4, u % 2
                    if u == 0:
                        wait(x_cv[s], 3)
                        wait(x_ca[s], 3)
                    elif u % 2 == 0 and u >= 4:
                        wait(x_rc[s], u // 2 - 1)
                    if u < XU:
                        r = slice(64 * h, 64 * h + 64)
                        q = xq[s][r, hp, t * P:(t + 1) * P]
                        mm(bank(s, 0), q, xk[s][r, hp, 0:S])
                        m = mm(bank(s, 1)[:, 0:SC], q, xk[s][r, hp, S:NK])
                    if u % 2 and u >= 3:
                        wait(x_rs[s], (u - 1) // 2)
                        m = mm(bank(s, 1)[:, 256:384], spread[s][:], ident)
                    m.then_inc(x_sc[s].sem, 1)

                def x_turn_b(u, s):
                    wait(x_ea[s], u + 1)
                    p = xp[s][:, u % 2, :]
                    pe.transpose(bank(s, 2)[:, 0:P], p[:, 3 * P:S], ident)
                    for c in range(2):
                        m = pe.transpose(bank(s, 2)[0:CH, (c + 1) * P:(c + 2) * P], p[:, S + c * CH:S + (c + 1) * CH], ident)
                    m.then_inc(x_tb[s].sem, 1)

                def x_values(j, s):
                    hp, t = j // 4, j % 4
                    wait(x_ea[s], 2 * j + 2)
                    wait(x_eb[s], 2 * j + 2)
                    if j:
                        wait(x_no[s], j)
                    for c in range(6):
                        k = P if c < 4 else CH
                        for h in range(2):
                            col = (2 * hp + h) * 64
                            m = mm(bank(s, 3)[64 * h:64 * h + 64, t * P:(t + 1) * P], xv[s][0:k, c, col:col + 64],
                                   xPT[s][0:k, (2 * j + h) % 4, c, :], start=c == 0, stop=c == 5)
                    m.then_inc(x_pv[s].sem, 1)

                def out_b(s):
                    wait(x_no[s], XU // 2)
                    for t in range(NT):
                        for c in range(4):
                            m = mm(bank(s, 3)[:, t * P:(t + 1) * P], xo[s][:, c, t * P:(t + 1) * P], xw_o[:, c, :],
                                   start=c == 0, stop=c == 3)
                    m.then_inc(branch[s].sem, 1)

                def logits(s):
                    wait(xT_ready[s], 5)
                    for t in range(NT):
                        m = mm(bank(s, 2)[:, t * E:(t + 1) * E], tokens(s, t), rw[:])
                    m.then_inc(c_lg[s].sem, 1)

                def turn_onehot(s):
                    wait(c_oh[s], 1)
                    for t in range(NT):
                        m = pe.transpose(bank(s, 2)[0:E, t * P:(t + 1) * P], oh[s][:, t, :], ident)
                    m.then_inc(c_ot[s].sem, 1)

                def hidden(c, s):
                    if c == 0:
                        wait(c_ov[s], 1)
                        wait(c_oa[s], 1)
                    if c >= 3:
                        wait((c_ha, c_hv)[(c - 3) % 2][s], (c - 3) // 2 + 1)
                    mm(bank(s, c % 3), selb[:, c, :], ohm[s][0:E, :], stop=False)
                    mm(bank(s, c % 3), w1[:, 4 * c:4 * c + 4, :].rearrange("p e h -> p (e h)"), xT[s][:, W:],
                       start=False).then_inc(c_h[s].sem, 1)

                def out_c(s):
                    wait(c_ha[s], 4)
                    wait(c_hv[s], 4)
                    for t in range(NT):
                        cols = slice(t * P, (t + 1) * P)
                        for c in range(EC):
                            mm(bank(s, 3)[:, cols], hid[s][:, c, cols], w2[:, c, :], start=c == 0, stop=False)
                        m = mm(bank(s, 3)[:, cols], ohT[s][0:E, cols], b2[:], start=False)
                    m.then_inc(branch[s].sem, 1)

                def d_products(s):
                    wait(xT_ready[s], 6)
                    mm(bank(s, 0)[0:32, :], dw_q[:], xT[s][:, W:])
                    mm(bank(s, 1)[0:32, :], dw_k[:], xT[s][:, W:])
                    for t in range(NT):
                        m = mm(bank(s, 3)[:, t * P:(t + 1) * P], tokens(s, t), dw_v[:])
                    m.then_inc(d_qkv[s].sem, 1)

                def d_scores(s):
                    wait(d_ca[s], 1)
                    wait(d_cv[s], 1)
                    for t in range(NT):
                        m = mm(bank(s, t), dq[s][0:32, t * P:(t + 1) * P], dk[s][0:32, :])
                    m.then_inc(d_sc[s].sem, 1)

                def d_turn(s):
                    wait(d_exp[s], 1)
                    for c in range(4):
                        for t in range(NT):
                            m = pe.transpose(bank(s, c)[:, t * P:(t + 1) * P], dz[s][:, t, c * P:(c + 1) * P], ident)
                    m.then_inc(d_tu[s].sem, 1)

                def out_d(s):
                    wait(d_ea[s], 1)
                    wait(d_ev[s], 1)
                    for t in range(NT):
                        for c in range(4):
                            m = mm(bank(s, 3)[:, t * P:(t + 1) * P], PT[s][:, c, t * P:(t + 1) * P], dv[s][:, c, :],
                                   start=c == 0, stop=c == 3)
                    m.then_inc(branch[s].sem, 1)

                def e_products(s):
                    wait(xT_ready[s], 7)
                    mm(bank(s, 0), ew_q[:], xT[s][:, W:])
                    mm(bank(s, 1)[:, 0:SC], ew_kv[:, 0:P], cT[s][:])
                    for t in range(2):
                        m = mm(bank(s, 2)[0:CH, t * P:(t + 1) * P], cT[s][:, t * CH:(t + 1) * CH], ew_kv[:, P:2 * P])
                    m.then_inc(e_qkv[s].sem, 1)

                def e_turn(u, s):
                    wait(e_exp[s], u + 1)
                    if u:
                        wait(e_c[s], u)
                    for j in range(8):
                        m = pe.transpose(bank(s, 2 + j // 4)[0:CH, (j % 4) * P:(j % 4 + 1) * P],
                                         esc[s][:, u % 2, j * CH:(j + 1) * CH], ident)
                    m.then_inc(e_tu[s].sem, 1)

                def e_scores(u, s):
                    t, g = u // 4, u % 4
                    if u == 0:
                        wait(e_ca[s], 1)
                        wait(e_cv[s], 1)
                    else:
                        wait(e_sub[s], min(u, 16))
                        if u % 4 == 2 and u > 4:
                            wait(e_no[s], u // 4)
                    if u < 16:
                        r = slice(32 * g, 32 * g + 32)
                        for k in range(2):
                            m = mm(bank(s, k)[:, 0:2 * SC], eqT[s][r, t * P:(t + 1) * P],
                                   ekm[s][r, 2 * k:2 * k + 2, :].rearrange("p h n -> p (h n)"))
                    if u % 4 == 1 and u > 4:
                        m = e_values(u // 4 - 1, s)
                    m.then_inc(e_sc[s].sem, 1)

                def e_values(t, s):
                    wait(e_c[s], 4 * t + 4)
                    for j in range(8):
                        for g in range(4):
                            r = slice(32 * g, 32 * g + 32)
                            mm(bank(s, 1)[r, 384:512], evm[s][0:CH, j % 2, j // 2, r], ePT[s][0:CH, g, j, :],
                               start=j == 0, stop=j == 7)
                    wait(e_rs[s], t + 1)
                    return mm(bank(s, 0)[:, 384:512], spread[s][:], ident)

                def out_e(s):
                    wait(e_no[s], 4)
                    for t in range(NT):
                        cols = slice(t * P, (t + 1) * P)
                        mm(bank(s, 3)[:, cols], eo[s][:, cols], ew_o[:], stop=False)
                        m = mm(bank(s, 3)[:, cols], ones[0:1, :], e_bo[:], start=False)
                    m.then_inc(branch[s].sem, 1)

                def f_hidden(s):
                    wait(xT_ready[s], 8)
                    for t in range(NT):
                        m = mm(bank(s, t), tokens(s, t), wfcT[:])
                    m.then_inc(f_h[s].sem, 1)

                def f_turn(s):
                    wait(normed[s], 8)
                    for c in range(FC):
                        for t in range(NT):
                            m = pe.transpose(bank(s, c)[:, t * P:(t + 1) * P], fg[s][:, t, c * P:(c + 1) * P], ident)
                    m.then_inc(f_tu[s].sem, 1)

                def out_f(s):
                    wait(f_ea[s], 1)
                    wait(f_ev[s], 1)
                    for t in range(NT):
                        for c in range(FC):
                            m = mm(bank(s, 3)[:, t * P:(t + 1) * P], fhT[s][:, c, t * P:(t + 1) * P], wpT[:, c, :],
                                   start=c == 0, stop=c == 3)
                    m.then_inc(branch[s].sem, 1)

                both = range(STREAMS)
                for step in (turn_in, qk, latent_qkv, window_v, gates):
                    for s in both:
                        step(s)
                for r in (1, 2, 3):
                    for s in both:
                        window_scores(r, s) if r < 3 else latent_scores(s)
                    for s in both:
                        turn_probs(r, s)
                    for s in both:
                        window_values(r, s) if r < 3 else latent_values(s)
                for s in both:
                    out_a(s)
                for s in both:
                    turn_ctx(s)
                for s in both:
                    ctx_keys(s, False)
                for s in both:
                    ctx_keys(s, True)
                for s in both:
                    turn_rows(INNER, 3, s)
                for s in both:
                    ctx_values(s)
                for k in (1, 2, 3):
                    for s in both:
                        x_products(k, s)
                for u in range(XU + 2):
                    for s in both:
                        if 1 <= u <= XU:
                            x_turn_a(u - 1, s)
                        if u != XU:
                            x_scores(u, s)
                        if 1 <= u <= XU:
                            x_turn_b(u - 1, s)
                        if u >= 3 and u % 2:
                            x_values((u - 3) // 2, s)
                for s in both:
                    out_b(s)
                for s in both:
                    turn_rows(5, 4, s)
                for s in both:
                    logits(s)
                for s in both:
                    turn_onehot(s)
                for c in range(EC):
                    for s in both:
                        hidden(c, s)
                for s in both:
                    out_c(s)
                for s in both:
                    turn_rows(6, 5, s)
                for step in (d_products, d_scores, d_turn, out_d):
                    for s in both:
                        step(s)
                for s in both:
                    turn_rows(7, 6, s)
                for s in both:
                    e_products(s)
                for u in range(18):
                    for s in both:
                        if 1 <= u <= 16:
                            e_turn(u - 1, s)
                        if u != 16:
                            e_scores(u, s)
                for s in both:
                    out_e(s)
                for s in both:
                    turn_rows(8, 7, s)
                for step in (f_hidden, f_turn, out_f):
                    for s in both:
                        step(s)

        @block.scalar
        def _(act):
            def copy(dst, src):
                return act.activation(dst, src, ACT.Copy)

            act.wait_ge(s_wF, 16 * 2)
            for k, w in enumerate((wf_raw, wp_raw)):
                act.activation(absd[:, k], w, ACT.Abs, accum_out=gam[:, k:k + 1]).then_inc(s_absum, 1)
            act.wait_ge(s_setup_pe, 3)
            copy(rw[:], bank(0, 3)[:, 0:E]).then_inc(s_setup_act, 1)
            copy(dw_vdT[:], bank(0, 3)[0:32, E:E + P]).then_inc(s_setup_act, 1)
            act.wait_ge(s_setup_pe, 4)
            copy(wfcT[:], bank(0, 1)).then_inc(s_setup_act, 1)
            copy(wpT[:].rearrange("p c d -> p (c d)"), bank(0, 2)).then_inc(s_setup_act, 1)
            act.wait_ge(s_setup_pe, 5)
            copy(dw_v[:], bank(0, 0)[:, P:2 * P]).then_inc(s_setup_act, 1)
            act.wait_ge(s_setup_vec, 1)

            with act.Fori(0, TURNS) as turn:
                def wait(sig, k):
                    act.wait_ge(sig.sem, sig.at(turn, k))

                def affine(dst, src, scale, bias):
                    return act.activation(dst, src, ACT.Identity, scale=scale, bias=bias)

                def rows_to_T(k, s):
                    wait(turned[s], k)
                    if k == 2:
                        m = copy(cT[s][:], bank(s, 3)[:, 0:SC])
                    elif k == 3:
                        m = affine(cnT[s][:], bank(s, 0)[:, 0:SC], lnp[:, 0:1], lnp[:, 1:2])
                    elif k == INNER:
                        m = affine(xT[s][:, W:], bank(s, 2), lnp[:, 2:3], lnp[:, 3:4])
                    else:
                        m = copy(xT[s][:, W:], bank(s, 2))
                    m.then_inc(xT_ready[s].sem, 1)

                def copy_qk(s):
                    wait(a_qk[s], 2)
                    copy(KP[s][:, W:], bank(s, 1)).then_inc(a_sp[s].sem, 1)
                    wait(a_qm[s], 1)
                    copy(QT[s], bank(s, 0)).then_inc(a_sp[s].sem, 1)

                def copy_gq(s):
                    wait(a_lat[s], 1)
                    copy(GQ[s][0:64, :], bank(s, 3)[0:64, :]).then_inc(a_sp[s].sem, 1)

                def copy_window_v(s):
                    wait(a_vw[s], 1)
                    copy(Vw[s].rearrange("p a b -> p (a b)"), bank(s, 0, 2)).then_inc(a_vwc[s].sem, 1)

                def tanh_gates(s):
                    wait(a_z[s], 1)
                    act.activation(tl[s], bank(s, 2), ACT.Tanh, scale=0.5)
                    act.activation(tr[s], bank(s, 3), ACT.Tanh, scale=0.5).then_inc(a_tanh[s].sem, 1)

                def exp_round(r, s):
                    wait(r_sub[s], r)
                    act.activation(sc[s], sc[s], ACT.Exp, scale=HD ** -0.5).then_inc(r_exp[s].sem, 1)

                def copy_round(r, s):
                    wait(r_turn[s], r)
                    copy(PT[s][:, 2:4, :].rearrange("p a b -> p (a b)"), bank(s, 2, 2)).then_inc(r_ea[s].sem, 1)

                def copy_remote(s):
                    wait(r_pv[s], 3)
                    copy(remT[s][0:64, :], bank(s, 0)[0:64, :]).then_inc(a_rem[s].sem, 1)

                def copy_ctx_values(s):
                    wait(x_ck[s], 3)
                    copy(xv[s][0:CH, 4:6, :].rearrange("p a b -> p (a b)"),
                         bank(s, 0, 2)[0:CH, :]).then_inc(x_cva[s].sem, 1)

                def copy_x(k, s):
                    wait(x_pr[s], k)
                    dst = (xq[s][:, 2:4, :], xk[s][:, 2:4, 0:S], xv[s][:, 2:4, :])[k - 1]
                    copy(dst, bank(s, 2, 2).rearrange("p (a b) -> p a b", a=2)).then_inc(x_ca[s].sem, 1)

                def x_exp_unit(u, s):
                    wait(x_nb[s], u + 1)
                    if u >= 2:
                        wait(x_tb[s], u - 1)
                    act.activation(xp[s][:, u % 2, :], PS[s][:, 0:NK], ACT.Exp, scale=XD ** -0.5, bias=nb[s][:, u:u + 1],
                                   accum_out=sums[s][:, u:u + 1]).then_inc(x_exp[s].sem, 1)

                def x_copy_b(u, s):
                    wait(x_tb[s], u + 1)
                    if u >= 4:
                        wait(x_pv[s], (u - 4) // 2 + 1)
                    copy(xPT[s][:, u % 4, 3:6, :].rearrange("p c q -> p (c q)"),
                         bank(s, 2)[:, 0:3 * P]).then_inc(x_eb[s].sem, 1)

                def x_copy_rsum(j, s):
                    if j == XU // 2 - 1:
                        wait(x_sc[s], XU + 1)
                    if j:
                        wait(x_no[s], j)
                    copy(xr[s], bank(s, 1)[:, 256:384]).then_inc(x_rc[s].sem, 1)

                def copy_onehot(s):
                    wait(c_ot[s], 1)
                    copy(ohT[s][0:E, :], bank(s, 2)[0:E, :]).then_inc(c_oa[s].sem, 1)

                def relu(c, s):
                    wait(c_h[s], c + 1)
                    act.activation(hid[s][:, c, :], bank(s, c % 3), ACT.Relu, bias=b1[:, c:c + 1]).then_inc(c_ha[s].sem, 1)

                def copy_dqk(s):
                    wait(d_qkv[s], 1)
                    copy(dq[s][0:32, :], bank(s, 0)[0:32, :])
                    copy(dk[s][0:32, :], bank(s, 1)[0:32, :]).then_inc(d_ca[s].sem, 1)

                def d_exp_rows(s):
                    wait(d_nb[s], 1)
                    for t in range(NT):
                        m = act.activation(dz[s][:, t, :], dz[s][:, t, :], ACT.Exp, bias=nb[s][:, t:t + 1],
                                           accum_out=sums[s][:, t:t + 1])
                    m.then_inc(d_exp[s].sem, 1)

                def copy_d(s):
                    wait(d_tu[s], 1)
                    copy(PT[s][:, 2:4, :].rearrange("p a b -> p (a b)"), bank(s, 2, 2)).then_inc(d_ea[s].sem, 1)

                def copy_eq(s):
                    wait(e_qkv[s], 1)
                    act.activation(eqT[s], bank(s, 0), ACT.Identity, bias=e_bq).then_inc(e_ca[s].sem, 1)

                def e_exp_unit(u, s):
                    wait(e_sub[s], u + 1)
                    act.activation(esc[s][:, u % 2, :], esc[s][:, u % 2, :], ACT.Exp,
                                   scale=HD ** -0.5).then_inc(e_exp[s].sem, 1)

                def e_copy_probs(u, s):
                    wait(e_tu[s], u + 1)
                    if u % 4 == 0 and u:
                        wait(e_sc[s], u + 2)
                    copy(ePT[s][0:CH, u % 4].rearrange("p a b -> p (a b)"), bank(s, 2, 2)[0:CH, :]).then_inc(e_c[s].sem, 1)

                def e_copy_rsum(t, s):
                    if t < NT - 1:
                        wait(e_sub[s], 4 * t + 6)
                    else:
                        wait(e_sc[s], 17)
                    copy(er[s], bank(s, 0)[:, 384:512]).then_inc(e_rc[s].sem, 1)

                def gelu(s):
                    wait(f_h[s], 1)
                    act.activation(fg[s].rearrange("p a b -> p (a b)"), PS[s][:], ACT.Gelu).then_inc(f_g[s].sem, 1)

                def copy_f(s):
                    wait(f_tu[s], 1)
                    for c in (2, 3):
                        m = affine(fhT[s][:, c, :], bank(s, c), f_w[:, c:c + 1], f_b[:, c:c + 1])
                    m.then_inc(f_ea[s].sem, 1)

                both = range(STREAMS)
                for s in both:
                    rows_to_T(1, s)
                    rows_to_T(2, s)
                for step in (copy_qk, copy_gq, copy_window_v, tanh_gates):
                    for s in both:
                        step(s)
                for r in (1, 2, 3):
                    for s in both:
                        exp_round(r, s)
                    for s in both:
                        copy_round(r, s)
                for s in both:
                    copy_remote(s)
                for s in both:
                    rows_to_T(3, s)
                for s in both:
                    rows_to_T(INNER, s)
                for s in both:
                    copy_ctx_values(s)
                for k in (1, 2, 3):
                    for s in both:
                        copy_x(k, s)
                for u in range(XU + 2):
                    for s in both:
                        if 1 <= u <= XU:
                            x_copy_b(u - 1, s)
                        if u < XU:
                            x_exp_unit(u, s)
                        if u >= 3 and u % 2:
                            x_copy_rsum((u - 3) // 2, s)
                for s in both:
                    rows_to_T(5, s)
                for s in both:
                    copy_onehot(s)
                for c in range(0, EC, 2):
                    for s in both:
                        relu(c, s)
                for s in both:
                    rows_to_T(6, s)
                for step in (copy_dqk, d_exp_rows, copy_d):
                    for s in both:
                        step(s)
                for s in both:
                    rows_to_T(7, s)
                for s in both:
                    copy_eq(s)
                for u in range(18):
                    for s in both:
                        if u < 16:
                            e_exp_unit(u, s)
                        if u % 4 == 1 and u > 4:
                            e_copy_rsum(u // 4 - 1, s)
                        if 1 <= u <= 16:
                            e_copy_probs(u - 1, s)
                for s in both:
                    rows_to_T(8, s)
                for step in (gelu, copy_f):
                    for s in both:
                        step(s)

        @block.vector
        def _(dve):
            dve.wait_ge(s_table, 32)
            for dst, src in ((latmask[:].rearrange("p a b -> p (a b)"), con16["latmask"]), (winmask[:], con16["winmask"]),
                             (winq[:], con16["winq"]), (identb[:], ident),
                             (selb[:].rearrange("p a b -> p (a b)"), con16["sel"][0:E])):
                dve.tensor_copy(dst, src).then_inc(s_casts, 1)
            dve.wait_ge(s_setup_pe, 2)
            dve.tensor_copy(vec[:], bank(1, 0)[:, 0:24]).then_inc(s_setup_vec, 1)
            dve.wait_ge(s_setup_vec, 1)
            dve.tensor_scalar(gate_l[:], con["headblk"], gatew[:, 0:1], None, ALU.mult).then_inc(s_setup_vec, 1)
            dve.tensor_scalar(gate_r[:], con["headblk"], gatew[:, 1:2], None, ALU.mult).then_inc(s_setup_vec, 1)
            dve.wait_ge(s_wB, 16 * 3)
            wk, wr = (w.rearrange("p (h d) -> p h d", d=XD) for w in (xw_kv[:, 0:512], xw_kr[:]))
            dve.tensor_scalar(wr[:, :, 0:32], wk[:, :, 32:64], -1.0, None, ALU.mult).then_inc(s_setup_vec, 1)
            dve.tensor_copy(wr[:, :, 32:64], wk[:, :, 0:32]).then_inc(s_setup_vec, 1)
            dve.wait_ge(s_setup_pe, 1)
            dve.tensor_scalar(gam[:, 2:4], bank(0, 0)[:, 0:2], 1.0 / (FH * D), 1e-6, ALU.mult, ALU.add).then_inc(s_setup_vec, 1)
            dve.wait_ge(s_setup_vec, 6)
            dve.tensor_scalar(gam[:, 4:6], gam[:, 2:4], 0.5, None, ALU.mult).then_inc(s_setup_vec, 1)
            dve.tensor_scalar(gam[:, 6:8], gam[:, 2:4], -0.5, None, ALU.mult).then_inc(s_setup_vec, 1)
            dve.wait_ge(s_setup_vec, 8)
            dve.wait_ge(s_wF, 16 * 2)
            for k, w in enumerate((wf_raw, wp_raw)):
                dve.tensor_scalar(below[:, k], w, gam[:, 6 + k:7 + k], None, ALU.is_lt).then_inc(s_setup_vec, 1)
            dve.wait_ge(s_setup_vec, 10)
            for k, (w, t) in enumerate(((wf_raw, wf_t), (wp_raw, wp_t))):
                dve.scalar_tensor_tensor(out=t, in0=w, scalar=gam[:, 4 + k:5 + k], in1=below[:, k], op0=ALU.is_gt,
                                         op1=ALU.subtract).then_inc(s_setup_vec, 1)
            for s in range(STREAMS):
                dve.memset(mv[s][:], 1.0).then_inc(gate[s].sem, 1)
            for q, n in ((s_wC, 5), (s_wE, 5)):
                dve.wait_ge(q, 16 * n)

            with dve.Fori(0, TURNS) as turn:
                steps_own = [0] * STREAMS

                def wait(sig, k):
                    dve.wait_ge(sig.sem, sig.at(turn, k))

                def own(s, ins):
                    steps_own[s] += 1
                    ins.then_inc(vown[s].sem, 1)
                    wait(vown[s], steps_own[s])

                def stats(k, s, src, n, rows=P):
                    for t in range(n):
                        m = dve.bn_stats(bn[s][0:rows, t, :], src[:, t, :])
                    own(s, m)
                    dve.memset(spacer[:], 0.0)
                    for t in range(n):
                        m = dve.bn_aggr(mv[s][0:rows, t, :], bn[s][0:rows, t, :])
                    m.then_inc(var_ready[s].sem, 1)

                def normalise(k, s, dst, src, n, rows=P):
                    wait(rstd_ready[s], k)
                    for t in range(n):
                        m = dve.tensor_scalar(dst[:, t, :], src[:, t, :], mv[s][0:rows, t, 0:1], rstd[s][0:rows, t:t + 1],
                                              ALU.subtract, ALU.mult)
                    m.then_inc(normed[s].sem, 1)

                def residual(b, k, s, scalar, op):
                    wait(branch[s], b)
                    own(s, dve.scalar_tensor_tensor(out=y[s][:].rearrange("p a b -> p (a b)"), in0=bank(s, 3),
                                                    scalar=scalar, in1=x_tm[s][:].rearrange("p a b -> p (a b)"),
                                                    op0=op, op1=ALU.add))
                    stats(k, s, y[s], NT)

                def ctx_stats(s):
                    wait(c_in[s], 1)
                    stats(1, s, c_tm[s], 2, CH)

                def pool_latents(s):
                    wait(xT_ready[s], 1)
                    own(s, dve.tensor_reduce(pooled[s][:, 0, :], xT[s][:, W:].rearrange("p (n k) -> p n k", k=S // NL), AX, ALU.add))
                    own(s, dve.tensor_scalar(pooled[s][:, 1, :], pooled[s][:, 0, :], NL / S, None, ALU.mult))
                    dve.tensor_copy(pooled[s][:, 0, :], pooled[s][:, 1, :]).then_inc(a_pool[s].sem, 1)

                def mask_q(s):
                    wait(a_qk[s], 1)
                    shape = [P, S // W, 4, W]
                    dve.tensor_tensor(Qm[s], bank(s, 0).rearrange("p (n q) -> p n q", q=W).unsqueeze(2).to_broadcast(shape),
                                      mask4.unsqueeze(1).unsqueeze(3).to_broadcast(shape), ALU.mult).then_inc(a_qm[s].sem, 1)

                def mask_latents(s):
                    wait(a_lat[s], 2)
                    dve.tensor_tensor(GKm[s][0:64], bank(s, 2)[0:64, 0:NL].unsqueeze(1).to_broadcast([64, 8, NL]),
                                      con["mask8"][0:64].unsqueeze(2).to_broadcast([64, 8, NL]),
                                      ALU.mult).then_inc(a_gkv[s].sem, 1)
                    dve.tensor_tensor(GVm[s], bank(s, 2)[:, NL:NL + 64].unsqueeze(1).to_broadcast([P, 4, 64]),
                                      con["gvmask"].rearrange("p (c f) -> p c f", c=4), ALU.mult).then_inc(a_gkv[s].sem, 1)

                def subtract_max(r, s):
                    wait(r_sc[s], r)
                    scores = PS[s][:].rearrange("p (u n) -> p u n", n=64)
                    own(s, dve.tensor_reduce(mx[s][:, 0:32], scores, AX, ALU.max))
                    dve.tensor_tensor(sc[s], scores, mx[s][:, 0:32].unsqueeze(2).to_broadcast([P, 32, 64]),
                                      ALU.subtract).then_inc(r_sub[s].sem, 1)

                def row_sums(r, s):
                    wait(r_exp[s], r)
                    own(s, dve.tensor_reduce(sums[s][:, 0:32], sc[s], AX, ALU.add))
                    dve.reciprocal(rsum[s][:, 0:32], sums[s][:, 0:32]).then_inc(r_rs[s].sem, 1)

                def copy_round(r, s):
                    wait(r_turn[s], r)
                    dve.tensor_copy(PT[s][:, 0:2, :].rearrange("p a b -> p (a b)"), bank(s, 0, 2)).then_inc(r_ev[s].sem, 1)

                def pick_heads(r, s):
                    wait(r_pv[s], r)
                    own(s, dve.tensor_tensor(picked[s].rearrange("p u h q -> p u h q"),
                                             bank(s, 0, 2).rearrange("p (u h q) -> p u h q", h=4, q=W),
                                             mask4.unsqueeze(1).unsqueeze(3).to_broadcast([P, 8, 4, W]), ALU.mult))
                    half = loc[s][:, (r - 1) * 256:r * 256].rearrange("p (m b q) -> p m b q", m=4, b=2)
                    for b in range(2):
                        m = dve.tensor_reduce(half[:, :, b, :],
                                              picked[s][:, 4 * b:4 * b + 4].rearrange("p u h q -> p u q h"), AX, ALU.add)
                    m.then_inc(a_loc[s].sem, 1)

                def mix(s):
                    wait(a_tanh[s], 1)
                    wait(a_loc[s], 2)
                    own(s, dve.scalar_tensor_tensor(out=loc[s], in0=tl[s], scalar=1.0, in1=loc[s], op0=ALU.add, op1=ALU.mult))
                    wait(a_ro[s], 1)
                    own(s, dve.scalar_tensor_tensor(out=tr[s], in0=tr[s], scalar=1.0, in1=bank(s, 1), op0=ALU.add,
                                                    op1=ALU.mult))
                    dve.tensor_tensor(mixT[s], loc[s], tr[s], ALU.add).then_inc(a_mix[s].sem, 1)

                def ctx_keys(s):
                    pairs = PS[s][:, 0:2 * BANK].rearrange("p (b c) -> p b c", b=2)[:, :, 0:2 * SC]
                    pairs = pairs.rearrange("p b (k j) -> p b k j", k=2)
                    spread = [con[n].unsqueeze(1).unsqueeze(1).to_broadcast([P, 2, 2, SC]) for n in ("cos", "sin")]
                    keys = xk[s][:, :, S:NK]
                    wait(x_ck[s], 1)
                    dve.tensor_tensor(keys.rearrange("p (b k) j -> p b k j", b=2), pairs, spread[0],
                                      ALU.mult).then_inc(x_ckv[s].sem, 1)
                    wait(x_ck[s], 2)
                    own(s, dve.tensor_tensor(rot[s].rearrange("p (b k) j -> p b k j", b=2), pairs, spread[1], ALU.mult))
                    wait(x_ckv[s], 1)
                    dve.tensor_tensor(keys, keys, rot[s], ALU.add).then_inc(x_ckv[s].sem, 1)

                def copy_x(k, s):
                    wait(x_pr[s], k)
                    dst = (xq[s][:, 0:2, :], xk[s][:, 0:2, 0:S], xv[s][:, 0:2, :])[k - 1]
                    dve.tensor_copy(dst, bank(s, 0, 2).rearrange("p (a b) -> p a b", a=2)).then_inc(x_cv[s].sem, 1)

                def x_max(u, s):
                    wait(x_sc[s], u + 1)
                    own(s, dve.tensor_reduce(mx[s][:, u:u + 1], PS[s][:, 0:NK], AX, ALU.max))
                    dve.tensor_scalar(nb[s][:, u:u + 1], mx[s][:, u:u + 1], -(XD ** -0.5), None,
                                      ALU.mult).then_inc(x_nb[s].sem, 1)

                def x_copy_a(u, s):
                    wait(x_ta[s], u + 1)
                    if u >= 4:
                        wait(x_pv[s], (u - 4) // 2 + 1)
                    dve.tensor_copy(xPT[s][:, u % 4, 0:3, :].rearrange("p c q -> p (c q)"),
                                    bank(s, 2)[:, 0:3 * P]).then_inc(x_ea[s].sem, 1)

                def x_spread(j, s):
                    wait(x_exp[s], 2 * j + 2)
                    if j:
                        wait(x_sc[s], 2 * j + 2)
                    u = slice(2 * j, 2 * j + 2)
                    own(s, dve.reciprocal(rsum[s][:, u], sums[s][:, u]))
                    dve.tensor_copy(spread[s][:].rearrange("p (h d) -> p h d", h=2),
                                    rsum[s][:, u].unsqueeze(2).to_broadcast([P, 2, 64])).then_inc(x_rs[s].sem, 1)

                def x_normalise(j, s):
                    hp, t = j // 4, j % 4
                    wait(x_pv[s], j + 1)
                    wait(x_rc[s], j + 1)
                    dve.tensor_tensor(xo[s][:, hp, t * P:(t + 1) * P], bank(s, 3)[:, t * P:(t + 1) * P], xr[s],
                                      ALU.mult).then_inc(x_no[s].sem, 1)

                def choose(s):
                    wait(c_lg[s], 1)
                    iota = con["iota"].unsqueeze(1).to_broadcast([P, NT, E])
                    own(s, dve.tensor_tensor(lg[s], bank(s, 2)[:, 0:NT * E].rearrange("p (t e) -> p t e", t=NT),
                                             rb[:].unsqueeze(1).to_broadcast([P, NT, E]), ALU.add))
                    own(s, dve.tensor_reduce(mx[s][:, 0:NT], lg[s], AX, ALU.max))
                    own(s, dve.tensor_tensor(eq[s], lg[s], mx[s][:, 0:NT].unsqueeze(2).to_broadcast([P, NT, E]),
                                             ALU.is_equal))
                    own(s, dve.tensor_tensor(pick[s], eq[s], iota, ALU.mult))
                    own(s, dve.tensor_reduce(mx[s][:, NT:2 * NT], pick[s], AX, ALU.min))
                    dve.tensor_tensor(oh[s], iota, mx[s][:, NT:2 * NT].unsqueeze(2).to_broadcast([P, NT, E]),
                                      ALU.is_equal).then_inc(c_oh[s].sem, 1)

                def onehot_less_one(s):
                    wait(c_oa[s], 1)
                    dve.tensor_scalar(ohm[s][0:E, :], ohT[s][0:E, :], -1.0, None, ALU.add).then_inc(c_ov[s].sem, 1)

                def relu(c, s):
                    wait(c_h[s], c + 1)
                    dve.tensor_scalar(hid[s][:, c, :], bank(s, c % 3), b1[:, c:c + 1], 0.0, ALU.add,
                                      ALU.max).then_inc(c_hv[s].sem, 1)

                def copy_dv(s):
                    wait(d_qkv[s], 1)
                    dve.tensor_copy(dv[s].rearrange("p a b -> p (a b)"), bank(s, 3)).then_inc(d_cv[s].sem, 1)

                def d_mask(s):
                    wait(d_sc[s], 1)
                    for t in range(NT):
                        a = S - P - t * P
                        m = dve.scalar_tensor_tensor(out=dz[s][:, t, :], in0=bank(s, t), scalar=32 ** -0.5,
                                                     in1=con["tri"][:, a:a + S], op0=ALU.mult, op1=ALU.mult)
                    own(s, m)
                    own(s, dve.tensor_scalar(de[s], dz[s], 0.0, FMIN, ALU.is_equal, ALU.mult))
                    own(s, dve.tensor_tensor(dz[s], dz[s], de[s], ALU.add))
                    own(s, dve.tensor_reduce(mx[s][:, 0:NT], dz[s], AX, ALU.max))
                    dve.tensor_scalar(nb[s][:, 0:NT], mx[s][:, 0:NT], -1.0, None, ALU.mult).then_inc(d_nb[s].sem, 1)

                def copy_d(s):
                    wait(d_exp[s], 1)
                    own(s, dve.reciprocal(rsum[s][:, 0:NT], sums[s][:, 0:NT]))
                    wait(d_tu[s], 1)
                    dve.tensor_copy(PT[s][:, 0:2, :].rearrange("p a b -> p (a b)"), bank(s, 0, 2)).then_inc(d_ev[s].sem, 1)

                def residual_d(s):
                    wait(branch[s], 4)
                    for t in range(NT):
                        m = dve.scalar_tensor_tensor(out=y[s][:, t, :], in0=bank(s, 3)[:, t * P:(t + 1) * P],
                                                     scalar=rsum[s][:, t:t + 1], in1=x_tm[s][:, t, :], op0=ALU.mult,
                                                     op1=ALU.add)
                    own(s, m)
                    stats(6, s, y[s], NT)

                def mask_ctx(s):
                    wait(e_qkv[s], 1)
                    own(s, dve.tensor_scalar(ekb[s], bank(s, 1)[:, 0:SC], e_bk, None, ALU.add))
                    dve.tensor_tensor(ekm[s], ekb[s].unsqueeze(1).to_broadcast([P, 4, SC]),
                                      mask4.unsqueeze(2).to_broadcast([P, 4, SC]), ALU.mult)
                    own(s, dve.tensor_tensor(evb[s][0:CH], bank(s, 2)[0:CH, 0:2 * P].rearrange("p (c f) -> p c f", c=2),
                                             e_bv[0:CH].unsqueeze(1).to_broadcast([CH, 2, P]), ALU.add))
                    heads = con["hmaskf"][0:CH].rearrange("p (h f) -> p h f", h=4)
                    dve.tensor_tensor(evm[s][0:CH], evb[s][0:CH].unsqueeze(2).to_broadcast([CH, 2, 4, P]),
                                      heads.unsqueeze(1).to_broadcast([CH, 2, 4, P]), ALU.mult).then_inc(e_cv[s].sem, 1)

                def e_subtract_max(u, s):
                    wait(e_sc[s], u + 1)
                    if u >= 2:
                        wait(e_tu[s], u - 1)
                    scores = PS[s][:, 0:2 * BANK].rearrange("p (b c) -> p b c", b=2)[:, :, 0:2 * SC]
                    scores = scores.rearrange("p b (k j) -> p b k j", k=2)
                    top = mx[s][:, 4 * u:4 * u + 4].rearrange("p (b k) -> p b k", b=2)
                    own(s, dve.tensor_reduce(top, scores, AX, ALU.max))
                    dve.tensor_tensor(esc[s][:, u % 2, :].rearrange("p (b k j) -> p b k j", b=2, k=2), scores,
                                      top.unsqueeze(3).to_broadcast([P, 2, 2, SC]), ALU.subtract).then_inc(e_sub[s].sem, 1)

                def e_sums(u, s):
                    wait(e_exp[s], u + 1)
                    m = dve.tensor_reduce(sums[s][:, 4 * u:4 * u + 4],
                                          esc[s][:, u % 2, :].rearrange("p (h j) -> p h j", h=4), AX, ALU.add)
                    if u % 4 == 3:
                        own(s, m)
                        t = u // 4
                        heads = slice(16 * t, 16 * t + 16)
                        own(s, dve.reciprocal(rsum[s][:, heads], sums[s][:, heads]))
                        dve.tensor_copy(spread[s][:].rearrange("p (h d) -> p h d", h=16),
                                        rsum[s][:, heads].unsqueeze(2).to_broadcast([P, 16, HD])
                                        ).then_inc(e_rs[s].sem, 1)

                def e_normalise(t, s):
                    wait(e_rc[s], t + 1)
                    dve.tensor_tensor(eo[s][:, t * P:(t + 1) * P], bank(s, 1)[:, 384:512], er[s],
                                      ALU.mult).then_inc(e_no[s].sem, 1)

                def copy_f(s):
                    wait(f_tu[s], 1)
                    for c in (0, 1):
                        m = dve.tensor_scalar(fhT[s][:, c, :], bank(s, c), f_w[:, c:c + 1], f_b[:, c:c + 1],
                                              ALU.mult, ALU.add)
                    m.then_inc(f_ev[s].sem, 1)

                both = range(STREAMS)
                for s in both:
                    ctx_stats(s)
                for s in both:
                    pool_latents(s)
                for s in both:
                    mask_q(s)
                for s in both:
                    normalise(1, s, cn[s], c_tm[s], 2, CH)
                    mask_latents(s)
                for r in (1, 2, 3):
                    for s in both:
                        subtract_max(r, s)
                    for s in both:
                        row_sums(r, s)
                    for s in both:
                        copy_round(r, s)
                    if r < 3:
                        for s in both:
                            pick_heads(r, s)
                for s in both:
                    mix(s)
                for s in both:
                    residual(1, 2, s, 0.5, ALU.mult)
                for s in both:
                    normalise(2, s, x_tm[s], y[s], NT)
                for s in both:
                    wait(normed[s], 2)
                    stats(3, s, x_tm[s], NT)
                for s in both:
                    normalise(3, s, y[s], x_tm[s], NT)
                for s in both:
                    ctx_keys(s)
                for k in (1, 2, 3):
                    for s in both:
                        copy_x(k, s)
                for u in range(XU + 3):
                    for s in both:
                        if 1 <= u <= XU:
                            x_copy_a(u - 1, s)
                        if u >= 4 and u % 2 == 0:
                            x_normalise((u - 4) // 2, s)
                        if u < XU:
                            x_max(u, s)
                        if u >= 2 and u % 2 == 0 and u <= XU:
                            x_spread((u - 2) // 2, s)
                for s in both:
                    residual(2, 4, s, 1.0, ALU.mult)
                for s in both:
                    normalise(4, s, x_tm[s], y[s], NT)
                for s in both:
                    choose(s)
                for s in both:
                    onehot_less_one(s)
                for c in range(1, EC, 2):
                    for s in both:
                        relu(c, s)
                for s in both:
                    residual(3, 5, s, 0.0, ALU.max)
                for s in both:
                    normalise(5, s, x_tm[s], y[s], NT)
                for step in (copy_dv, d_mask, copy_d, residual_d):
                    for s in both:
                        step(s)
                for s in both:
                    normalise(6, s, x_tm[s], y[s], NT)
                for s in both:
                    mask_ctx(s)
                for u in range(18):
                    for s in both:
                        if u < 16:
                            e_subtract_max(u, s)
                        if 1 <= u <= 16:
                            e_sums(u - 1, s)
                        if u % 4 == 1 and u > 4:
                            e_normalise(u // 4 - 1, s)
                for s in both:
                    residual(5, 7, s, 1.0, ALU.mult)
                for s in both:
                    normalise(7, s, x_tm[s], y[s], NT)
                for s in both:
                    wait(f_g[s], 1)
                    stats(8, s, fg[s], NT)
                for s in both:
                    normalise(8, s, fg[s], fg[s], NT)
                for s in both:
                    copy_f(s)
                for s in both:
                    residual(6, 9, s, 1.0, ALU.mult)
                for s in both:
                    normalise(9, s, x_tm[s], y[s], NT)
                for s in both:
                    wait(stored[s], 1)
                    dve.memset(mv[s][:], 1.0).then_inc(gate[s].sem, 1)
                assert steps_own == [vown[0].per] * STREAMS, steps_own


_INS = ["L0_attn_wq", "L0_attn_wk", "L0_attn_wv", "L0_attn_wgq", "L0_attn_wgk", "L0_attn_wgv", "L0_attn_r_out_w",
        "L0_attn_gate_local_w", "L0_attn_gate_remote_w", "L0_attn_w_out", "L0_xattn_gamma_x", "L0_xattn_beta_x",
        "L0_xattn_gamma_l", "L0_xattn_beta_l", "L0_xattn_Wq", "L0_xattn_Wkv", "L0_xattn_Wo", "L0_ffn_router_w",
        "L0_ffn_router_b", "L0_ffn_weights1", "L0_ffn_bias1", "L0_ffn_weights2", "L0_ffn_bias2", "L1_attn_Wq",
        "L1_attn_Wk", "L1_attn_Wvdown", "L1_attn_Wvup", "L1_xattn_Wq", "L1_xattn_bq", "L1_xattn_Wkv", "L1_xattn_bkv",
        "L1_xattn_Wo", "L1_xattn_bo", "L1_ffn_W_fc", "L1_ffn_ln_w", "L1_ffn_ln_b", "L1_ffn_W_proj"]


def kernel(**inputs):
    import concourse.bacc as bacc
    from concourse.bass_utils import run_bass_kernel_spmd

    nc = bacc.Bacc("TRN2", target_bir_lowering=False, num_devices=1)
    arrays = {n: np.ascontiguousarray(inputs[n]) for n in ["x", "ctx_1024"] + _INS}
    arrays["table"], arrays["table16"] = constants()
    io = {n: nc.dram_tensor(f"in_{n}", a.shape, mybir.dt.from_np(a.dtype), kind="ExternalInput").ap()
          for n, a in arrays.items()}
    out = nc.dram_tensor("out_x", (B, S, D), F32, kind="ExternalOutput").ap()
    build(nc, io, out)
    r = run_bass_kernel_spmd(nc, [{f"in_{n}": a for n, a in arrays.items()}], core_ids=[0])
    return r.results[0]["out_x"]
```

```python
from contextlib import ExitStack

import numpy as np

import concourse.bass as bass
from concourse import mybir
from concourse.alu_op_type import AluOpType as ALU

F32 = mybir.dt.float32
BF16 = mybir.dt.bfloat16
ACT = mybir.ActivationFunctionType
AX = mybir.AxisListType.X

B, S, D, SC = 4, 512, 128, 154
P = 128
NT = S // P
STREAMS = 2
TURNS = B // STREAMS
CH = SC // 2
BANK = 512
EPS = 1e-5
INNER = 4
MASKED = -1e30
FMIN = float(np.finfo(np.float32).min)
W, HD, NL = 32, 8, 64
XH, XD = 8, 64
XU = XH * NT
NK = S + SC
E, EH = 32, 32
EC = E * EH // P
EU = NT * 4
EV = -(-4 * SC // P)
ELAST = 4 * SC - (EV - 1) * P
FH = 512
FC = FH // P

CONST = dict(ident=P, headsel=32, mask4=4, mask8=8, group=4, headblk=P, gvmask=4 * 64, iota=E, cos=SC, sin=SC, tri=P,
             vmask=EV * P)
CONST16 = dict(winq=P, winmask=2 * P, latmask=NT * NL)


def constants():
    p = np.arange(P)[:, None]
    f = np.arange(P)[None, :]
    c = {}
    c["ident"] = p == f
    c["mask4"] = (p % 32) // HD == np.arange(4)[None, :]
    c["mask8"] = p // HD == np.arange(8)[None, :]
    c["group"] = p // W == np.arange(4)[None, :]
    c["headblk"] = p // HD == f // HD
    c["headsel"] = p // W == np.arange(32)[None, :] // HD
    c["winq"] = p % W == f % W
    i, j = p % W, np.arange(2 * W)[None, :]
    band = (j > i) & (j <= i + W)
    usual = np.where(np.tile(band, (1, 2)), 0.0, MASKED)
    first = np.where(np.concatenate([band & (j >= W), band], 1), 0.0, MASKED)
    c["winmask"] = np.concatenate([first, usual], 1)
    t, n = np.arange(NT)[None, :, None], np.arange(NL)[None, None, :]
    c["latmask"] = np.where(n <= (t * P + p[:, :, None]) // (S // NL), 0.0, MASKED)
    k, g = np.arange(4)[None, :, None], np.arange(64)[None, None, :]
    c["gvmask"] = g // HD == 2 * k + p[:, :, None] // NL
    c["iota"] = np.broadcast_to(np.arange(E)[None, :] - 2.0 * E, (P, E))
    inv = (1.0 / np.float32(10000.0) ** (np.arange(0, XD, 2, dtype=np.float32) / np.float32(XD))).astype(np.float32)
    theta = (np.arange(SC, dtype=np.float32)[:, None] * inv[None, :]).astype(np.float32)
    angle = np.concatenate([theta, theta] * 2, 1).T
    c["cos"], c["sin"] = np.cos(angle), np.sin(angle)
    c["tri"] = f <= p
    k = np.arange(EV)[None, :, None]
    c["vmask"] = (f[:, None, :] // HD) % 4 == (k * P + p[:, :, None]) // SC
    k = np.arange(EC)[None, :, None]
    sel = np.where(p[:, :, None] == 4 * k + f[:, None, :] // EH, -MASKED, 0.0)
    return [np.concatenate([np.asarray(c[n], np.float32).reshape(P, w) for n, w in names.items()], 1)
            for names in (CONST, CONST16)] + [sel[0:E].reshape(E, EC * P).astype(np.float32)]


class Signal:

    def __init__(self, sem, per, step=1, before=0):
        self.sem, self.per, self.step, self.before = sem, per, step, before

    def at(self, turn, k):
        return turn * (self.per * self.step) + (self.before + k) * self.step


def build(nc, io, out):
    with ExitStack() as ctx:
        def sb(name, shape, dt=F32):
            return ctx.enter_context(nc.sbuf_tensor(name, shape, dt))

        def sem(name):
            return ctx.enter_context(nc.semaphore(name))

        def signal(name, per, step=1):
            return [Signal(sem(f"{name}{s}"), per, step) for s in range(STREAMS)]

        def signals(name, *pers):
            sems = [sem(f"{name}{s}") for s in range(STREAMS)]
            return [[Signal(q, sum(pers), 1, sum(pers[:k])) for q in sems] for k in range(len(pers))]

        ncon = sum(CONST.values())
        table = sb("table", [P, ncon])
        con, at = {}, 0
        for name, w in CONST.items():
            con[name] = table[:, at:at + w]
            at += w
        ident = con["ident"]
        mask4 = con["mask4"]
        latmask = sb("latmask_b", [P, NT, NL], BF16)
        winmask = sb("winmask_b", [P, 5 * P], BF16)
        tri = sb("tri", [P, 2 * S - P], BF16)
        winq = sb("winq_b", [P, P], BF16)
        identb = sb("ident_b", [P, P], BF16)
        selb = sb("sel_b", [E, EC, P], BF16)
        ones = sb("ones", [P, P])
        halves, epsilon = sb("halves", [P, NT]), sb("epsilon", [P, NT])
        w_q, w_k, w_v, w_o = (sb(f"a_{n}", [P, P]) for n in ("wq", "wk", "wv", "wo"))
        w_gq, w_gk, w_gv = (sb(f"a_{n}", [P, 64]) for n in ("wgq", "wgk", "wgv"))
        w_rout = sb("a_rout", [64, P])
        vec_rows, vec = sb("vec_rows", [24, P]), sb("vec", [P, 24])
        gatew, lnp, e_bq, e_bk = vec[:, 0:2], vec[:, 2:6], vec[:, 6:7], vec[:, 7:8]
        b1, f_w, f_b = vec[:, 8:16], vec[:, 16:20], vec[:, 20:24]
        gate_l, gate_r = sb("a_gl", [P, P]), sb("a_gr", [P, P])
        xw_q, xw_kv = sb("b_wq", [P, 512]), sb("b_wkv", [P, 1024])
        xw_kr = sb("b_wkr", [P, 512])
        xw_o = sb("b_wo", [P, 4, P])
        rw = sb("c_rw", [P, E])
        rb = sb("c_rb", [P, E])
        w1 = sb("c_w1", [P, E, EH])
        w2 = sb("c_w2", [P, EC, P])
        b2 = sb("c_b2", [E, P])
        dw_q, dw_k = (sb(f"d_{n}", [P, P]) for n in ("wq", "wk"))
        dw_vdT, dw_vu, dw_v = sb("d_wvdT", [32, P]), sb("d_wvu", [32, P]), sb("d_wv", [P, P])
        ew_q, ew_kv, ew_o = sb("e_wq", [P, P]), sb("e_wkv", [P, 2 * P]), sb("e_wo", [P, P])
        e_bv, e_bo = sb("e_bv", [P, P]), sb("e_bo", [1, P])
        wfcT, wpT = sb("f_wfcT", [P, FH]), sb("f_wpT", [P, FC, P])
        gam = sb("f_gam", [P, 8])
        e_bqm = sb("e_bqm", [P, 4])

        x_tm = [sb(f"x_tm{s}", [P, NT, D]) for s in range(STREAMS)]
        xT = [sb(f"xT{s}", [P, W + S]) for s in range(STREAMS)]
        y = [sb(f"y{s}", [P, NT, D]) for s in range(STREAMS)]
        result = [sb(f"result{s}", [P, NT, D]) for s in range(STREAMS)]
        c_tm = [sb(f"c_tm{s}", [CH, 2, D]) for s in range(STREAMS)]
        cn = [sb(f"cn{s}", [CH, 2, D]) for s in range(STREAMS)]
        cT = [sb(f"cT{s}", [P, SC]) for s in range(STREAMS)]
        cnT = [sb(f"cnT{s}", [P, SC]) for s in range(STREAMS)]
        bn = [sb(f"bn{s}", [P, NT, 6]) for s in range(STREAMS)]
        mv = [sb(f"mv{s}", [P, NT, 2]) for s in range(STREAMS)]
        veps = [sb(f"veps{s}", [P, NT]) for s in range(STREAMS)]
        rstd = [sb(f"rstd{s}", [P, NT]) for s in range(STREAMS)]
        mx, nb, sums, rsum = ([sb(f"{n}{s}", [P, 64]) for s in range(STREAMS)] for n in ("mx", "nb", "sums", "rsum"))
        spacer, used = sb("spacer", [P, 1]), [sb(f"used{s}", [P, 1]) for s in range(STREAMS)]
        spread = [sb(f"spread{s}", [P, P]) for s in range(STREAMS)]
        arena_w = [sb(f"arena_w{s}", [P, 6144]) for s in range(STREAMS)]
        arena_q = [sb(f"arena_q{s}", [P, 11164]) for s in range(STREAMS)]

        def view(arena, at, *shape):
            n = int(np.prod(shape))
            v = arena[:, at:at + n]
            if len(shape) == 2:
                v = v.rearrange("p (a b) -> p a b", b=shape[1])
            if len(shape) == 3:
                v = v.rearrange("p (a b c) -> p a b c", b=shape[1], c=shape[2])
            return v

        Qm = [view(a, 0, S // W, 4, W) for a in arena_q]
        QT = [view(a, 2048, S) for a in arena_q]
        GQ = [view(a, 2560, S) for a in arena_q]
        GKm = [view(a, 3072, 8, NL) for a in arena_q]
        GVm = [view(a, 3584, 4, 64) for a in arena_q]
        Vw = [view(a, 3840, 8, P) for a in arena_q]
        tl = [view(a, 4864, S) for a in arena_q]
        tr = [view(a, 5376, S) for a in arena_q]
        loc = [view(a, 5888, S) for a in arena_q]
        pooled = [view(a, 6400, 2, NL) for a in arena_q]
        remT = [view(a, 10144, S) for a in arena_q]
        mixT = [view(a, 7040, S) for a in arena_q]
        picked = [view(a, 7552, 8, 4, W) for a in arena_q]
        KP = [[view(q, 8576, W + S), view(w, 5120, W + S), view(q, 6912, W + S), view(q, 10620, W + S)]
              for q, w in zip(arena_q, arena_w)]
        sc = [view(a, 0, 2, BANK) for a in arena_w]
        PTr = [[view(a, 1024 + 2048 * k, 4, S) for k in range(2)] for a in arena_w]
        PT = [v[0] for v in PTr]
        dg = [view(a, 9120, 4, 8 * W) for a in arena_q]
        lspread = [view(a, 9120, NT, 64) for a in arena_q]
        Rs = [view(a, 6400, S) for a in arena_q]
        xq = [view(a, 0, 4, S) for a in arena_q]
        xk = [view(a, 2048, 4, NK) for a in arena_q]
        xv = [view(a, 4712, 6, 512) for a in arena_q]
        xp = [view(a, 7784, 2, NK) for a in arena_q]
        xo = [view(a, 9116, 4, S) for a in arena_q]
        xPT = [view(a, 0, 4, 6, P) for a in arena_w]
        rot = [view(a, 0, 4, SC) for a in arena_w]
        xr = [v[:].rearrange("p a b -> p (a b)")[:, 0:P] for v in y]
        lg = [view(a, 0, NT, E) for a in arena_q]
        eq = [view(a, 128, NT, E) for a in arena_q]
        pick = [view(a, 256, NT, E) for a in arena_q]
        oh = [view(a, 384, NT, E) for a in arena_q]
        ohT = [view(a, 512, S) for a in arena_q]
        ohm = [a[:, 1024:1024 + S // 2].bitcast(BF16) for a in arena_q]
        hid = [view(a, 1280, EC, S) for a in arena_q]
        dq = [view(a, 0, S) for a in arena_q]
        dk = [view(a, 512, S) for a in arena_q]
        dv = [view(a, 1024, NT, P) for a in arena_q]
        dz = [view(a, 1536, NT, S) for a in arena_q]
        de = [view(a, 3584, NT, S) for a in arena_q]
        eqm = [view(a, 1536, 4, S) for a in arena_q]
        cT4 = [view(a, 5632, 4, SC) for a in arena_q]
        ekb = [view(a, 6914, SC) for a in arena_q]
        ekm = [view(a, 6298, 4, SC) for a in arena_q]
        evm = [view(a, 7170, EV, P) for a in arena_q]
        esc = [view(a, 8194, 2, 4 * SC) for a in arena_q]
        eo = [view(a, 9426, S) for a in arena_q]
        er = [view(a, 9938, P) for a in arena_q]
        ePT = [view(a, 0, 4, EV, P) for a in arena_w]
        fg = [view(a, 0, NT, FH) for a in arena_q]
        fhT = [view(a, 2048, FC, S) for a in arena_q]

        table16 = arena_w[0][:, 0:sum(CONST16.values())]
        sel32 = arena_w[0][0:E, 1024:1024 + EC * P]
        con16, at = {}, 0
        for name, w in CONST16.items():
            con16[name] = table16[:, at:at + w]
            at += w
        wf_raw, wp_raw, wf_t, wp_t = (view(arena_w[1], 512 * k, FC, P) for k in range(4))
        below = view(arena_w[1], 2048, 2, FC, P)
        absd = view(arena_w[1], 3072, 2, FC, P)
        rw_rows = arena_w[1][0:E, 4096:4096 + P]
        dw_vd = arena_w[1][:, 4224:4256]

        PS = [ctx.enter_context(nc.psum_tensor(f"PS{s}", [P, 4 * BANK], F32)) for s in range(STREAMS)]

        def bank(s, i, n=1):
            return PS[s][:, i * BANK:(i + n) * BANK]

        s_table = sem("tables_loaded")
        s_vec, s_vec2 = sem("vectors_loaded"), sem("other_vectors_loaded")
        s_wA, s_wB, s_wC, s_wD, s_wE, s_wF = (sem(f"weights_{n}") for n in "ABCDEF")
        s_wkv, s_wturn = sem("weights_kv"), sem("weights_to_turn")
        s_pool0 = sem("constants_set")
        s_casts = sem("constants_cast")
        s_absum = sem("abs_summed")
        s_setup_pe = sem("setup_products")
        s_setup_act = sem("setup_copies")
        s_setup_vec = sem("setup_vector")

        gate = signal("inputs_used", 1)
        x_in = signal("x_in", 1, 16)
        c_in = signal("c_in", 1, 16)
        stored = signal("stored", 1, 16)
        vown = signal("vector_own", 115)
        var_ready = signal("var_ready", 9)
        rstd_ready = signal("rstd_ready", 9)
        normed = signal("normed", 9)
        turned = signal("turned", 8)
        xT_ready = signal("xT_ready", 8)
        branch = signal("branch_done", 6)
        a_qk, a_lat, a_vw, a_z, a_ro = signals("a_products", 2, 2, 1, 1, 1)
        a_sp, a_vwc, a_tanh = signals("a_copied", 6, 1, 1)
        a_pool, a_qm, a_gkv, a_loc, a_rem, a_mix = signals("a_vector", 1, 1, 2, 2, 1, 1)
        r_sc, r_turn = signal("round_scores", 12), signal("round_turned", 12)
        r_exp, r_ev = signal("round_exp", 12), signal("round_evac", 12)
        r_sub, r_inv, r_rs = (signal(f"round_{n}", 12) for n in ("subtracted", "inverted", "rsum"))
        r_R, r_pv, r_Rc = (signal(f"round_{n}", 3) for n in ("rsum_spread", "values", "rsum_copied"))
        x_ck, x_pr = signals("x_products", 3, 3)
        x_ckv, x_cv = signals("x_copied_v", 2, 3)
        x_cva, x_ca = signals("x_copied_s", 1, 3)
        x_sc = signal("x_scores", XU + 1)
        x_nb, x_exp = signal("x_bias", XU), signal("x_exp", XU)
        x_ta, x_tb = signal("x_turned_a", XU), signal("x_turned_b", XU)
        x_ea, x_eb = signal("x_evac_a", XU), signal("x_evac_b", XU)
        x_pv, x_rs = signal("x_values", XU // 2), signal("x_spread", XU // 2)
        x_rc, x_no = signal("x_rsum_copied", XU // 2), signal("x_normalised", XU // 2)
        c_lg, c_ot, c_h = signals("c_products", 1, 1, EC)
        c_oa, c_ha = signals("c_scalar", 1, EC // 2)
        c_oh, c_ov, c_hv = signals("c_vector", 1, 1, EC // 2)
        d_qkv, d_sc, d_tu = signals("d_products", 1, 1, 1)
        d_ca, d_exp, d_ea = signals("d_scalar", 1, 1, 1)
        d_nb, d_ev = signals("d_vector", 1, 1)
        e_kv, e_q, e_sc = signals("e_scores", 1, 1, EU + 1)
        e_ca, e_exp = signals("e_exp", 4, 2 * EU)
        e_cr, e_cv, e_nb = signals("e_bias", 1, 1, EU)
        e_tu = signal("e_turned", 2 * EU)
        e_ea, e_ev = signal("e_evac_s", EU), signal("e_evac_v", EU)
        e_rs, e_no = signal("e_rsum", NT), signal("e_normalised", NT)
        e_rc = signal("e_rsum_copied", NT)
        f_h, f_tu = signals("f_products", NT, 1)
        f_g, f_ea = signals("f_scalar", NT, 1)
        f_ev = signal("f_evac_v", 1)
        eps_done = signal("eps_added", 9)
        d_far = signal("far_tokens_masked", NT - 1)
        kp_zero = signal("window_zeroed", 4)

        vector_rows, row = [], 0
        for n in ("L0_attn_gate_local_w", "L0_attn_gate_remote_w", "L0_xattn_gamma_x", "L0_xattn_beta_x",
                  "L0_xattn_gamma_l", "L0_xattn_beta_l", "L1_xattn_bq", "L1_xattn_bkv", "L0_ffn_bias1",
                  "L1_ffn_ln_w", "L1_ffn_ln_b"):
            v = io[n][0:P] if n == "L1_xattn_bkv" else io[n]
            if n.startswith("L0_attn_gate"):
                v = v.rearrange("(o h) d -> o (h d)", o=1)
            elif n == "L0_ffn_bias1":
                v = v.rearrange("(c e) h -> c (e h)", c=EC)
            else:
                v = v.rearrange("(c p) -> c p", p=P)
            vector_rows.append((row, v))
            row += v.shape[0]
        assert row == 24

        block = ctx.enter_context(nc.Block())

        @block.sync
        def _(sp):
            def load(dst, name, s, ap=None):
                sp.dma_start(dst, io[name] if ap is None else ap).then_inc(s, 16)

            def stream_in(turn, s):
                b = bass.ds(STREAMS * turn + s, 1)
                sp.dma_start(x_tm[s][:], io["x"][b].rearrange("o (t p) d -> (o p) t d", p=P)).then_inc(x_in[s].sem, 16)
                sp.dma_start(c_tm[s][:], io["ctx_1024"][b].rearrange("o (t p) d -> (o p) t d", p=CH)).then_inc(c_in[s].sem, 16)

            load(table[:], "table", s_table)
            load(wf_raw, None, s_wF, io["L1_ffn_W_fc"].rearrange("(c p) d -> p c d", p=P))
            load(wp_raw, None, s_wF, io["L1_ffn_W_proj"].rearrange("d (c h) -> d c h", h=P))
            load(xw_kv[:], "L0_xattn_Wkv", s_wkv)
            load(table16, "table16", s_table)
            load(sel32, "table_sel", s_table)
            for s in range(STREAMS):
                stream_in(0, s)
            for n, dst in (("wq", w_q), ("wk", w_k), ("wv", w_v), ("wgq", w_gq), ("wgk", w_gk), ("wgv", w_gv),
                           ("r_out_w", w_rout), ("w_out", w_o)):
                load(dst[:], "L0_attn_" + n, s_wA)
            load(xw_q[:], "L0_xattn_Wq", s_wB)
            load(xw_o[:], None, s_wB, io["L0_xattn_Wo"].rearrange("(c p) n -> p c n", p=P))
            load(rb[:], None, s_wC, io["L0_ffn_router_b"].rearrange("(o e) -> o e", o=1).to_broadcast([P, E]))
            load(w1[:], None, s_wC, io["L0_ffn_weights1"].rearrange("e d h -> d e h"))
            load(w2[:], None, s_wC, io["L0_ffn_weights2"].rearrange("(c e) h d -> (e h) c d", c=EC))
            load(b2[:], "L0_ffn_bias2", s_wC)
            load(dw_q[:, 0:32], "L1_attn_Wq", s_wD)
            load(dw_k[:, 0:32], "L1_attn_Wk", s_wD)
            load(ew_q[:], "L1_xattn_Wq", s_wE)
            load(ew_kv[:], "L1_xattn_Wkv", s_wE)
            load(ew_o[:], "L1_xattn_Wo", s_wE)
            load(e_bv[:], None, s_wE, io["L1_xattn_bkv"][P:2 * P].rearrange("(o d) -> o d", o=1).to_broadcast([P, P]))
            load(e_bo[:], None, s_wE, io["L1_xattn_bo"].rearrange("(o d) -> o d", o=1))

            def stream_out(turn, s):
                sp.wait_ge(normed[s].sem, normed[s].at(turn, 9))
                b = bass.ds(STREAMS * turn + s, 1)
                sp.dma_start(out[b].rearrange("o (t p) d -> (o p) t d", p=P), result[s][:]).then_inc(stored[s].sem, 16)

            with sp.Fori(0, TURNS - 1) as turn:
                for s in range(STREAMS):
                    sp.wait_ge(gate[s].sem, gate[s].at(turn, 1))
                    stream_in(turn + 1, s)
                for s in range(STREAMS):
                    stream_out(turn, s)
            for s in range(STREAMS):
                stream_out(TURNS - 1, s)
            for s in range(STREAMS):
                sp.wait_ge(stored[s].sem, 16 * TURNS)

        @block.gpsimd
        def _(pool):
            pool.memset(ones[:], 1.0).then_inc(s_pool0, 1)
            for row, v in vector_rows[0::2]:
                pool.dma_start(vec_rows[row:row + v.shape[0], :], v).then_inc(s_vec, 16)
            pool.memset(tri[:, 0:S - P], 1.0).then_inc(s_pool0, 1)
            pool.memset(tri[:, S:], 0.0).then_inc(s_pool0, 1)
            pool.memset(dw_q[:, 32:], 0.0).then_inc(s_pool0, 1)
            pool.memset(dw_k[:, 32:], 0.0).then_inc(s_pool0, 1)
            pool.memset(halves[:], -0.5).then_inc(s_pool0, 1)
            pool.memset(epsilon[:], EPS).then_inc(s_pool0, 1)
            for s in range(STREAMS):
                pool.memset(xT[s][:, 0:W], 0.0).then_inc(s_pool0, 1)
            pool.wait_ge(s_pool0, 7 + STREAMS)
            with pool.Fori(0, TURNS) as turn:
                def inv_std(k, s):
                    pool.wait_ge(var_ready[s].sem, var_ready[s].at(turn, k))
                    pool.tensor_tensor(veps[s][:], mv[s][:, :, 1], epsilon[:], ALU.add).then_inc(eps_done[s].sem, 1)
                    pool.wait_ge(eps_done[s].sem, eps_done[s].at(turn, k))
                    pool.tensor_tensor(rstd[s][:], veps[s][:], halves[:], ALU.pow).then_inc(rstd_ready[s].sem, 1)

                for s in range(STREAMS):
                    inv_std(1, s)
                    for g in range(4):
                        pool.memset(KP[s][g][:, 0:W], 0.0).then_inc(kp_zero[s].sem, 1)

                def lay_out(v, s):
                    inv = rsum[s][:, 8 * (v % 2):8 * (v % 2) + 8]
                    if v in (4, 8):
                        pool.wait_ge(r_R[s].sem, r_R[s].at(turn, v // 4))
                    pool.wait_ge(r_inv[s].sem, r_inv[s].at(turn, v + 1))
                    if v < 8:
                        m = pool.tensor_tensor(dg[s][:, v % 4, :].rearrange("p (u q) -> p u q", q=W),
                                               winq[:, 0:W].unsqueeze(1).to_broadcast([P, 8, W]),
                                               inv.unsqueeze(2).to_broadcast([P, 8, W]), ALU.mult)
                    else:
                        m = pool.tensor_tensor(lspread[s][:, v - 8, :].rearrange("p (h d) -> p h d", d=HD),
                                               ones[:, 0:64].rearrange("p (h d) -> p h d", d=HD),
                                               inv.unsqueeze(2).to_broadcast([P, 8, HD]), ALU.mult)
                    m.then_inc(r_rs[s].sem, 1)

                for v in range(12):
                    for s in range(STREAMS):
                        lay_out(v, s)
                for k in range(2, 10):
                    for s in range(STREAMS):
                        inv_std(k, s)
                        if k == 5:
                            for t in range(NT - 1):
                                pool.memset(dz[s][:, t, (t + 1) * P:S], FMIN).then_inc(d_far[s].sem, 1)
                for s in range(STREAMS):
                    pool.wait_ge(stored[s].sem, stored[s].at(turn, 1))

        @block.tensor
        def _(pe):
            pe.wait_ge(s_pool0, 7 + STREAMS)
            pe.wait_ge(s_absum, 2)
            pe.matmul(bank(0, 0)[:, 0:2], ones[:], gam[:, 0:2], start=True, stop=True).then_inc(s_setup_pe, 1)
            pe.wait_ge(s_table, 16 * 3)
            pe.wait_ge(s_vec, 16 * 6)
            pe.wait_ge(s_vec2, 16 * 5)
            pe.transpose(bank(1, 0)[:, 0:24], vec_rows[:], ident[0:24, 0:24]).then_inc(s_setup_pe, 1)
            pe.wait_ge(s_wturn, 16 * 3)
            pe.transpose(bank(0, 3)[:, 0:E], rw_rows, ident[0:E, 0:E])
            pe.transpose(bank(0, 3)[0:32, E:E + P], dw_vd, ident).then_inc(s_setup_pe, 1)
            pe.wait_ge(s_setup_vec, 11)
            for c in range(FC):
                pe.transpose(bank(0, 1)[:, c * P:(c + 1) * P], wf_t[:, c, :], ident)
            for c in range(FC):
                mm = pe.transpose(bank(0, 2)[:, c * P:(c + 1) * P], wp_t[:, c, :], ident)
            mm.then_inc(s_setup_pe, 1)
            pe.wait_ge(s_setup_act, 2)
            pe.matmul(bank(0, 0)[:, P:2 * P], dw_vdT[:], dw_vu[:], start=True, stop=True).then_inc(s_setup_pe, 1)
            pe.wait_ge(s_setup_act, 5)
            pe.wait_ge(s_casts, 7)
            pe.wait_ge(s_wA, 16 * 8)
            pe.wait_ge(s_setup_vec, 13)

            with pe.Fori(0, TURNS) as turn:
                def mm(out_, lhsT, rhs, start=True, stop=True):
                    return pe.matmul(out_, lhsT, rhs, start=start, stop=stop, skip_group_check=True)

                def turn_in(s):
                    pe.wait_ge(x_in[s].sem, x_in[s].at(turn, 1))
                    for t in range(NT):
                        m = pe.transpose(bank(s, 2)[:, t * P:(t + 1) * P], x_tm[s][:, t, :], ident)
                    m.then_inc(turned[s].sem, 1)
                    pe.wait_ge(c_in[s].sem, c_in[s].at(turn, 1))
                    for t in range(2):
                        m = pe.transpose(bank(s, 3)[:, t * CH:(t + 1) * CH], c_tm[s][:, t, :], ident[0:CH, 0:CH])
                    m.then_inc(turned[s].sem, 1)

                def tokens(s, t):
                    return xT[s][:, W + t * P:W + (t + 1) * P]

                def turn_rows(k, ln, s):
                    pe.wait_ge(normed[s].sem, normed[s].at(turn, ln))
                    pe.wait_ge(xT_ready[s].sem, xT_ready[s].at(turn, k - 1))
                    for t in range(NT):
                        src = y[s] if k == INNER else x_tm[s]
                        m = pe.transpose(bank(s, 2)[:, t * P:(t + 1) * P], src[:, t, :], ident)
                    m.then_inc(turned[s].sem, 1)

                def qk(s):
                    pe.wait_ge(xT_ready[s].sem, xT_ready[s].at(turn, 1))
                    for i, w in enumerate((w_q, w_k)):
                        mm(bank(s, i), w[:], xT[s][:, W:]).then_inc(a_qk[s].sem, 1)

                def latent_qkv(s):
                    pe.wait_ge(xT_ready[s].sem, xT_ready[s].at(turn, 2))
                    mm(bank(s, 3)[0:64, :], w_gq[:], xT[s][:, W:]).then_inc(a_lat[s].sem, 1)
                    pe.wait_ge(a_pool[s].sem, a_pool[s].at(turn, 1))
                    mm(bank(s, 2)[0:64, 0:NL], w_gk[:], pooled[s][:, 0, :])
                    mm(bank(s, 2)[:, NL:NL + 64], pooled[s].rearrange("p a n -> p (a n)"),
                       w_gv[:]).then_inc(a_lat[s].sem, 1)

                def window_v(s):
                    pe.wait_ge(a_qm[s].sem, a_qm[s].at(turn, 1))
                    pe.wait_ge(a_sp[s].sem, a_sp[s].at(turn, 5))
                    for m in range(8):
                        for b in range(2):
                            a = 64 * m + W * b
                            v = mm(PS[s][64 * b:64 * b + 64, m * P:(m + 1) * P], xT[s][:, a:a + 64], w_v[:])
                    v.then_inc(a_vw[s].sem, 1)

                def gates(s):
                    pe.wait_ge(a_gkv[s].sem, a_gkv[s].at(turn, 2))
                    pe.wait_ge(a_sp[s].sem, a_sp[s].at(turn, 6))
                    mm(bank(s, 2), gate_l[:], QT[s])
                    mm(bank(s, 3), gate_r[:], QT[s]).then_inc(a_z[s].sem, 1)

                def a_scores(v, s):
                    if v == 0:
                        pe.wait_ge(kp_zero[s].sem, kp_zero[s].at(turn, 4))
                        pe.wait_ge(a_tanh[s].sem, a_tanh[s].at(turn, 1))
                    else:
                        pe.wait_ge(r_sub[s].sem, r_sub[s].at(turn, v))
                    if v < 8:
                        half, g = v // 4, v % 4
                        mm(bank(s, 0), winq[:], winmask[:, half * P:(half + 4) * P], stop=False)
                        for u in range(8):
                            n = 8 * half + u
                            for h in range(4):
                                m = mm(bank(s, 0)[32 * h:32 * h + 32, u * 64:(u + 1) * 64], Qm[s][:, n, h],
                                       KP[s][g][:, n * W:(n + 2) * W], start=False)
                    else:
                        t = v - 8
                        mm(bank(s, 0), identb[:], latmask[:, t, :].unsqueeze(1).to_broadcast([P, 8, NL]), stop=False)
                        m = mm(bank(s, 0), GQ[s][0:64, t * P:(t + 1) * P],
                               GKm[s][0:64].rearrange("p h n -> p (h n)"), start=False)
                    m.then_inc(r_sc[s].sem, 1)

                def a_turn(v, s):
                    pe.wait_ge(r_exp[s].sem, r_exp[s].at(turn, v + 1))
                    if v:
                        pe.wait_ge(r_ev[s].sem, r_ev[s].at(turn, v))
                    for j in range(4):
                        m = pe.transpose(bank(s, 1)[:, j * P:(j + 1) * P], sc[s][:, v % 2, j * P:(j + 1) * P], ident)
                    m.then_inc(r_turn[s].sem, 1)

                def window_rsum(r, s):
                    pe.wait_ge(r_rs[s].sem, r_rs[s].at(turn, 4 * r))
                    if r > 1:
                        pe.wait_ge(a_loc[s].sem, a_loc[s].at(turn, r - 1))
                    for g in range(4):
                        m = mm(bank(s, 2)[32 * g:32 * g + 32, 0:8 * W], con["headsel"], dg[s][:, g, :])
                    m.then_inc(r_R[s].sem, 1)

                def window_values(r, s):
                    pe.wait_ge(r_Rc[s].sem, r_Rc[s].at(turn, r))
                    pe.wait_ge(r_ev[s].sem, r_ev[s].at(turn, 4 * r))
                    mm(bank(s, 2)[0:32, 0:1], ident[:, 0:32], ident[:, 0:1])
                    for j in range(4):
                        for b in range(2):
                            k = slice(64 * b, 64 * b + 64)
                            for g in range(4):
                                m = mm(bank(s, 2 + b)[32 * g:32 * g + 32, j * P:(j + 1) * P],
                                       Vw[s][k, 4 * (r - 1) + j, 32 * g:32 * g + 32],
                                       PTr[s][r % 2][k, g, j * P:(j + 1) * P])
                    m.then_inc(r_pv[s].sem, 1)

                def latent_values(t, s):
                    pe.wait_ge(r_rs[s].sem, r_rs[s].at(turn, 9 + t))
                    if t == 0:
                        pe.wait_ge(a_loc[s].sem, a_loc[s].at(turn, 2))
                    cols = slice(t * P, (t + 1) * P)
                    m = mm(bank(s, 3)[0:64, cols], lspread[s][:, t, :], ident)
                    if t == NT - 1:
                        m.then_inc(r_R[s].sem, 1)
                    pe.wait_ge(r_ev[s].sem, r_ev[s].at(turn, 9 + t))
                    for c in range(4):
                        m = mm(bank(s, 2)[0:64, cols], GVm[s][:, c, :], PTr[s][1][:, c, cols], start=c == 0, stop=c == 3)
                    if t == NT - 1:
                        m.then_inc(r_pv[s].sem, 1)

                def latent_out(s):
                    pe.wait_ge(a_rem[s].sem, a_rem[s].at(turn, 1))
                    mm(bank(s, 2), w_rout[:], remT[s][0:64, :]).then_inc(a_ro[s].sem, 1)

                def out_a(s):
                    pe.wait_ge(a_mix[s].sem, a_mix[s].at(turn, 1))
                    for t in range(NT):
                        m = mm(bank(s, 3)[:, t * P:(t + 1) * P], mixT[s][:, t * P:(t + 1) * P], w_o[:])
                    m.then_inc(branch[s].sem, 1)

                def turn_ctx(s):
                    pe.wait_ge(normed[s].sem, normed[s].at(turn, 1))
                    for t in range(2):
                        m = pe.transpose(bank(s, 0)[:, t * CH:(t + 1) * CH], cn[s][:, t, :], ident[0:CH, 0:CH])
                    m.then_inc(turned[s].sem, 1)

                def ctx_keys(s, rotated):
                    if rotated:
                        pe.wait_ge(x_ckv[s].sem, x_ckv[s].at(turn, 1))
                    else:
                        pe.wait_ge(xT_ready[s].sem, xT_ready[s].at(turn, 3))
                    w = xw_kr if rotated else xw_kv
                    for c in range(4):
                        m = mm(bank(s, c // 2)[:, (c % 2) * SC:(c % 2 + 1) * SC], w[:, c * P:(c + 1) * P], cnT[s][:])
                    m.then_inc(x_ck[s].sem, 1)

                def ctx_values(s):
                    pe.wait_ge(x_ckv[s].sem, x_ckv[s].at(turn, 2))
                    for t in range(2):
                        m = mm(bank(s, t)[0:CH, :], cnT[s][:, t * CH:(t + 1) * CH], xw_kv[:, 512:1024])
                    m.then_inc(x_ck[s].sem, 1)

                def x_products(k, s):
                    if k == 1:
                        pe.wait_ge(s_wB, 16 * 2)
                        pe.wait_ge(xT_ready[s].sem, xT_ready[s].at(turn, 4))
                        pe.wait_ge(x_cva[s].sem, x_cva[s].at(turn, 1))
                    else:
                        pe.wait_ge(x_cv[s].sem, x_cv[s].at(turn, k - 1))
                        pe.wait_ge(x_ca[s].sem, x_ca[s].at(turn, k - 1))
                    for c in range(4):
                        if k == 1:
                            m = mm(bank(s, c), xw_q[:, c * P:(c + 1) * P], xT[s][:, W:])
                        elif k == 2:
                            m = mm(bank(s, c), xw_kv[:, c * P:(c + 1) * P], xT[s][:, W:])
                        else:
                            m = mm(bank(s, c), tokens(s, c), xw_kv[:, 512:1024])
                    m.then_inc(x_pr[s].sem, 1)

                def x_turn_a(u, s):
                    pe.wait_ge(x_exp[s].sem, x_exp[s].at(turn, u + 1))
                    if u:
                        pe.wait_ge(x_eb[s].sem, x_eb[s].at(turn, u))
                    for c in range(3):
                        m = pe.transpose(bank(s, 2)[:, c * P:(c + 1) * P], xp[s][:, u % 2, c * P:(c + 1) * P], ident)
                    m.then_inc(x_ta[s].sem, 1)

                def x_scores(u, s):
                    hp, t, h = u // 8, u // 2 % 4, u % 2
                    if u == 0:
                        pe.wait_ge(x_cv[s].sem, x_cv[s].at(turn, 3))
                        pe.wait_ge(x_ca[s].sem, x_ca[s].at(turn, 3))
                    elif u % 2 == 0 and u >= 4:
                        pe.wait_ge(x_rc[s].sem, x_rc[s].at(turn, u // 2 - 1))
                    if u < XU:
                        r = slice(64 * h, 64 * h + 64)
                        q = xq[s][r, hp, t * P:(t + 1) * P]
                        mm(bank(s, 0), q, xk[s][r, hp, 0:S])
                        m = mm(bank(s, 1)[:, 0:SC], q, xk[s][r, hp, S:NK])
                    if u % 2 and u >= 3:
                        pe.wait_ge(x_rs[s].sem, x_rs[s].at(turn, (u - 1) // 2))
                        m = mm(bank(s, 1)[:, 256:384], spread[s][:], ident)
                    m.then_inc(x_sc[s].sem, 1)

                def x_turn_b(u, s):
                    pe.wait_ge(x_ea[s].sem, x_ea[s].at(turn, u + 1))
                    p = xp[s][:, u % 2, :]
                    pe.transpose(bank(s, 2)[:, 0:P], p[:, 3 * P:S], ident)
                    for c in range(2):
                        m = pe.transpose(bank(s, 2)[0:CH, (c + 1) * P:(c + 2) * P], p[:, S + c * CH:S + (c + 1) * CH], ident)
                    m.then_inc(x_tb[s].sem, 1)

                def x_values(j, s):
                    hp, t = j // 4, j % 4
                    pe.wait_ge(x_ea[s].sem, x_ea[s].at(turn, 2 * j + 2))
                    pe.wait_ge(x_eb[s].sem, x_eb[s].at(turn, 2 * j + 2))
                    if j:
                        pe.wait_ge(x_no[s].sem, x_no[s].at(turn, j))
                    for c in range(6):
                        k = P if c < 4 else CH
                        for h in range(2):
                            col = (2 * hp + h) * 64
                            m = mm(bank(s, 3)[64 * h:64 * h + 64, t * P:(t + 1) * P], xv[s][0:k, c, col:col + 64],
                                   xPT[s][0:k, (2 * j + h) % 4, c, :], start=c == 0, stop=c == 5)
                    m.then_inc(x_pv[s].sem, 1)

                def out_b(s):
                    pe.wait_ge(x_no[s].sem, x_no[s].at(turn, XU // 2))
                    for t in range(NT):
                        for c in range(4):
                            m = mm(bank(s, 3)[:, t * P:(t + 1) * P], xo[s][:, c, t * P:(t + 1) * P], xw_o[:, c, :],
                                   start=c == 0, stop=c == 3)
                    m.then_inc(branch[s].sem, 1)

                def logits(s):
                    pe.wait_ge(xT_ready[s].sem, xT_ready[s].at(turn, 5))
                    for t in range(NT):
                        m = mm(bank(s, 2)[:, t * E:(t + 1) * E], tokens(s, t), rw[:])
                    m.then_inc(c_lg[s].sem, 1)

                def turn_onehot(s):
                    pe.wait_ge(c_oh[s].sem, c_oh[s].at(turn, 1))
                    for t in range(NT):
                        m = pe.transpose(bank(s, 2)[0:E, t * P:(t + 1) * P], oh[s][:, t, :], ident)
                    m.then_inc(c_ot[s].sem, 1)

                def hidden_product(c, s):
                    if c == 0:
                        pe.wait_ge(s_wC, 16 * 4)
                    if c >= 3:
                        relu_done = (c_ha, c_hv)[(c - 3) % 2][s]
                        pe.wait_ge(relu_done.sem, relu_done.at(turn, (c - 3) // 2 + 1))
                    mm(bank(s, c % 3), w1[:, 4 * c:4 * c + 4, :].rearrange("p e h -> p (e h)"), xT[s][:, W:], stop=False)

                def hidden_mask(c, s):
                    if c == 0:
                        pe.wait_ge(c_ov[s].sem, c_ov[s].at(turn, 1))
                    mm(bank(s, c % 3), selb[:, c, :], ohm[s][0:E, :], start=False).then_inc(c_h[s].sem, 1)

                def out_c(s):
                    pe.wait_ge(c_ha[s].sem, c_ha[s].at(turn, 4))
                    pe.wait_ge(c_hv[s].sem, c_hv[s].at(turn, 4))
                    for t in range(NT):
                        cols = slice(t * P, (t + 1) * P)
                        for c in range(EC):
                            mm(bank(s, 3)[:, cols], hid[s][:, c, cols], w2[:, c, :], start=c == 0, stop=False)
                        m = mm(bank(s, 3)[:, cols], ohT[s][0:E, cols], b2[:], start=False)
                    m.then_inc(branch[s].sem, 1)

                def d_products(s):
                    pe.wait_ge(s_wD, 16 * 2)
                    pe.wait_ge(e_cr[s].sem, e_cr[s].at(turn, 1))
                    pe.wait_ge(xT_ready[s].sem, xT_ready[s].at(turn, 6))
                    mm(bank(s, 0), dw_q[:], xT[s][:, W:])
                    mm(bank(s, 1), dw_k[:], xT[s][:, W:])
                    for t in range(NT):
                        m = mm(bank(s, 3)[:, t * P:(t + 1) * P], tokens(s, t), dw_v[:])
                    m.then_inc(d_qkv[s].sem, 1)

                def d_scores(s):
                    pe.wait_ge(d_ca[s].sem, d_ca[s].at(turn, 1))
                    for t in range(NT):
                        m = mm(bank(s, t)[:, 0:(t + 1) * P], dq[s][:, t * P:(t + 1) * P], dk[s][:, 0:(t + 1) * P])
                    m.then_inc(d_sc[s].sem, 1)

                def d_turn(s):
                    pe.wait_ge(d_exp[s].sem, d_exp[s].at(turn, 1))
                    for c in range(4):
                        for t in range(NT):
                            m = pe.transpose(bank(s, c)[:, t * P:(t + 1) * P], dz[s][:, t, c * P:(c + 1) * P], ident)
                    m.then_inc(d_tu[s].sem, 1)

                def out_d(s):
                    pe.wait_ge(d_ea[s].sem, d_ea[s].at(turn, 1))
                    pe.wait_ge(d_ev[s].sem, d_ev[s].at(turn, 1))
                    for t in range(NT):
                        for c in range(4):
                            m = mm(bank(s, 3)[:, t * P:(t + 1) * P], PT[s][:, c, t * P:(t + 1) * P], dv[s][:, c, :],
                                   start=c == 0, stop=c == 3)
                    m.then_inc(branch[s].sem, 1)

                def e_context(s):
                    pe.wait_ge(s_wE, 16 * 5)
                    mm(bank(s, 1)[:, 0:SC], ew_kv[:, 0:P], cT[s][:])
                    rows = cT4[s].rearrange("p h j -> p (h j)")
                    for c in range(EV - 1):
                        mm(bank(s, 0)[:, c * P:(c + 1) * P], rows[:, c * P:(c + 1) * P], ew_kv[:, P:2 * P])
                    mm(bank(s, 1)[0:ELAST, 256:384], rows[:, (EV - 1) * P:], ew_kv[:, P:2 * P]).then_inc(e_kv[s].sem, 1)

                def e_queries(s):
                    pe.wait_ge(xT_ready[s].sem, xT_ready[s].at(turn, 7))
                    mm(bank(s, 3), ew_q[:], xT[s][:, W:]).then_inc(e_q[s].sem, 1)

                def e_turn(u, s):
                    pe.wait_ge(e_exp[s].sem, e_exp[s].at(turn, 2 * u + 1))
                    if u:
                        pe.wait_ge(e_ev[s].sem, e_ev[s].at(turn, u))
                    for c in range(EV - 1):
                        if c == 2 * SC // P:
                            pe.wait_ge(e_exp[s].sem, e_exp[s].at(turn, 2 * u + 2))
                        m = pe.transpose(bank(s, 2)[:, c * P:(c + 1) * P], esc[s][:, u % 2, c * P:(c + 1) * P], ident)
                    m.then_inc(e_tu[s].sem, 1)
                    if u:
                        pe.wait_ge(e_ea[s].sem, e_ea[s].at(turn, u))
                    pe.transpose(bank(s, 3)[0:ELAST, 0:P], esc[s][:, u % 2, (EV - 1) * P:4 * SC],
                                 ident).then_inc(e_tu[s].sem, 1)

                def e_scores(u, s):
                    t, g = u // 4, u % 4
                    if u < 4:
                        pe.wait_ge(e_ca[s].sem, e_ca[s].at(turn, u + 1))
                    if u == 0:
                        pe.wait_ge(e_cv[s].sem, e_cv[s].at(turn, 1))
                    else:
                        pe.wait_ge(e_exp[s].sem, e_exp[s].at(turn, min(2 * u - 1, 2 * EU)))
                        if u % 4 == 2 and u > 4:
                            pe.wait_ge(e_no[s].sem, e_no[s].at(turn, u // 4))
                    if u < EU:
                        for k in range(2):
                            if k and u:
                                pe.wait_ge(e_exp[s].sem, e_exp[s].at(turn, 2 * u))
                            m = mm(bank(s, k)[:, 0:2 * SC], eqm[s][:, g, t * P:(t + 1) * P],
                                   ekm[s][:, 2 * k:2 * k + 2, :].rearrange("p h n -> p (h n)"))
                    if u % 4 == 1 and u > 4:
                        m = e_values(u // 4 - 1, s)
                    m.then_inc(e_sc[s].sem, 1)

                def e_values(t, s):
                    pe.wait_ge(e_ea[s].sem, e_ea[s].at(turn, 4 * t + 4))
                    pe.wait_ge(e_ev[s].sem, e_ev[s].at(turn, 4 * t + 4))
                    for c in range(EV):
                        k = P if c < EV - 1 else ELAST
                        for g in range(4):
                            r = slice(32 * g, 32 * g + 32)
                            mm(bank(s, 1)[r, 384:512], evm[s][0:k, c, r], ePT[s][0:k, g, c, :], start=c == 0,
                               stop=c == EV - 1)
                    pe.wait_ge(e_rs[s].sem, e_rs[s].at(turn, t + 1))
                    return mm(bank(s, 0)[:, 384:512], spread[s][:], ident)

                def out_e(s):
                    pe.wait_ge(e_no[s].sem, e_no[s].at(turn, 4))
                    for t in range(NT):
                        cols = slice(t * P, (t + 1) * P)
                        mm(bank(s, 3)[:, cols], eo[s][:, cols], ew_o[:], stop=False)
                        m = mm(bank(s, 3)[:, cols], ones[0:1, :], e_bo[:], start=False)
                    m.then_inc(branch[s].sem, 1)

                def f_hidden(s):
                    pe.wait_ge(xT_ready[s].sem, xT_ready[s].at(turn, 8))
                    for t in range(NT):
                        mm(bank(s, t), tokens(s, t), wfcT[:]).then_inc(f_h[s].sem, 1)

                def f_turn(s):
                    pe.wait_ge(normed[s].sem, normed[s].at(turn, 8))
                    for c in range(FC):
                        for t in range(NT):
                            m = pe.transpose(bank(s, c)[:, t * P:(t + 1) * P], fg[s][:, t, c * P:(c + 1) * P], ident)
                    m.then_inc(f_tu[s].sem, 1)

                def out_f(s):
                    pe.wait_ge(f_ea[s].sem, f_ea[s].at(turn, 1))
                    pe.wait_ge(f_ev[s].sem, f_ev[s].at(turn, 1))
                    for t in range(NT):
                        for c in range(FC):
                            m = mm(bank(s, 3)[:, t * P:(t + 1) * P], fhT[s][:, c, t * P:(t + 1) * P], wpT[:, c, :],
                                   start=c == 0, stop=c == 3)
                    m.then_inc(branch[s].sem, 1)

                both = range(STREAMS)
                for step in (turn_in, qk, latent_qkv, window_v, gates):
                    for s in both:
                        step(s)
                for v in range(14):
                    for s in both:
                        if 1 <= v <= 12:
                            a_turn(v - 1, s)
                        if v < 12:
                            a_scores(v, s)
                        if v in (5, 9):
                            window_rsum(v // 4, s)
                        if v in (6, 10):
                            window_values(v // 4, s)
                        if v == 11:
                            latent_values(0, s)
                        if v >= 11:
                            latent_values(v - 10, s)
                for s in both:
                    latent_out(s)
                for s in both:
                    turn_ctx(s)
                for s in both:
                    ctx_keys(s, False)
                    out_a(s)
                for s in both:
                    ctx_keys(s, True)
                for s in both:
                    ctx_values(s)
                for s in both:
                    turn_rows(INNER, 3, s)
                for k in (1, 2, 3):
                    for s in both:
                        x_products(k, s)
                for u in range(XU + 2):
                    for s in both:
                        if 1 <= u <= XU:
                            x_turn_a(u - 1, s)
                        if u != XU:
                            x_scores(u, s)
                        if 1 <= u <= XU:
                            x_turn_b(u - 1, s)
                        if u >= 3 and u % 2:
                            x_values((u - 3) // 2, s)
                for s in both:
                    out_b(s)
                for s in both:
                    turn_rows(5, 4, s)
                    logits(s)
                    for c in range(2):
                        hidden_product(c, s)
                for s in both:
                    turn_onehot(s)
                for c in range(EC):
                    for s in both:
                        if c >= 2:
                            hidden_product(c, s)
                        hidden_mask(c, s)
                for s in both:
                    out_c(s)
                    e_context(s)
                for s in both:
                    turn_rows(6, 5, s)
                    if s == 1:
                        d_scores(0)
                    d_products(s)
                d_scores(1)
                for s in both:
                    d_turn(s)
                    out_d(s)
                for s in both:
                    turn_rows(7, 6, s)
                    e_queries(s)
                    e_scores(0, s)
                for u in range(1, EU + 2):
                    for s in both:
                        if u <= EU:
                            e_turn(u - 1, s)
                        if u != EU:
                            e_scores(u, s)
                for s in both:
                    out_e(s)
                for s in both:
                    turn_rows(8, 7, s)
                    f_hidden(s)
                for s in both:
                    f_turn(s)
                    out_f(s)

        @block.scalar
        def _(act):
            def copy(dst, src):
                return act.activation(dst, src, ACT.Copy)

            act.dma_start(rw_rows, io["L0_ffn_router_w"]).then_inc(s_wturn, 16)
            act.dma_start(dw_vd, io["L1_attn_Wvdown"]).then_inc(s_wturn, 16)
            act.dma_start(dw_vu[:], io["L1_attn_Wvup"]).then_inc(s_wturn, 16)
            for row, v in vector_rows[1::2]:
                act.dma_start(vec_rows[row:row + v.shape[0], :], v).then_inc(s_vec2, 16)
            act.wait_ge(s_wF, 16 * 2)
            for k, w in enumerate((wf_raw, wp_raw)):
                act.activation(absd[:, k], w, ACT.Abs, accum_out=gam[:, k:k + 1]).then_inc(s_absum, 1)
            act.wait_ge(s_setup_pe, 3)
            copy(rw[:], bank(0, 3)[:, 0:E]).then_inc(s_setup_act, 1)
            copy(dw_vdT[:], bank(0, 3)[0:32, E:E + P]).then_inc(s_setup_act, 1)
            act.wait_ge(s_setup_pe, 4)
            copy(wfcT[:], bank(0, 1)).then_inc(s_setup_act, 1)
            copy(wpT[:].rearrange("p c d -> p (c d)"), bank(0, 2)).then_inc(s_setup_act, 1)
            act.wait_ge(s_setup_pe, 5)
            copy(dw_v[:], bank(0, 0)[:, P:2 * P]).then_inc(s_setup_act, 1)
            act.wait_ge(s_setup_vec, 1)

            with act.Fori(0, TURNS) as turn:
                def affine(dst, src, scale, bias):
                    return act.activation(dst, src, ACT.Identity, scale=scale, bias=bias)

                def rows_to_T(k, s):
                    act.wait_ge(turned[s].sem, turned[s].at(turn, k))
                    if k == 2:
                        m = copy(cT[s][:], bank(s, 3)[:, 0:SC])
                    elif k == 3:
                        m = affine(cnT[s][:], bank(s, 0)[:, 0:SC], lnp[:, 0:1], lnp[:, 1:2])
                    elif k == INNER:
                        m = affine(xT[s][:, W:], bank(s, 2), lnp[:, 2:3], lnp[:, 3:4])
                    else:
                        m = copy(xT[s][:, W:], bank(s, 2))
                    m.then_inc(xT_ready[s].sem, 1)

                def copy_qk(s):
                    act.wait_ge(a_qk[s].sem, a_qk[s].at(turn, 2))
                    for g in range(4):
                        act.activation(KP[s][g][:, W:], bank(s, 1), ACT.Identity,
                                       scale=con["group"][:, g:g + 1]).then_inc(a_sp[s].sem, 1)
                    act.wait_ge(a_qm[s].sem, a_qm[s].at(turn, 1))
                    copy(QT[s], bank(s, 0)).then_inc(a_sp[s].sem, 1)

                def copy_gq(s):
                    act.wait_ge(a_lat[s].sem, a_lat[s].at(turn, 1))
                    copy(GQ[s][0:64, :], bank(s, 3)[0:64, :]).then_inc(a_sp[s].sem, 1)

                def copy_window_v(s):
                    act.wait_ge(a_vw[s].sem, a_vw[s].at(turn, 1))
                    copy(Vw[s].rearrange("p a b -> p (a b)"), bank(s, 0, 2)).then_inc(a_vwc[s].sem, 1)

                def tanh_gates(s):
                    act.wait_ge(a_z[s].sem, a_z[s].at(turn, 1))
                    act.activation(tl[s], bank(s, 2), ACT.Tanh, scale=0.5)
                    act.activation(tr[s], bank(s, 3), ACT.Tanh, scale=0.5).then_inc(a_tanh[s].sem, 1)

                def a_exp(v, s):
                    act.wait_ge(r_sub[s].sem, r_sub[s].at(turn, v + 1))
                    act.activation(sc[s][:, v % 2, :], sc[s][:, v % 2, :], ACT.Exp,
                                   scale=HD ** -0.5).then_inc(r_exp[s].sem, 1)

                def a_copy_probs(v, s):
                    act.wait_ge(r_turn[s].sem, r_turn[s].at(turn, v + 1))
                    if v == 8:
                        act.wait_ge(r_pv[s].sem, r_pv[s].at(turn, 1))
                    if v < 8:
                        m = copy(PTr[s][(v // 4 + 1) % 2][:, v % 4, :], bank(s, 1))
                    else:
                        t = v - 8
                        m = copy(PTr[s][1][:, :, t * P:(t + 1) * P], bank(s, 1).rearrange("p (c q) -> p c q", c=4))
                    m.then_inc(r_ev[s].sem, 1)

                def a_copy_rsum(r, s):
                    act.wait_ge(r_R[s].sem, r_R[s].at(turn, r))
                    if r > 1:
                        act.wait_ge(a_loc[s].sem, a_loc[s].at(turn, r - 1))
                    m = copy(Rs[s][:, 0:8 * W], bank(s, 2)[:, 0:8 * W]) if r < 3 else copy(Rs[s][0:64, :], bank(s, 3)[0:64, :])
                    m.then_inc(r_Rc[s].sem, 1)

                def copy_ctx_values(s):
                    act.wait_ge(x_ck[s].sem, x_ck[s].at(turn, 3))
                    copy(xv[s][0:CH, 4:6, :].rearrange("p a b -> p (a b)"),
                         bank(s, 0, 2)[0:CH, :]).then_inc(x_cva[s].sem, 1)

                def copy_x(k, s):
                    act.wait_ge(x_pr[s].sem, x_pr[s].at(turn, k))
                    dst = (xq[s][:, 2:4, :], xk[s][:, 2:4, 0:S], xv[s][:, 2:4, :])[k - 1]
                    copy(dst, bank(s, 2, 2).rearrange("p (a b) -> p a b", a=2)).then_inc(x_ca[s].sem, 1)

                def x_exp_unit(u, s):
                    act.wait_ge(x_nb[s].sem, x_nb[s].at(turn, u + 1))
                    if u >= 2:
                        act.wait_ge(x_tb[s].sem, x_tb[s].at(turn, u - 1))
                    act.activation(xp[s][:, u % 2, :], PS[s][:, 0:NK], ACT.Exp, scale=XD ** -0.5, bias=nb[s][:, u:u + 1],
                                   accum_out=sums[s][:, u:u + 1]).then_inc(x_exp[s].sem, 1)

                def x_copy_b(u, s):
                    act.wait_ge(x_tb[s].sem, x_tb[s].at(turn, u + 1))
                    if u >= 4:
                        act.wait_ge(x_pv[s].sem, x_pv[s].at(turn, (u - 4) // 2 + 1))
                    copy(xPT[s][:, u % 4, 3:6, :].rearrange("p c q -> p (c q)"),
                         bank(s, 2)[:, 0:3 * P]).then_inc(x_eb[s].sem, 1)

                def x_copy_rsum(j, s):
                    if j == XU // 2 - 1:
                        act.wait_ge(x_sc[s].sem, x_sc[s].at(turn, XU + 1))
                    if j:
                        act.wait_ge(x_no[s].sem, x_no[s].at(turn, j))
                    copy(xr[s], bank(s, 1)[:, 256:384]).then_inc(x_rc[s].sem, 1)

                def copy_onehot(s):
                    act.wait_ge(c_ot[s].sem, c_ot[s].at(turn, 1))
                    copy(ohT[s][0:E, :], bank(s, 2)[0:E, :]).then_inc(c_oa[s].sem, 1)

                def relu(c, s):
                    act.wait_ge(c_h[s].sem, c_h[s].at(turn, c + 1))
                    act.activation(hid[s][:, c, :], bank(s, c % 3), ACT.Relu, bias=b1[:, c:c + 1]).then_inc(c_ha[s].sem, 1)

                def copy_dqkv(s):
                    act.wait_ge(d_qkv[s].sem, d_qkv[s].at(turn, 1))
                    copy(dq[s], bank(s, 0))
                    copy(dk[s], bank(s, 1))
                    copy(dv[s].rearrange("p a b -> p (a b)"), bank(s, 3)).then_inc(d_ca[s].sem, 1)

                def d_exp_rows(s):
                    act.wait_ge(d_far[s].sem, d_far[s].at(turn, NT - 1))
                    act.wait_ge(d_nb[s].sem, d_nb[s].at(turn, 1))
                    for t in range(NT):
                        m = act.activation(dz[s][:, t, :], dz[s][:, t, :], ACT.Exp, bias=nb[s][:, t:t + 1],
                                           accum_out=sums[s][:, t:t + 1])
                    m.then_inc(d_exp[s].sem, 1)

                def copy_d(s):
                    act.wait_ge(d_tu[s].sem, d_tu[s].at(turn, 1))
                    copy(PT[s][:, 2:4, :].rearrange("p a b -> p (a b)"), bank(s, 2, 2)).then_inc(d_ea[s].sem, 1)

                def copy_eq(s):
                    act.wait_ge(e_q[s].sem, e_q[s].at(turn, 1))
                    for g in range(4):
                        act.activation(eqm[s][:, g, :], bank(s, 3), ACT.Identity, scale=con["group"][:, g:g + 1],
                                       bias=e_bqm[:, g:g + 1]).then_inc(e_ca[s].sem, 1)

                def e_exp_unit(u, s):
                    act.wait_ge(e_nb[s].sem, e_nb[s].at(turn, u + 1))
                    if u >= 2:
                        act.wait_ge(e_tu[s].sem, e_tu[s].at(turn, 2 * u - 2))
                    for h in range(4):
                        j = 4 * u + h
                        m = act.activation(esc[s][:, u % 2, h * SC:(h + 1) * SC],
                                           bank(s, h // 2)[:, (h % 2) * SC:(h % 2 + 1) * SC], ACT.Exp,
                                           scale=HD ** -0.5, bias=nb[s][:, j:j + 1], accum_out=sums[s][:, j:j + 1])
                        if h % 2:
                            m.then_inc(e_exp[s].sem, 1)

                def e_copy_probs(u, s):
                    act.wait_ge(e_tu[s].sem, e_tu[s].at(turn, 2 * u + 2))
                    if u % 4 == 0 and u:
                        act.wait_ge(e_sc[s].sem, e_sc[s].at(turn, u + 2))
                    copy(ePT[s][0:ELAST, u % 4, EV - 1, :], bank(s, 3)[0:ELAST, 0:P]).then_inc(e_ea[s].sem, 1)

                def e_copy_rsum(t, s):
                    if t == NT - 1:
                        act.wait_ge(e_sc[s].sem, e_sc[s].at(turn, EU + 1))
                    copy(er[s], bank(s, 0)[:, 384:512]).then_inc(e_rc[s].sem, 1)

                def gelu(s):
                    for t in range(NT):
                        act.wait_ge(f_h[s].sem, f_h[s].at(turn, t + 1))
                        act.activation(fg[s][:, t, :], bank(s, t), ACT.Gelu).then_inc(f_g[s].sem, 1)

                def copy_f(s):
                    act.wait_ge(f_tu[s].sem, f_tu[s].at(turn, 1))
                    for c in (2, 3):
                        m = affine(fhT[s][:, c, :], bank(s, c), f_w[:, c:c + 1], f_b[:, c:c + 1])
                    m.then_inc(f_ea[s].sem, 1)

                both = range(STREAMS)
                for s in both:
                    rows_to_T(1, s)
                    rows_to_T(2, s)
                for step in (copy_qk, copy_gq, copy_window_v, tanh_gates):
                    for s in both:
                        step(s)
                for v in range(14):
                    for s in both:
                        if 1 <= v <= 12:
                            a_copy_probs(v - 1, s)
                        if v < 12:
                            a_exp(v, s)
                        if v in (5, 9, 13):
                            a_copy_rsum(v // 4, s)
                for s in both:
                    rows_to_T(3, s)
                for s in both:
                    copy_ctx_values(s)
                for s in both:
                    rows_to_T(INNER, s)
                for k in (1, 2, 3):
                    for s in both:
                        copy_x(k, s)
                for u in range(XU + 2):
                    for s in both:
                        if 1 <= u <= XU:
                            x_copy_b(u - 1, s)
                        if u < XU:
                            x_exp_unit(u, s)
                        if u >= 3 and u % 2:
                            x_copy_rsum((u - 3) // 2, s)
                for s in both:
                    rows_to_T(5, s)
                for s in both:
                    copy_onehot(s)
                for c in range(0, EC, 2):
                    for s in both:
                        relu(c, s)
                for s in both:
                    rows_to_T(6, s)
                    copy_dqkv(s)
                for s in both:
                    d_exp_rows(s)
                    copy_d(s)
                for s in both:
                    rows_to_T(7, s)
                    copy_eq(s)
                for u in range(EU + 2):
                    for s in both:
                        if u < EU:
                            e_exp_unit(u, s)
                        if u % 4 == 1 and u > 4:
                            e_copy_rsum(u // 4 - 1, s)
                        if 1 <= u <= EU:
                            e_copy_probs(u - 1, s)
                for s in both:
                    rows_to_T(8, s)
                    gelu(s)
                for s in both:
                    copy_f(s)

        @block.vector
        def _(dve):
            dve.wait_ge(s_table, 16 * 3)
            for dst, src in ((latmask[:].rearrange("p a b -> p (a b)"), con16["latmask"]), (winmask[:, 0:P], con16["winmask"][:, 0:P]),
                             (winmask[:, P:].rearrange("p (a b) -> p a b", b=P),
                              con16["winmask"][:, P:].unsqueeze(1).to_broadcast([P, 4, P])),
                             (tri[:, S - P:S], con["tri"]),
                             (winq[:], con16["winq"]), (identb[:], ident),
                             (selb[:].rearrange("p a b -> p (a b)"), sel32)):
                dve.tensor_copy(dst, src).then_inc(s_casts, 1)
            dve.wait_ge(s_setup_pe, 2)
            dve.tensor_copy(vec[:], bank(1, 0)[:, 0:24]).then_inc(s_setup_vec, 1)
            dve.wait_ge(s_setup_vec, 1)
            dve.tensor_scalar(gate_l[:], con["headblk"], gatew[:, 0:1], None, ALU.mult).then_inc(s_setup_vec, 1)
            dve.tensor_scalar(gate_r[:], con["headblk"], gatew[:, 1:2], None, ALU.mult).then_inc(s_setup_vec, 1)
            dve.tensor_scalar(e_bqm[:], con["group"], e_bq, None, ALU.mult).then_inc(s_setup_vec, 1)
            dve.wait_ge(s_setup_pe, 1)
            dve.tensor_scalar(gam[:, 2:4], bank(0, 0)[:, 0:2], 1.0 / (FH * D), 1e-6, ALU.mult, ALU.add).then_inc(s_setup_vec, 1)
            dve.wait_ge(s_setup_vec, 5)
            dve.tensor_scalar(gam[:, 4:6], gam[:, 2:4], 0.5, None, ALU.mult).then_inc(s_setup_vec, 1)
            dve.tensor_scalar(gam[:, 6:8], gam[:, 2:4], -0.5, None, ALU.mult).then_inc(s_setup_vec, 1)
            dve.wait_ge(s_setup_vec, 7)
            dve.wait_ge(s_wF, 16 * 2)
            for k, w in enumerate((wf_raw, wp_raw)):
                dve.tensor_scalar(below[:, k], w, gam[:, 6 + k:7 + k], None, ALU.is_lt).then_inc(s_setup_vec, 1)
            dve.wait_ge(s_setup_vec, 9)
            for k, (w, t) in enumerate(((wf_raw, wf_t), (wp_raw, wp_t))):
                dve.scalar_tensor_tensor(out=t, in0=w, scalar=gam[:, 4 + k:5 + k], in1=below[:, k], op0=ALU.is_gt,
                                         op1=ALU.subtract).then_inc(s_setup_vec, 1)
            dve.wait_ge(s_wkv, 16)
            wk, wr = (w.rearrange("p (h d) -> p h d", d=XD) for w in (xw_kv[:, 0:512], xw_kr[:]))
            dve.tensor_scalar(wr[:, :, 0:32], wk[:, :, 32:64], -1.0, None, ALU.mult).then_inc(s_setup_vec, 1)
            dve.tensor_copy(wr[:, :, 32:64], wk[:, :, 0:32]).then_inc(s_setup_vec, 1)
            for s in range(STREAMS):
                dve.memset(mv[s][:], 1.0).then_inc(s_casts, 1)
            dve.wait_ge(s_casts, 7 + STREAMS)
            dve.wait_ge(s_pool0, 7 + STREAMS)

            with dve.Fori(0, TURNS) as turn:
                steps_own = [0] * STREAMS

                def own(s, ins):
                    steps_own[s] += 1
                    ins.then_inc(vown[s].sem, 1)
                    dve.wait_ge(vown[s].sem, vown[s].at(turn, steps_own[s]))

                def stats(k, s, src, n, rows=P):
                    for t in range(n):
                        m = dve.bn_stats(bn[s][0:rows, t, :], src[:, t, :])
                    own(s, m)
                    dve.memset(spacer[:], 0.0)
                    for t in range(n):
                        m = dve.bn_aggr(mv[s][0:rows, t, :], bn[s][0:rows, t, :])
                    m.then_inc(var_ready[s].sem, 1)

                def normalise(k, s, dst, src, n, rows=P):
                    dve.wait_ge(rstd_ready[s].sem, rstd_ready[s].at(turn, k))
                    for t in range(n):
                        m = dve.tensor_scalar(dst[:, t, :], src[:, t, :], mv[s][0:rows, t, 0:1], rstd[s][0:rows, t:t + 1],
                                              ALU.subtract, ALU.mult)
                    m.then_inc(normed[s].sem, 1)

                def residual(b, k, s, scalar, op):
                    dve.wait_ge(branch[s].sem, branch[s].at(turn, b))
                    own(s, dve.scalar_tensor_tensor(out=y[s][:].rearrange("p a b -> p (a b)"), in0=bank(s, 3),
                                                    scalar=scalar, in1=x_tm[s][:].rearrange("p a b -> p (a b)"),
                                                    op0=op, op1=ALU.add))
                    stats(k, s, y[s], NT)

                def ctx_stats(s):
                    dve.wait_ge(c_in[s].sem, c_in[s].at(turn, 1))
                    stats(1, s, c_tm[s], 2, CH)

                def pool_latents(s):
                    dve.wait_ge(xT_ready[s].sem, xT_ready[s].at(turn, 1))
                    own(s, dve.tensor_reduce(pooled[s][:, 0, :], xT[s][:, W:].rearrange("p (n k) -> p n k", k=S // NL), AX, ALU.add))
                    own(s, dve.tensor_scalar(pooled[s][:, 1, :], pooled[s][:, 0, :], NL / S, None, ALU.mult))
                    dve.tensor_copy(pooled[s][:, 0, :], pooled[s][:, 1, :]).then_inc(a_pool[s].sem, 1)

                def mask_q(s):
                    dve.wait_ge(a_qk[s].sem, a_qk[s].at(turn, 1))
                    shape = [P, S // W, 4, W]
                    dve.tensor_tensor(Qm[s], bank(s, 0).rearrange("p (n q) -> p n q", q=W).unsqueeze(2).to_broadcast(shape),
                                      mask4.unsqueeze(1).unsqueeze(3).to_broadcast(shape), ALU.mult).then_inc(a_qm[s].sem, 1)

                def mask_latents(s):
                    dve.wait_ge(a_lat[s].sem, a_lat[s].at(turn, 2))
                    dve.tensor_tensor(GKm[s][0:64], bank(s, 2)[0:64, 0:NL].unsqueeze(1).to_broadcast([64, 8, NL]),
                                      con["mask8"][0:64].unsqueeze(2).to_broadcast([64, 8, NL]),
                                      ALU.mult).then_inc(a_gkv[s].sem, 1)
                    dve.tensor_tensor(GVm[s], bank(s, 2)[:, NL:NL + 64].unsqueeze(1).to_broadcast([P, 4, 64]),
                                      con["gvmask"].rearrange("p (c f) -> p c f", c=4), ALU.mult).then_inc(a_gkv[s].sem, 1)

                def a_softmax(v, s):
                    last, half = (v - 1) % 2, slice(8 * ((v - 1) % 2), 8 * ((v - 1) % 2) + 8)
                    if v:
                        dve.wait_ge(r_exp[s].sem, r_exp[s].at(turn, v))
                        m = dve.tensor_reduce(sums[s][:, half], sc[s][:, last, :].rearrange("p (u n) -> p u n", n=64), AX,
                                              ALU.add)
                    if v < 12:
                        dve.wait_ge(r_sc[s].sem, r_sc[s].at(turn, v + 1))
                        scores = bank(s, 0).rearrange("p (u n) -> p u n", n=64)
                        m = dve.tensor_reduce(mx[s][:, 0:8], scores, AX, ALU.max)
                    own(s, m)
                    if v < 12:
                        if v >= 2:
                            dve.wait_ge(r_turn[s].sem, r_turn[s].at(turn, v - 1))
                        dve.tensor_tensor(sc[s][:, v % 2, :].rearrange("p (u n) -> p u n", n=64), scores,
                                          mx[s][:, 0:8].unsqueeze(2).to_broadcast([P, 8, 64]),
                                          ALU.subtract).then_inc(r_sub[s].sem, 1)
                    if v:
                        if v >= 3:
                            dve.wait_ge(r_rs[s].sem, r_rs[s].at(turn, v - 2))
                        dve.reciprocal(rsum[s][:, half], sums[s][:, half]).then_inc(r_inv[s].sem, 1)

                def pick_heads(r, s):
                    dve.wait_ge(r_pv[s].sem, r_pv[s].at(turn, r))
                    own(s, dve.tensor_tensor(picked[s], bank(s, 2, 2).rearrange("p (u h q) -> p u h q", h=4, q=W),
                                             mask4.unsqueeze(1).unsqueeze(3).to_broadcast([P, 8, 4, W]), ALU.mult))
                    part = loc[s][:, (r - 1) * 256:r * 256]
                    half = part.rearrange("p (m b q) -> p m b q", m=4, b=2)
                    for b in range(2):
                        m = dve.tensor_reduce(half[:, :, b, :],
                                              picked[s][:, 4 * b:4 * b + 4].rearrange("p u h q -> p u q h"), AX, ALU.add)
                    own(s, m)
                    dve.wait_ge(r_Rc[s].sem, r_Rc[s].at(turn, r))
                    dve.tensor_tensor(part, part, Rs[s][:, 0:8 * W], ALU.mult).then_inc(a_loc[s].sem, 1)

                def remote(s):
                    dve.wait_ge(r_pv[s].sem, r_pv[s].at(turn, 3))
                    dve.wait_ge(r_Rc[s].sem, r_Rc[s].at(turn, 3))
                    dve.tensor_tensor(remT[s][0:64, :], bank(s, 2)[0:64, :], Rs[s][0:64, :], ALU.mult).then_inc(a_rem[s].sem, 1)

                def gate_local(s):
                    dve.wait_ge(a_tanh[s].sem, a_tanh[s].at(turn, 1))
                    dve.wait_ge(a_loc[s].sem, a_loc[s].at(turn, 2))
                    own(s, dve.scalar_tensor_tensor(out=loc[s], in0=tl[s], scalar=1.0, in1=loc[s], op0=ALU.add, op1=ALU.mult))

                def mix(s):
                    dve.wait_ge(a_ro[s].sem, a_ro[s].at(turn, 1))
                    own(s, dve.scalar_tensor_tensor(out=tr[s], in0=tr[s], scalar=1.0, in1=bank(s, 2), op0=ALU.add,
                                                    op1=ALU.mult))
                    dve.tensor_tensor(mixT[s], loc[s], tr[s], ALU.add).then_inc(a_mix[s].sem, 1)

                def ctx_keys(rotated, s):
                    pairs = PS[s][:, 0:2 * BANK].rearrange("p (b c) -> p b c", b=2)[:, :, 0:2 * SC]
                    pairs = pairs.rearrange("p b (k j) -> p b k j", k=2)
                    angle = con["sin" if rotated else "cos"].unsqueeze(1).unsqueeze(1).to_broadcast([P, 2, 2, SC])
                    keys = xk[s][:, :, S:NK]
                    if rotated:
                        dve.wait_ge(x_ck[s].sem, x_ck[s].at(turn, 2))
                        own(s, dve.tensor_tensor(rot[s].rearrange("p (b k) j -> p b k j", b=2), pairs, angle, ALU.mult))
                        dve.wait_ge(x_ckv[s].sem, x_ckv[s].at(turn, 1))
                        dve.tensor_tensor(keys, keys, rot[s], ALU.add).then_inc(x_ckv[s].sem, 1)
                    else:
                        dve.wait_ge(x_ck[s].sem, x_ck[s].at(turn, 1))
                        dve.tensor_tensor(keys.rearrange("p (b k) j -> p b k j", b=2), pairs, angle,
                                          ALU.mult).then_inc(x_ckv[s].sem, 1)

                def copy_x(k, s):
                    dve.wait_ge(x_pr[s].sem, x_pr[s].at(turn, k))
                    dst = (xq[s][:, 0:2, :], xk[s][:, 0:2, 0:S], xv[s][:, 0:2, :])[k - 1]
                    dve.tensor_copy(dst, bank(s, 0, 2).rearrange("p (a b) -> p a b", a=2)).then_inc(x_cv[s].sem, 1)

                def x_max(u, s):
                    dve.wait_ge(x_sc[s].sem, x_sc[s].at(turn, u + 1))
                    own(s, dve.tensor_reduce(mx[s][:, u:u + 1], PS[s][:, 0:NK], AX, ALU.max))
                    dve.tensor_scalar(nb[s][:, u:u + 1], mx[s][:, u:u + 1], -(XD ** -0.5), None,
                                      ALU.mult).then_inc(x_nb[s].sem, 1)

                def x_copy_a(u, s):
                    dve.wait_ge(x_ta[s].sem, x_ta[s].at(turn, u + 1))
                    if u >= 4:
                        dve.wait_ge(x_pv[s].sem, x_pv[s].at(turn, (u - 4) // 2 + 1))
                    dve.tensor_copy(xPT[s][:, u % 4, 0:3, :].rearrange("p c q -> p (c q)"),
                                    bank(s, 2)[:, 0:3 * P]).then_inc(x_ea[s].sem, 1)

                def x_spread(j, s):
                    dve.wait_ge(x_exp[s].sem, x_exp[s].at(turn, 2 * j + 2))
                    if j:
                        dve.wait_ge(x_sc[s].sem, x_sc[s].at(turn, 2 * j + 2))
                    u = slice(2 * j, 2 * j + 2)
                    own(s, dve.reciprocal(rsum[s][:, u], sums[s][:, u]))
                    dve.tensor_copy(spread[s][:].rearrange("p (h d) -> p h d", h=2),
                                    rsum[s][:, u].unsqueeze(2).to_broadcast([P, 2, 64])).then_inc(x_rs[s].sem, 1)

                def x_normalise(j, s):
                    hp, t = j // 4, j % 4
                    dve.wait_ge(x_pv[s].sem, x_pv[s].at(turn, j + 1))
                    dve.wait_ge(x_rc[s].sem, x_rc[s].at(turn, j + 1))
                    dve.tensor_tensor(xo[s][:, hp, t * P:(t + 1) * P], bank(s, 3)[:, t * P:(t + 1) * P], xr[s],
                                      ALU.mult).then_inc(x_no[s].sem, 1)

                def choose(s):
                    dve.wait_ge(s_wC, 16 * 4)
                    dve.wait_ge(c_lg[s].sem, c_lg[s].at(turn, 1))
                    iota = con["iota"].unsqueeze(1).to_broadcast([P, NT, E])
                    own(s, dve.tensor_tensor(lg[s], bank(s, 2)[:, 0:NT * E].rearrange("p (t e) -> p t e", t=NT),
                                             rb[:].unsqueeze(1).to_broadcast([P, NT, E]), ALU.add))
                    own(s, dve.tensor_reduce(mx[s][:, 0:NT], lg[s], AX, ALU.max))
                    own(s, dve.tensor_tensor(eq[s], lg[s], mx[s][:, 0:NT].unsqueeze(2).to_broadcast([P, NT, E]),
                                             ALU.is_equal))
                    own(s, dve.tensor_tensor(pick[s], eq[s], iota, ALU.mult))
                    own(s, dve.tensor_reduce(mx[s][:, NT:2 * NT], pick[s], AX, ALU.min))
                    dve.tensor_tensor(oh[s], iota, mx[s][:, NT:2 * NT].unsqueeze(2).to_broadcast([P, NT, E]),
                                      ALU.is_equal).then_inc(c_oh[s].sem, 1)

                def onehot_less_one(s):
                    dve.wait_ge(c_oa[s].sem, c_oa[s].at(turn, 1))
                    dve.tensor_scalar(ohm[s][0:E, :], ohT[s][0:E, :], -1.0, None, ALU.add).then_inc(c_ov[s].sem, 1)

                def relu(c, s):
                    dve.wait_ge(c_h[s].sem, c_h[s].at(turn, c + 1))
                    dve.tensor_scalar(hid[s][:, c, :], bank(s, c % 3), b1[:, c:c + 1], 0.0, ALU.add,
                                      ALU.max).then_inc(c_hv[s].sem, 1)

                def d_mask(s):
                    dve.wait_ge(d_sc[s].sem, d_sc[s].at(turn, 1))
                    for t in range(NT):
                        own_tiles, a = slice(0, (t + 1) * P), S - P - t * P
                        m = dve.scalar_tensor_tensor(out=dz[s][:, t, own_tiles], in0=bank(s, t)[:, own_tiles],
                                                     scalar=32 ** -0.5, in1=tri[:, a:a + (t + 1) * P], op0=ALU.mult,
                                                     op1=ALU.mult)
                    own(s, m)
                    for t in range(NT):
                        z, e = dz[s][:, t, 0:(t + 1) * P], de[s][:, t, 0:(t + 1) * P]
                        m = dve.tensor_scalar(e, z, 0.0, FMIN, ALU.is_equal, ALU.mult)
                    own(s, m)
                    for t in range(NT):
                        z, e = dz[s][:, t, 0:(t + 1) * P], de[s][:, t, 0:(t + 1) * P]
                        m = dve.tensor_tensor(z, z, e, ALU.add)
                    own(s, m)
                    for t in range(NT):
                        m = dve.tensor_reduce(mx[s][:, t:t + 1], dz[s][:, t, 0:(t + 1) * P], AX, ALU.max)
                    own(s, m)
                    dve.tensor_scalar(nb[s][:, 0:NT], mx[s][:, 0:NT], -1.0, None, ALU.mult).then_inc(d_nb[s].sem, 1)

                def copy_d(s):
                    dve.wait_ge(d_exp[s].sem, d_exp[s].at(turn, 1))
                    own(s, dve.reciprocal(rsum[s][:, 0:NT], sums[s][:, 0:NT]))
                    dve.wait_ge(d_tu[s].sem, d_tu[s].at(turn, 1))
                    dve.tensor_copy(PT[s][:, 0:2, :].rearrange("p a b -> p (a b)"), bank(s, 0, 2)).then_inc(d_ev[s].sem, 1)

                def residual_d(s):
                    dve.wait_ge(branch[s].sem, branch[s].at(turn, 4))
                    for t in range(NT):
                        m = dve.scalar_tensor_tensor(out=y[s][:, t, :], in0=bank(s, 3)[:, t * P:(t + 1) * P],
                                                     scalar=rsum[s][:, t:t + 1], in1=x_tm[s][:, t, :], op0=ALU.mult,
                                                     op1=ALU.add)
                    own(s, m)
                    stats(6, s, y[s], NT)

                def add_ctx_biases(s):
                    dve.wait_ge(s_wE, 16 * 5)
                    dve.wait_ge(e_kv[s].sem, e_kv[s].at(turn, 1))
                    last = slice(0, ELAST)
                    dve.tensor_scalar(ekb[s], bank(s, 1)[:, 0:SC], e_bk, None, ALU.add)
                    dve.tensor_tensor(evm[s][:, 0:EV - 1], bank(s, 0).rearrange("p (c f) -> p c f", f=P),
                                      e_bv[:].unsqueeze(1).to_broadcast([P, EV - 1, P]), ALU.add)
                    dve.tensor_tensor(evm[s][last, EV - 1], bank(s, 1)[last, 256:384], e_bv[last],
                                      ALU.add).then_inc(e_cr[s].sem, 1)

                def mask_ctx(s):
                    dve.wait_ge(e_cr[s].sem, e_cr[s].at(turn, 1))
                    last, mask = slice(0, ELAST), con["vmask"].rearrange("p (c f) -> p c f", c=EV)
                    dve.tensor_tensor(ekm[s], ekb[s].unsqueeze(1).to_broadcast([P, 4, SC]),
                                      mask4.unsqueeze(2).to_broadcast([P, 4, SC]), ALU.mult)
                    dve.tensor_tensor(evm[s][:, 0:EV - 1], evm[s][:, 0:EV - 1], mask[:, 0:EV - 1], ALU.mult)
                    dve.tensor_tensor(evm[s][last, EV - 1], evm[s][last, EV - 1], mask[last, EV - 1],
                                      ALU.mult).then_inc(e_cv[s].sem, 1)

                def e_max(u, s):
                    dve.wait_ge(e_sc[s].sem, e_sc[s].at(turn, u + 1))
                    scores = PS[s][:, 0:2 * BANK].rearrange("p (b c) -> p b c", b=2)[:, :, 0:2 * SC]
                    heads = slice(4 * u, 4 * u + 4)
                    own(s, dve.tensor_reduce(mx[s][:, heads].rearrange("p (b k) -> p b k", b=2),
                                             scores.rearrange("p b (k j) -> p b k j", k=2), AX, ALU.max))
                    dve.tensor_scalar(nb[s][:, heads], mx[s][:, heads], -(HD ** -0.5), None,
                                      ALU.mult).then_inc(e_nb[s].sem, 1)

                def e_copy_probs(u, s):
                    dve.wait_ge(e_tu[s].sem, e_tu[s].at(turn, 2 * u + 1))
                    dve.tensor_copy(ePT[s][:, u % 4, 0:EV - 1].rearrange("p a b -> p (a b)"),
                                    bank(s, 2)).then_inc(e_ev[s].sem, 1)

                def e_spread(t, s):
                    dve.wait_ge(e_exp[s].sem, e_exp[s].at(turn, 8 * t + 8))
                    heads = slice(16 * t, 16 * t + 16)
                    own(s, dve.reciprocal(rsum[s][:, heads], sums[s][:, heads]))
                    dve.tensor_copy(spread[s][:].rearrange("p (h d) -> p h d", h=16),
                                    rsum[s][:, heads].unsqueeze(2).to_broadcast([P, 16, HD])).then_inc(e_rs[s].sem, 1)

                def e_normalise(t, s):
                    dve.wait_ge(e_rc[s].sem, e_rc[s].at(turn, t + 1))
                    dve.tensor_tensor(eo[s][:, t * P:(t + 1) * P], bank(s, 1)[:, 384:512], er[s],
                                      ALU.mult).then_inc(e_no[s].sem, 1)

                def copy_f(s):
                    dve.wait_ge(f_tu[s].sem, f_tu[s].at(turn, 1))
                    for c in (0, 1):
                        m = dve.tensor_scalar(fhT[s][:, c, :], bank(s, c), f_w[:, c:c + 1], f_b[:, c:c + 1],
                                              ALU.mult, ALU.add)
                    m.then_inc(f_ev[s].sem, 1)

                both = range(STREAMS)
                for s in both:
                    ctx_stats(s)
                for s in both:
                    pool_latents(s)
                for s in both:
                    mask_q(s)
                for s in both:
                    normalise(1, s, cn[s], c_tm[s], 2, CH)
                    mask_latents(s)
                for v in range(14):
                    for s in both:
                        if v <= 12:
                            a_softmax(v, s)
                        if v in (6, 10):
                            pick_heads(v // 4, s)
                for s in both:
                    gate_local(s)
                for s in both:
                    remote(s)
                for s in both:
                    mix(s)
                for s in both:
                    ctx_keys(False, s)
                    residual(1, 2, s, 0.5, ALU.mult)
                for s in both:
                    normalise(2, s, x_tm[s], y[s], NT)
                    dve.wait_ge(normed[s].sem, normed[s].at(turn, 2))
                    stats(3, s, x_tm[s], NT)
                    ctx_keys(True, s)
                for s in both:
                    normalise(3, s, y[s], x_tm[s], NT)
                for k in (1, 2, 3):
                    for s in both:
                        copy_x(k, s)
                for u in range(XU + 3):
                    for s in both:
                        if 1 <= u <= XU:
                            x_copy_a(u - 1, s)
                        if u >= 4 and u % 2 == 0:
                            x_normalise((u - 4) // 2, s)
                        if u < XU:
                            x_max(u, s)
                        if u >= 2 and u % 2 == 0 and u <= XU:
                            x_spread((u - 2) // 2, s)
                for s in both:
                    residual(2, 4, s, 1.0, ALU.mult)
                    dve.tensor_copy(cT4[s], cT[s][:].unsqueeze(1).to_broadcast([P, 4, SC]))
                    normalise(4, s, x_tm[s], y[s], NT)
                for s in both:
                    choose(s)
                for s in both:
                    onehot_less_one(s)
                for c in range(1, EC, 2):
                    for s in both:
                        relu(c, s)
                for s in both:
                    residual(3, 5, s, 0.0, ALU.max)
                    add_ctx_biases(s)
                    normalise(5, s, x_tm[s], y[s], NT)
                    mask_ctx(s)
                d_mask(0)
                d_mask(1)
                copy_d(0)
                residual_d(0)
                copy_d(1)
                normalise(6, 0, x_tm[0], y[0], NT)
                residual_d(1)
                normalise(6, 1, x_tm[1], y[1], NT)
                for u in range(EU + 2):
                    for s in both:
                        if u < EU:
                            e_max(u, s)
                        if 1 <= u <= EU:
                            e_copy_probs(u - 1, s)
                        if u % 4 == 0 and u:
                            e_spread(u // 4 - 1, s)
                        if u % 4 == 1 and u > 4:
                            e_normalise(u // 4 - 1, s)
                for s in both:
                    residual(5, 7, s, 1.0, ALU.mult)
                    normalise(7, s, x_tm[s], y[s], NT)
                def hidden_stats(s):
                    for t in range(NT):
                        dve.wait_ge(f_g[s].sem, f_g[s].at(turn, t + 1))
                        m = dve.bn_stats(bn[s][:, t, :], fg[s][:, t, :])
                    own(s, m)
                    dve.memset(spacer[:], 0.0)
                    for t in range(NT):
                        m = dve.bn_aggr(mv[s][:, t, :], bn[s][:, t, :])
                    m.then_inc(var_ready[s].sem, 1)

                def residual_f(s):
                    residual(6, 9, s, 1.0, ALU.mult)
                    dve.memset(used[s][:], 0.0).then_inc(gate[s].sem, 1)

                hidden_stats(0)
                normalise(8, 0, fg[0], fg[0], NT)
                hidden_stats(1)
                copy_f(0)
                normalise(8, 1, fg[1], fg[1], NT)
                residual_f(0)
                copy_f(1)
                normalise(9, 0, result[0], y[0], NT)
                residual_f(1)
                normalise(9, 1, result[1], y[1], NT)
                assert steps_own == [vown[0].per] * STREAMS, steps_own


_INS = ["L0_attn_wq", "L0_attn_wk", "L0_attn_wv", "L0_attn_wgq", "L0_attn_wgk", "L0_attn_wgv", "L0_attn_r_out_w",
        "L0_attn_gate_local_w", "L0_attn_gate_remote_w", "L0_attn_w_out", "L0_xattn_gamma_x", "L0_xattn_beta_x",
        "L0_xattn_gamma_l", "L0_xattn_beta_l", "L0_xattn_Wq", "L0_xattn_Wkv", "L0_xattn_Wo", "L0_ffn_router_w",
        "L0_ffn_router_b", "L0_ffn_weights1", "L0_ffn_bias1", "L0_ffn_weights2", "L0_ffn_bias2", "L1_attn_Wq",
        "L1_attn_Wk", "L1_attn_Wvdown", "L1_attn_Wvup", "L1_xattn_Wq", "L1_xattn_bq", "L1_xattn_Wkv", "L1_xattn_bkv",
        "L1_xattn_Wo", "L1_xattn_bo", "L1_ffn_W_fc", "L1_ffn_ln_w", "L1_ffn_ln_b", "L1_ffn_W_proj"]


def kernel(**inputs):
    import concourse.bacc as bacc
    from concourse.bass_utils import run_bass_kernel_spmd

    nc = bacc.Bacc("TRN2", target_bir_lowering=False, num_devices=1)
    arrays = {n: np.ascontiguousarray(inputs[n]) for n in ["x", "ctx_1024"] + _INS}
    arrays["table"], arrays["table16"], arrays["table_sel"] = constants()
    io = {n: nc.dram_tensor(f"in_{n}", a.shape, mybir.dt.from_np(a.dtype), kind="ExternalInput").ap()
          for n, a in arrays.items()}
    out = nc.dram_tensor("out_x", (B, S, D), F32, kind="ExternalOutput").ap()
    build(nc, io, out)
    r = run_bass_kernel_spmd(nc, [{f"in_{n}": a for n, a in arrays.items()}], core_ids=[0])
    return r.results[0]["out_x"]
```
